# Optimizing a Trainium2 kernel written in Bass

```python
import numpy as np
import jax
import jax.numpy as jnp

def _softmax(x, axis=-1):
    return jax.nn.softmax(x, axis=axis)
def _gelu(x):
    return jax.nn.gelu(x, approximate=True)
def _silu(x):
    return jax.nn.silu(x)
def _sigmoid(x):
    return jax.nn.sigmoid(x)
def _layernorm(x, axis=-1, eps=1e-5):
    m = jnp.mean(x, axis=axis, keepdims=True)
    v = jnp.var(x, axis=axis, keepdims=True)
    return (x - m) / jnp.sqrt(v + eps)
def _scatter_add(tgt, idx, src, axis=0):
    return tgt.at[idx].add(src)
def _segment_sum(src, seg, n):
    return jax.ops.segment_sum(src, seg, n)

kernel_name = 'mk_conv_attn_hybrid_d2_conv_nhwc128_22227b'

def setup_inputs(seed: int = 0):
    np.random.seed(seed)
    _w = jnp.asarray
    def _rec_inputs():
        import jax
        import jax.numpy as jnp
        _gk = jax.random.key(seed)
        x = -0.0005207 + 1.001 * jax.random.normal(jax.random.fold_in(_gk, 1), (4, 64, 64, 128), jnp.float32)
        return x
    x = _rec_inputs()
    def _L0_conv_setup():
        import jax, jax.numpy as jnp
        import numpy as np
        NUM_HEAD = 8

        def conv_same(x, w, b):
            return jax.lax.conv_general_dilated(x, w, window_strides=(1, 1), padding='SAME', dimension_numbers=('NHWC', 'HWIO', 'NHWC')) + b

        def _gated_resnet(x, W1, b1, W2, b2, Wq, bq, Wk, bk, Wv, bv, W3, b3):
            B, H, W, C = x.shape
            c1 = conv_same(jax.nn.elu(x), W1, b1)
            c2 = conv_same(c1, W2, b2)
            a, b = jnp.split(c2, 2, axis=-1)
            c3 = a * jax.nn.sigmoid(b)
            N = H * W
            f = c3.reshape(B, N, C)
            q = f @ Wq + bq
            k = f @ Wk + bk
            v = f @ Wv + bv
            scale = jnp.float32(np.sqrt(C // 8))
            dot = jnp.einsum('bnd,bmd->bnm', q, k) / scale
            mask = jnp.tril(jnp.ones((N, N), jnp.float32), -1)
            dot = dot - (1.0 - mask) * 10000000000.0
            dot = dot - jnp.max(dot, axis=-1, keepdims=True)
            e = jnp.exp(dot) * mask
            probs = e / (jnp.sum(e, axis=-1, keepdims=True) + 1e-10)
            atten = jnp.einsum('bnm,bmd->bnd', probs, v)
            multihead = jnp.tile(atten, (1, 1, NUM_HEAD)).reshape(B, H, W, -1)
            mh = multihead @ W3 + b3
            c3 = c3 + mh.reshape(B, H, W, C)
            return x + c3
        key = jax.random.key(seed)
        ks = jax.random.split(key, 8)
        B, H, W, C = (4, 64, 64, 128)
        DQK, DV = (4, 16)
        s = 0.02
        return {'x': jax.random.normal(ks[0], (B, H, W, C), dtype=jnp.float32), 'W1': jax.random.normal(ks[1], (3, 3, C, C), dtype=jnp.float32) * s, 'b1': jnp.zeros((C,), jnp.float32), 'W2': jax.random.normal(ks[2], (3, 3, C, 2 * C), dtype=jnp.float32) * s, 'b2': jnp.zeros((2 * C,), jnp.float32), 'Wq': jax.random.normal(ks[3], (C, DQK), dtype=jnp.float32) * s, 'bq': jnp.zeros((DQK,), jnp.float32), 'Wk': jax.random.normal(ks[4], (C, DQK), dtype=jnp.float32) * s, 'bk': jnp.zeros((DQK,), jnp.float32), 'Wv': jax.random.normal(ks[5], (C, DV), dtype=jnp.float32) * s, 'bv': jnp.zeros((DV,), jnp.float32), 'W3': jax.random.normal(ks[6], (NUM_HEAD * DV, C), dtype=jnp.float32) * s, 'b3': jnp.zeros((C,), jnp.float32)}
    _L0_conv_all = _L0_conv_setup()
    _L0_conv_in = {k: v for k, v in _L0_conv_all.items() if k in ('W1', 'b1', 'W2', 'b2', 'Wq', 'bq', 'Wk', 'bk', 'Wv', 'bv', 'W3', 'b3', )}
    del _L0_conv_all

    def _L1_attn_setup():
        import jax, jax.numpy as jnp
        import numpy as np
        key = jax.random.key(seed)
        x = jax.random.normal(key, (4, 4096, 128), dtype=jnp.float32)
        return {'x': x}
    _L1_attn_all = _L1_attn_setup()
    _L1_attn_in = {k: v for k, v in _L1_attn_all.items() if k in ()}
    del _L1_attn_all

    def _L1_ffn_setup():
        import jax, jax.numpy as jnp
        import numpy as np
        B, S, D, E, H, O, K = (512, 2048, 128, 64, 512, 128, 8)
        key = jax.random.key(seed)
        k0, k1, k2, k3 = jax.random.split(key, 4)
        x = jax.random.normal(k0, (B, S, D), dtype=jnp.float32)
        gate_w = jax.random.normal(k1, (E, D), dtype=jnp.float32) * (1.0 / np.sqrt(D))
        gate_b = jnp.zeros((E,), dtype=jnp.float32)
        weight1 = jax.random.uniform(k2, (E, D + 1, H), dtype=jnp.float32, minval=-1.0, maxval=1.0) * (1.0 / np.sqrt(D + 1))
        weight2 = jax.random.uniform(k3, (E, H + 1, O), dtype=jnp.float32, minval=-1.0, maxval=1.0) * (1.0 / np.sqrt(H + 1))
        return {'x': x, 'gate_w': gate_w, 'gate_b': gate_b, 'weight1': weight1, 'weight2': weight2}
    _L1_ffn_all = _L1_ffn_setup()
    _L1_ffn_in = {k: v for k, v in _L1_ffn_all.items() if k in ('gate_w', 'gate_b', 'weight1', 'weight2', )}
    del _L1_ffn_all

    return {
        "x": x,
        "L0_conv_W1": _L0_conv_in["W1"],
        "L0_conv_b1": _L0_conv_in["b1"],
        "L0_conv_W2": _L0_conv_in["W2"],
        "L0_conv_b2": _L0_conv_in["b2"],
        "L0_conv_Wq": _L0_conv_in["Wq"],
        "L0_conv_bq": _L0_conv_in["bq"],
        "L0_conv_Wk": _L0_conv_in["Wk"],
        "L0_conv_bk": _L0_conv_in["bk"],
        "L0_conv_Wv": _L0_conv_in["Wv"],
        "L0_conv_bv": _L0_conv_in["bv"],
        "L0_conv_W3": _L0_conv_in["W3"],
        "L0_conv_b3": _L0_conv_in["b3"],
        "L1_ffn_gate_w": _L1_ffn_in["gate_w"],
        "L1_ffn_gate_b": _L1_ffn_in["gate_b"],
        "L1_ffn_weight1": _L1_ffn_in["weight1"],
        "L1_ffn_weight2": _L1_ffn_in["weight2"],
    }

def reference(x, L0_conv_W1, L0_conv_b1, L0_conv_W2, L0_conv_b2, L0_conv_Wq, L0_conv_bq, L0_conv_Wk, L0_conv_bk, L0_conv_Wv, L0_conv_bv, L0_conv_W3, L0_conv_b3, L1_ffn_gate_w, L1_ffn_gate_b, L1_ffn_weight1, L1_ffn_weight2):
    import jax
    import jax.numpy as jnp
    def _L0_conv_ref(x, W1, b1, W2, b2, Wq, bq, Wk, bk, Wv, bv, W3, b3):
        import jax, jax.numpy as jnp
        import numpy as np
        NUM_HEAD = 8

        def conv_same(x, w, b):
            return jax.lax.conv_general_dilated(x, w, window_strides=(1, 1), padding='SAME', dimension_numbers=('NHWC', 'HWIO', 'NHWC')) + b

        def _gated_resnet(x, W1, b1, W2, b2, Wq, bq, Wk, bk, Wv, bv, W3, b3):
            B, H, W, C = x.shape
            c1 = conv_same(jax.nn.elu(x), W1, b1)
            c2 = conv_same(c1, W2, b2)
            a, b = jnp.split(c2, 2, axis=-1)
            c3 = a * jax.nn.sigmoid(b)
            N = H * W
            f = c3.reshape(B, N, C)
            q = f @ Wq + bq
            k = f @ Wk + bk
            v = f @ Wv + bv
            scale = jnp.float32(np.sqrt(C // 8))
            dot = jnp.einsum('bnd,bmd->bnm', q, k) / scale
            mask = jnp.tril(jnp.ones((N, N), jnp.float32), -1)
            dot = dot - (1.0 - mask) * 10000000000.0
            dot = dot - jnp.max(dot, axis=-1, keepdims=True)
            e = jnp.exp(dot) * mask
            probs = e / (jnp.sum(e, axis=-1, keepdims=True) + 1e-10)
            atten = jnp.einsum('bnm,bmd->bnd', probs, v)
            multihead = jnp.tile(atten, (1, 1, NUM_HEAD)).reshape(B, H, W, -1)
            mh = multihead @ W3 + b3
            c3 = c3 + mh.reshape(B, H, W, C)
            return x + c3
        return _gated_resnet(x, W1, b1, W2, b2, Wq, bq, Wk, bk, Wv, bv, W3, b3)

    def _L1_attn_ref(x):
        import jax, jax.numpy as jnp
        import numpy as np
        scores = jnp.einsum('btd,bsd->bts', x, x)
        out = jnp.einsum('bts,bsd->btd', scores, x)
        return out

    def _L1_ffn_ref(x, gate_w, gate_b, weight1, weight2):
        import jax, jax.numpy as jnp
        import numpy as np
        B, S, D, E, H, O, K = (512, 2048, 128, 64, 512, 128, 8)
        Bn, Sn, Dn = x.shape
        logits = jnp.einsum('bsd,ed->bse', x, gate_w) + gate_b
        probs = jax.nn.softmax(logits, axis=1)
        vals, idx = jax.lax.top_k(probs.transpose(0, 2, 1), K)
        topv = vals.transpose(0, 2, 1)
        topi = idx.transpose(0, 2, 1)
        flat_idx = topi.reshape(Bn, K * E)
        gathered = jnp.take_along_axis(x, flat_idx[:, :, None], axis=1)
        gathered = gathered.reshape(Bn, K, E, Dn)
        pooled = jnp.einsum('bked,bke->bed', gathered, topv)
        ones = jnp.ones((E, Bn, 1), dtype=x.dtype)
        h = jnp.concatenate([pooled.transpose(1, 0, 2), ones], axis=-1)
        h = jax.nn.gelu(jnp.einsum('ebd,edh->ebh', h, weight1), approximate=False)
        h = jnp.concatenate([h, ones], axis=-1)
        out = jnp.einsum('ebh,eho->ebo', h, weight2)
        out = out.transpose(1, 0, 2)
        weighted = jnp.einsum('beo,bke->bkeo', out, topv).reshape(Bn, K * E, O)
        outputs = jnp.zeros((Bn, Sn, O), dtype=x.dtype)
        outputs = outputs.at[jnp.arange(Bn)[:, None], flat_idx].add(weighted)
        return outputs

    def _gn(v, G=32, eps=1e-5):
        B_, H_, W_, C_ = v.shape
        g = v.reshape(B_, H_, W_, G, C_ // G)
        m = jnp.mean(g, axis=(1, 2, 4), keepdims=True)
        s = jnp.var(g, axis=(1, 2, 4), keepdims=True)
        return ((g - m) / jnp.sqrt(s + eps)).reshape(v.shape)

    def _ln_c(v, eps=1e-6):
        m = jnp.mean(v, axis=-1, keepdims=True)
        s = jnp.var(v, axis=-1, keepdims=True)
        return (v - m) / jnp.sqrt(s + eps)

    def _ln_t(v, eps=1e-5):
        m = jnp.mean(v, axis=-1, keepdims=True)
        s = jnp.var(v, axis=-1, keepdims=True)
        return (v - m) / jnp.sqrt(s + eps)

    def _to_tokens(v):
        B_, H_, W_, C_ = v.shape
        return v.reshape(B_, H_ * W_, C_)
    def _from_tokens(t, like):
        return t.reshape(like.shape)

    x = _L0_conv_ref(x, L0_conv_W1, L0_conv_b1, L0_conv_W2, L0_conv_b2, L0_conv_Wq, L0_conv_bq, L0_conv_Wk, L0_conv_bk, L0_conv_Wv, L0_conv_bv, L0_conv_W3, L0_conv_b3)
    t = _to_tokens(x)
    t = t + _L1_attn_ref(_ln_t(t))
    t = t + _L1_ffn_ref(_ln_t(t), L1_ffn_gate_w, L1_ffn_gate_b, L1_ffn_weight1, L1_ffn_weight2)
    x = _from_tokens(t, x)
    return x


_drawn_inputs = setup_inputs


def setup_inputs(seed=0):
    import zlib

    import numpy as np

    out = dict(_drawn_inputs(seed))
    spreads = {'L0_conv_b1': (0.0, 0.1),
     'L0_conv_b2': (0.0, 0.1),
     'L0_conv_bq': (0.0, 2.0),
     'L0_conv_bk': (0.0, 2.0),
     'L0_conv_bv': (0.0, 0.1),
     'L0_conv_b3': (0.0, 0.1),
     'L1_ffn_gate_b': (0.0, 0.1)}
    factors = {'L0_conv_Wq': 64.0,
     'L0_conv_Wk': 64.0,
     'L0_conv_Wv': 4.855,
     'L1_ffn_gate_w': 64.0,
     'L1_ffn_weight1': 179.309,
     'L1_ffn_weight2': 64.0}
    for name, (base, spread) in spreads.items():
        noise = np.random.default_rng([zlib.crc32(name.encode()), seed]).standard_normal(out[name].shape)
        drawn = base * np.exp(spread * noise) if base else spread * noise
        out[name] = jnp.asarray(drawn.astype(out[name].dtype))
    for name, factor in factors.items():
        out[name] = (out[name] * factor).astype(out[name].dtype)
    return out
```

```python
from contextlib import ExitStack

import concourse.bass as bass
from concourse import mybir

F32 = mybir.dt.float32
F32R = mybir.dt.float32r
ALU = mybir.AluOpType
ACT = mybir.ActivationFunctionType
AX = mybir.AxisListType

B, IH, IW, C = 4, 64, 64, 128
TOK = IH * IW
GROUPS = 8
GT = TOK // GROUPS
GR = IH // GROUPS
NT = GT // 128
PW = IW + 2
DK, DV, HEADS = 4, 16, 8
E, HID, KTOP = 64, 512, 8
SLOTS = 3
ESL = 3
QUAD = 32
TINY = 1e-10
EPS = 1e-5
K_ID, K_SEL, K_DEN, K_NQ, K_NK, K_ONE, K_POW, K_END = 0, 128, 256, 257, 258, 259, 260, 264


class Signal:

    def __init__(self, sem, per, unit=1):
        self.sem, self.per, self.unit = sem, per, unit

    def at(self, b, k):
        return (b * self.per + (self.per + k + 1)) * self.unit

    def before(self, b, k):
        return (b * self.per + (k + 1)) * self.unit


def score_units(g):
    whole = [[(i, 0)] for i in range(NT * g)]
    d = NT * g
    return whole + [[(d, 0)], [(d + 1, 128), (d + 3, 384)], [(d + 2, 256)]]


def attention_steps():
    out = []

    def group_a(g):
        return [("qkv", g)]

    out += group_a(0)
    for g in range(GROUPS):
        if g + 1 < GROUPS:
            out += group_a(g + 1)
        out += [("max", g, r, c) for c in range(g + 1) for r in range(NT)]
        out += [("fold", g)]
        out += [("exp", g, u) for u in range(len(score_units(g)))]
        out += [("mix", g), ("norm", g)]
    for g in range(GROUPS):
        out += [("lin", g)]
        if g:
            out += [("logit", g - 1)]
    out += [("logit", GROUPS - 1), ("topk",)]
    out += [("pool", n) for n in range(4)]
    return out


def conv_steps():
    out = [("load", 0), ("load", 1), ("elu", 0)]
    for g in range(GROUPS):
        if g + 2 < GROUPS:
            out += [("load", g + 2)]
        if g + 1 < GROUPS:
            out += [("elu", g + 1)]
        out += [("c1", g)]
        if g:
            out += [("c2", g - 1)]
    return out + [("c2", GROUPS - 1)]


def merged():
    return attention_steps() + conv_steps()


def program(nc, x_cm, x_nat, w1, b1, w2, b2, wq, bq, wk, bk, wv, bv, w3, b3, gate_wt, gate_b,
            f1, f1b, f2, f2b, consts, masks, out, t1_dram, p_dram, o_dram):
    ATT, CONV, BOTH = attention_steps(), conv_steps(), merged()
    misc_order, score_order, conv_order = [], [], []
    for st in ATT:
        k, a = st[0], st[1:]
        if k == "qkv":
            misc_order += [("q", a[0]), ("k", a[0]), ("v", a[0])]
        if k == "max" or k == "exp":
            score_order.append(st)
        if k == "fold":
            misc_order.append(("fold", a[0]))
        if k == "mix":
            misc_order += [("den", a[0]), ("mh", a[0]), ("ct", a[0])]
        if k == "norm":
            misc_order += [("gram", a[0]), ("zt", a[0])]
        if k == "lin":
            misc_order.append(("lin", a[0]))
        if k == "logit":
            misc_order += [("z2t", a[0]), ("logit", a[0])]
        if k == "pool":
            misc_order += [("pt", a[0]), ("pool", a[0])]
    for st in CONV:
        if st[0] == "c1":
            conv_order.append((("c1", st[1]), st[1] % 2))
        if st[0] == "c2":
            conv_order += [(("c2b", st[1]), 1), (("c2a", st[1]), 0)]
    NM, NS = len(misc_order), len(score_order)
    exp_order = [st for st in score_order if st[0] == "exp"]
    NE = len(exp_order)

    ctx = ExitStack()
    loopctx = ExitStack()

    def sb(name, shape, dt=F32, c=None):
        return (c or loopctx).enter_context(nc.sbuf_tensor(name, shape, dt))

    def semaphore(name):
        return ctx.enter_context(nc.semaphore(name))

    signals = []

    def signal(name, per, unit=1):
        s = Signal(semaphore(name), per, unit)
        signals.append(s)
        return s

    with ctx:
        ps = ctx.enter_context(nc.psum_tensor("ps", [128, 8, 512], F32))
        cbank = [ps[:, 0, :], ps[:, 1, :]]
        sbank = [ps[:, 2 + n, :] for n in range(SLOTS)]
        pvbank = ps[:, 5, :]
        mbank = [ps[:, 6, :], ps[:, 7, :]]

        con = sb("con", [128, K_END], c=ctx)
        ident = con[:, K_ID:K_ID + 128]
        pooled = sb("pooled", [128, B, E], c=ctx)

        identr = sb("identr", [128, 128], F32R)
        maskr = sb("maskr", [128, 2, 128], F32R)
        wqs = sb("wqs", [128, 2, 128])
        wvs = sb("wvs", [128, QUAD])
        bvs = sb("bvs", [128, QUAD])
        w3s = sb("w3s", [128, C])
        b3s = sb("b3s", [128, C])
        gws = sb("gws", [128, E])
        cols = sb("cols", [128, 8])
        c3 = sb("c3", [128, TOK])
        qv = sb("qv", [128, 2, GT])
        qh = sb("qh", [128, GT], F32R)
        kv = sb("kv", [128, GT])
        kh = sb("kh", [128, GT], F32R)
        qst = sb("qst", [128, 2, GT], F32R)
        qm = sb("qm", [128, GT], F32R)
        kst = sb("kst", [128, TOK], F32R)
        vs = sb("vs", [128, TOK // 128, QUAD])
        zl = sb("zl", [128, QUAD])
        hb = sb("hb", [128, 2])
        fh = sb("fh", [128, GT], F32R)
        mpart = sb("mpart", [128, NT, GROUPS])
        nm = sb("nm", [128, NT])
        dg = sb("dg", [128, NT, 128])
        ex = sb("ex", [128, ESL, GT])
        asb = sb("asb", [128, GT])
        xn = sb("xn", [128, 2, NT, C])
        rd = sb("rd", [128, 2, NT])
        T = sb("T", [128, TOK // 128, C])
        stat = sb("stat", [128, NT, 6])
        mv = sb("mv", [128, NT, 2])
        rs = sb("rs", [128, 2, NT])
        zr = sb("zr", [128, NT, C])
        zt = sb("zt", [128, TOK])
        G = sb("G", [128, C])
        z2t = sb("z2t", [128, GT])
        p = sb("p", [E, TOK])
        ptt = z2t[:, :].rearrange("p (t e) -> p t e", e=E)
        pacc = sb("pacc", [128, E])
        tk = sb("tk", [E, 12])
        w1s = sb("w1s", [128, 2, 9, C], F32R)
        w2s = sb("w2s", [128, 2, 9, 2 * C], F32R)
        xi = sb("xi", [128, 2, GR + 2, IW])
        el = sb("el", [128, GR + 2, IW])
        xp = sb("xp", [128, 2, 2, GR + 2, PW], F32R)
        cp = sb("cp", [128, 2, IH, PW], F32R)
        sg = sb("sg", [128, GT])
        loopctx.close()

        tail = ExitStack()
        RW = 4
        wa = sb("wa", [128, RW, 4, HID], c=tail)
        wb = sb("wb", [128, RW, 4, 4, C], c=tail)
        fb1 = sb("fb1", [E, HID], c=tail)
        fb2 = sb("fb2", [E, C], c=tail)
        px = sb("px", [128, E, QUAD], c=tail)
        eb = sb("eb", [E, E, QUAD], c=tail)
        hs = sb("hs", [128, 2, HID], c=tail)
        ht = sb("ht", [128, 2, 4, 128], c=tail)
        oall = sb("oall", [128, E // 4, C], c=tail)
        oo = sb("oo", [128, B, C], c=tail)
        pp = sb("pp", [128, 2, TOK], c=tail)
        LT = 4
        tl = sb("tl", [128, LT, NT, C], c=tail)
        tail.close()

        s_con, s_w, s_b = semaphore("consts_in"), semaphore("weights_in"), semaphore("biases_in")
        s_zero, s_set, s_setp, s_seta = (semaphore(n) for n in ("zeroed", "setup_dve", "setup_pool", "setup_act"))
        s_dset = semaphore("setup_steps")
        s_held = semaphore("held")
        x_in = [signal(f"x_in{n}", GROUPS // 2, 16) for n in range(2)]
        elu_exp = signal("elu_exp", GROUPS)
        elu_min = signal("elu_min", GROUPS)
        elu_out = signal("elu_out", GROUPS)
        x_high = signal("x_high", GROUPS)
        x_low = signal("x_low", GROUPS)
        cmm = signal("conv_products", 3 * GROUPS)
        c_high = signal("c_high", GROUPS)
        c_low = signal("c_low", GROUPS)
        gate_tanh = signal("gate_tanh", GROUPS)
        gate_half = signal("gate_half", GROUPS)
        c3_out = signal("c3_out", GROUPS)
        cmm_index = {k: n for n, (k, _) in enumerate(conv_order)}
        mmm = signal("misc_products", NM)
        smm = signal("scores", NS)
        q_val, q_high, q_st = (signal(n, GROUPS) for n in ("q_value", "q_high", "q_stacked"))
        k_val, k_high, k_st = (signal(n, GROUPS) for n in ("k_value", "k_high", "k_stacked"))
        v_out = signal("v_out", GROUPS)
        smax = signal("max_parts", NS - NE)
        nm_out = signal("neg_max", GROUPS)
        dg_out = signal("max_diagonal", GROUPS)
        fold_sum, fold_high, qm_out = (signal(n, GROUPS) for n in ("fold_sum", "fold_high", "q_with_max"))
        e_out = signal("exponentials", NE)
        pv = signal("pv_used", NE)
        a_out = signal("attention_copied", GROUPS)
        xn_in = [signal(f"xn_in{n}", GROUPS // 2, 16) for n in range(2)]
        xb_out = signal("x_plus_b3", GROUPS)
        den_sum, rd_out = signal("den_sum", GROUPS), signal("den_reciprocal", GROUPS)
        t_scaled, t_out = signal("t_scaled", GROUPS), signal("t_out", GROUPS)
        st1, mv1, ve1, rs1 = (signal(n, GROUPS) for n in ("ln1_stats", "ln1_mean_var", "ln1_var_eps", "ln1_rstd"))
        z_out, gram_out, zt_out = (signal(n, GROUPS) for n in ("z_out", "gram_out", "z_transposed"))
        t1_out = signal("t1_out", GROUPS)
        t1_store = signal("t1_stored", GROUPS, 16)
        st2, mv2, ve2, rs2 = (signal(n, GROUPS) for n in ("ln2_stats", "ln2_mean_var", "ln2_var_eps", "ln2_rstd"))
        z2_out, z2t_out, logit_out = (signal(n, GROUPS) for n in ("z2_out", "z2_transposed", "logits_out"))
        tkd = signal("topk_steps", 6)
        tke = signal("topk_exp", 1)
        p_store = signal("p_stored", 1, 16)
        pt_out, pool_out = signal("p_transposed", 4), signal("pooled_part", 4)

        midx = {k: n for n, k in enumerate(misc_order)}
        sidx = {k: n for n, k in enumerate(score_order)}
        eidx = {k: n for n, k in enumerate(exp_order)}

        xidx = {st: n for n, st in enumerate(st for st in score_order if st[0] == "max")}
        readers = {"q": q_high, "k": k_high, "v": v_out, "fold": fold_sum, "den": den_sum, "mh": t_scaled,
                   "ct": t_out, "gram": gram_out, "zt": zt_out, "lin": t1_out, "z2t": z2t_out,
                   "logit": logit_out, "pt": pt_out, "pool": pool_out, "c1": c_low, "c2a": c3_out,
                   "c2b": gate_tanh}

        def read_of(key):
            if key[0] == "max":
                return smax, xidx[key]
            if key[0] == "exp":
                return e_out, eidx[key]
            return readers[key[0]], key[1]

        def reused(order, bank_of, n, b):
            same = [m for m in range(n) if bank_of(m) == bank_of(n)]
            if same:
                s, k = read_of(order[same[-1]])
                return s.sem, s.at(b, k)
            s, k = read_of(order[[m for m in range(len(order)) if bank_of(m) == bank_of(n)][-1]])
            return s.sem, s.before(b, k)

        conv_keys = [k for k, _ in conv_order]
        conv_bank = [n for _, n in conv_order]

        def misc(key):
            return mbank[midx[key] % 2]

        def x_rows(g):
            lo, hi = max(GR * g - 1, 0), min(GR * g + GR + 1, IH)
            return lo, hi, lo - (GR * g - 1)

        s_fb = semaphore("ffn_biases_in")
        wa_in = [semaphore(f"wa_in{n}") for n in range(RW)]
        wb_in = [semaphore(f"wb_in{n}") for n in range(RW)]
        ffn1, ffn2, gelu, htr, htc = (semaphore(n) for n in ("ffn1", "ffn2", "gelu", "h_transposed", "h_copied"))
        p_in, o_out, o_stored, oo_in = (semaphore(n) for n in ("p_in", "o_out", "o_stored", "oo_in"))
        tl_in = [semaphore(f"tl_in{n}") for n in range(LT)]
        out_st = [semaphore(f"out_stored{n}") for n in range(LT)]
        sum_out, fin, s_px = semaphore("sum_out"), semaphore("final_products"), semaphore("ffn_operands")

        N_W, N_B = 16 * 5, 16 * (16 + 4 + 5)
        block = ctx.enter_context(nc.Block())

        @block.sync
        def _(sp):
            for s in signals:
                sp.sem_inc(s.sem, s.per * s.unit)
            sp.dma_start(con[:, :], consts).then_inc(s_con, 16)
            sp.dma_start(zr[:, 0:2, :], masks).then_inc(s_w, 16)
            sp.dma_start(c3[:, 0:9 * C], w1.rearrange("p t c -> p (t c)")).then_inc(s_w, 16)
            sp.dma_start(T[:, :, :].rearrange("p t c -> p (t c)")[:, 0:18 * C],
                         w2.rearrange("p t c -> p (t c)")).then_inc(s_w, 16)
            sp.dma_start(gws[:, :], gate_wt).then_inc(s_w, 16)
            sp.dma_start(b3s[:, :], b3.partition_broadcast(128)).then_inc(s_w, 16)
            sp.wait_ge(s_zero, 1)
            for q in range(4):
                sp.dma_start(wqs[:, 0, QUAD * q:QUAD * q + DK], wq).then_inc(s_b, 16)
                sp.dma_start(wqs[:, 1, QUAD * q:QUAD * q + DK], wk).then_inc(s_b, 16)
                sp.dma_start(cols[QUAD * q:QUAD * q + DK, 3:4], bq).then_inc(s_b, 16)
                sp.dma_start(cols[QUAD * q:QUAD * q + DK, 4:5], bk).then_inc(s_b, 16)
            for q in range(4):
                sp.dma_start(zt[QUAD * q:QUAD * q + DV, 0:HEADS * C], w3).then_inc(s_b, 16)
            sp.dma_start(wvs[:, 0:DV], wv).then_inc(s_b, 16)
            sp.dma_start(bvs[:, 0:DV], bv.partition_broadcast(128)).then_inc(s_b, 16)
            sp.dma_start(cols[:, 0:1], b1).then_inc(s_b, 16)
            sp.dma_start(cols[:, 1:3], b2).then_inc(s_b, 16)
            sp.dma_start(cols[0:E, 5:6], gate_b).then_inc(s_b, 16)

            def load(b, g):
                sp.wait_ge(elu_out.sem, elu_out.at(b, g - 2) if g >= 2 else elu_out.before(b, g + 6))
                lo, hi, r = x_rows(g)
                sp.dma_start(xi[:, g % 2, r:r + hi - lo, :].rearrange("p r w -> p (r w)"),
                             x_cm[b, :, lo * IW:hi * IW]).then_inc(x_in[g % 2].sem, 16)

            def load_nat(b, g):
                sp.wait_ge(t_scaled.sem, t_scaled.at(b, g - 2) if g >= 2 else t_scaled.before(b, g + 6))
                sp.dma_start(xn[:, g % 2, :, :], x_nat[b, g, :, :, :]).then_inc(xn_in[g % 2].sem, 16)

            def store_t1(b, g):
                sp.wait_ge(t1_out.sem, t1_out.at(b, g))
                sp.dma_start(t1_dram[b, g, :, :, :], T[:, NT * g:NT * g + NT, :]).then_inc(t1_store.sem, 16)

            def store_p(b):
                sp.wait_ge(tkd.sem, tkd.at(b, 5))
                sp.dma_start(p_dram[b, :, :], p[:, :]).then_inc(p_store.sem, 16)

            def run(steps, b, c):
                for st in steps:
                    if st[0] == "load":
                        load(c, st[1])
                    if st[0] == "qkv":
                        load_nat(b, st[1])
                    if st[0] == "lin":
                        store_t1(b, st[1])
                    if st[0] == "topk":
                        store_p(b)

            run(CONV, None, 0)
            with sp.Fori(0, B - 1) as b:
                run(BOTH, b, b + 1)
            run(ATT, B - 1, None)

            last = B - 1
            sp.wait_ge(pool_out.sem, pool_out.at(last, 3))
            sp.wait_ge(p_store.sem, p_store.at(last, 0))
            sp.wait_ge(t1_store.sem, t1_store.at(last, GROUPS - 1))
            sp.dma_start(fb1[:, :], f1b).then_inc(s_fb, 16)
            sp.dma_start(fb2[:, :], f2b).then_inc(s_fb, 16)
            for i in range(E // 4):
                if i >= RW:
                    sp.wait_ge(ffn1, i - RW + 1)
                sp.dma_start(wa[:, i % RW, :, :], f1[:, 4 * i:4 * i + 4, :]).then_inc(wa_in[i % RW], 16)
                if i >= RW:
                    sp.wait_ge(ffn2, i - RW + 1)
                sp.dma_start(wb[:, i % RW, :, :, :], f2[:, 4 * i:4 * i + 4, :, :]).then_inc(wb_in[i % RW], 16)
                if i % 4 == 3:
                    n = i // 4
                    sp.dma_start(pp[E * (n % 2):E * (n % 2) + E, n // 2, :], p_dram[n, :, :]).then_inc(p_in, 16)
            for n in range(LT):
                sp.dma_start(tl[:, n, :, :], t1_dram[n // GROUPS, n % GROUPS, :, :, :]).then_inc(tl_in[n], 16)
            sp.wait_ge(o_out, E // 4)
            for n in range(B):
                sp.dma_start(o_dram[n, :, :].rearrange("(i j) o -> j i o", j=4),
                             oall[n:128:QUAD, :, :]).then_inc(o_stored, 16)
            sp.wait_ge(o_stored, 16 * B)
            for h in range(2):
                sp.dma_start(oo[E * h:E * h + E, :, :], o_dram.rearrange("b e o -> e b o")).then_inc(oo_in, 16)
            for n in range(B * GROUPS):
                sp.wait_ge(sum_out, n + 1)
                sp.dma_start(out[n // GROUPS, n % GROUPS, :, :, :], tl[:, n % LT, :, :]).then_inc(out_st[n % LT], 16)
                m = n + LT
                if m < B * GROUPS:
                    sp.wait_ge(out_st[n % LT], 16 * (n // LT + 1))
                    sp.dma_start(tl[:, n % LT, :, :], t1_dram[m // GROUPS, m % GROUPS, :, :, :]).then_inc(tl_in[n % LT], 16)
            for n in range(LT):
                sp.wait_ge(out_st[n], 16 * (B * GROUPS // LT))



        @block.tensor
        def _(pe):
            pe.wait_ge(s_setp, 1)
            pe.wait_ge(s_set, 1)
            pe.wait_ge(s_seta, 1)

            def conv(bank, w, lo, x, rows):
                acc = bank.rearrange("p (r w) -> p r w", w=IW)
                n = 0
                for dy in (1, 0, 2):
                    src, dst = rows(dy)
                    for dx in range(3):
                        for wi, xi_ in ((0, 0), (0, 1), (1, 0)):
                            n += 1
                            mm = pe.matmul(acc[:, dst, :], w[:, wi, 3 * dy + dx, lo:lo + C],
                                           x[:, xi_, src, dx:dx + IW], start=(n == 1), stop=(n == 27))
                return mm

            def edges(g, dy):
                return (1 if g == 0 and dy == 0 else 0), (GR - 1 if g == GROUPS - 1 and dy == 2 else GR)

            def bank_wait(key, b):
                pe.wait_ge(*reused(conv_keys, lambda m: conv_bank[m], cmm_index[key], b))

            def c1(b, g):
                def rows(dy):
                    r0, r1 = edges(g, dy)
                    return slice(r0 + dy, r1 + dy), slice(r0, r1)
                pe.wait_ge(x_low.sem, x_low.at(b, g))
                bank_wait(("c1", g), b)
                conv(cbank[g % 2], w1s, 0, xp[:, g % 2], rows).then_inc(cmm.sem, 1)

            def c2(b, g):
                def rows(dy):
                    r0, r1 = edges(g, dy)
                    return slice(GR * g + r0 + dy - 1, GR * g + r1 + dy - 1), slice(r0, r1)
                pe.wait_ge(c_low.sem, c_low.at(b, min(g + 1, GROUPS - 1)))
                for key, half in (("c2b", 1), ("c2a", 0)):
                    bank_wait((key, g), b)
                    conv(cbank[half], w2s, half * C, cp, rows).then_inc(cmm.sem, 1)

            def misc_bank(b, key):
                pe.wait_ge(*reused(misc_order, lambda m: m % 2, midx[key], b))
                return misc(key)

            def qkv(b, g):
                x = c3[:, GT * g:GT * g + GT]
                pe.wait_ge(c3_out.sem, c3_out.at(b, g))
                bank = misc_bank(b, ("q", g))
                pe.matmul(bank, wqs[:, 0, :], x, start=True, stop=True).then_inc(mmm.sem, 1)
                bank = misc_bank(b, ("k", g))
                pe.matmul(bank, wqs[:, 1, :], x, start=True, stop=True).then_inc(mmm.sem, 1)
                bank = misc_bank(b, ("v", g))
                for r in range(NT):
                    mm = pe.matmul(bank[:, QUAD * r:QUAD * r + QUAD], x[:, 128 * r:128 * r + 128], wvs[:, :],
                                   start=True, stop=True)
                mm.then_inc(mmm.sem, 1)

            def score_bank(b, st):
                n = sidx[st]
                pe.wait_ge(*reused(score_order, lambda m: m % SLOTS, n, b))
                return sbank[n % SLOTS]

            def max_scores(b, g, r, c):
                if r == 0 and c == 0:
                    pe.wait_ge(q_st.sem, q_st.at(b, g))
                    pe.wait_ge(k_st.sem, k_st.at(b, g))
                bank = score_bank(b, ("max", g, r, c))
                w = GT if c < g else 128 * (r + 1)
                mm = pe.matmul(bank[:, 0:w], qst[:, g % 2, 128 * r:128 * r + 128], kst[:, GT * c:GT * c + w],
                               start=True, stop=(c < g))
                if c == g:
                    mm = pe.matmul(bank[:, w - 128:w], identr[:, :], maskr[:, 0, :], start=False, stop=True)
                mm.then_inc(smm.sem, 1)

            def fold(b, g):
                pe.wait_ge(dg_out.sem, dg_out.at(b, g))
                bank = misc_bank(b, ("fold", g))
                pe.matmul(bank, con[:, K_SEL:K_SEL + 128], dg[:, :, :].rearrange("p t n -> p (t n)"),
                          start=True, stop=True).then_inc(mmm.sem, 1)

            def exp_scores(b, g, u):
                if u == 0:
                    pe.wait_ge(qm_out.sem, qm_out.at(b, g))
                bank = score_bank(b, ("exp", g, u))
                at = 0
                for i, n0 in score_units(g)[u]:
                    w = GT - n0 if i >= NT * g else GT
                    diag = i >= NT * g
                    q0 = 128 * (i - NT * g) if diag else 0
                    w = GT - q0
                    mm = pe.matmul(bank[:, at:at + w], kst[:, 128 * i:128 * i + 128], qm[:, q0:GT],
                                   start=True, stop=not diag)
                    if diag:
                        mm = pe.matmul(bank[:, at:at + 128], identr[:, :], maskr[:, 1, :], start=False, stop=True)
                    at += w
                mm.then_inc(smm.sem, 1)

            def values(b, g, u):
                n = eidx[("exp", g, u)]
                if u == 0:
                    pe.wait_ge(a_out.sem, a_out.at(b, g - 1) if g else a_out.before(b, GROUPS - 1))
                pe.wait_ge(e_out.sem, e_out.at(b, n))
                e = ex[:, n % ESL, :]
                if g == 0 and u == 0:
                    for q in range(1, 4):
                        pe.matmul(pvbank[QUAD * q:QUAD * q + QUAD, :], zl[:, :], e, start=True, stop=False,
                                  skip_group_check=True)
                at = 0
                for i, _ in score_units(g)[u]:
                    q0 = 128 * (i - NT * g) if i >= NT * g else 0
                    w = GT - q0
                    q = i % 4
                    mm = pe.matmul(pvbank[QUAD * q:QUAD * q + QUAD, q0:GT], vs[:, i, :], e[:, at:at + w],
                                   start=(i < 4 and not (g == 0 and i > 0)), stop=(i >= NT * g),
                                   skip_group_check=True)
                    at += w
                mm.then_inc(pv.sem, 1)

            def mix(b, g):
                pe.wait_ge(a_out.sem, a_out.at(b, g))
                bank = misc_bank(b, ("den", g))
                for r in range(NT):
                    mm = pe.matmul(bank[:, r:r + 1], asb[:, 128 * r:128 * r + 128], con[:, K_DEN:K_DEN + 1],
                                   start=True, stop=True)
                mm.then_inc(mmm.sem, 1)
                bank = misc_bank(b, ("mh", g))
                for r in range(NT):
                    mm = pe.matmul(bank[:, 128 * r:128 * r + 128], asb[:, 128 * r:128 * r + 128], w3s[:, :],
                                   start=True, stop=True)
                mm.then_inc(mmm.sem, 1)
                turn(b, ("ct", g), c3[:, GT * g:GT * g + GT])

            def turn(b, key, x):
                bank = misc_bank(b, key)
                for r in range(NT):
                    mm = pe.transpose(bank[:, 128 * r:128 * r + 128], x[:, 128 * r:128 * r + 128], ident)
                mm.then_inc(mmm.sem, 1)

            def norm(b, g):
                pe.wait_ge(z_out.sem, z_out.at(b, g))
                bank = misc_bank(b, ("gram", g))
                for r in range(NT):
                    mm = pe.matmul(bank[:, 0:C], zr[:, r, :], zr[:, r, :], start=(r == 0), stop=(r == NT - 1))
                mm.then_inc(mmm.sem, 1)
                turn(b, ("zt", g), zr[:, :, :].rearrange("p t c -> p (t c)"))

            def lin(b, g):
                if g == 0:
                    pe.wait_ge(gram_out.sem, gram_out.at(b, GROUPS - 1))
                    pe.wait_ge(zt_out.sem, zt_out.at(b, GROUPS - 1))
                bank = misc_bank(b, ("lin", g))
                for r in range(NT):
                    t = GT * g + 128 * r
                    mm = pe.matmul(bank[:, 128 * r:128 * r + 128], zt[:, t:t + 128], G[:, :], start=True, stop=True)
                mm.then_inc(mmm.sem, 1)

            def logit(b, g):
                pe.wait_ge(z2_out.sem, z2_out.at(b, g))
                turn(b, ("z2t", g), zt[:, GT * g:GT * g + GT])
                pe.wait_ge(z2t_out.sem, z2t_out.at(b, g))
                bank = misc_bank(b, ("logit", g))
                pe.matmul(bank[0:E, :], gws[:, :], z2t[:, :], start=True, stop=True).then_inc(mmm.sem, 1)

            def pool(b, n):
                if n == 0:
                    pe.wait_ge(tkd.sem, tkd.at(b, 5))
                bank = misc_bank(b, ("pt", n))
                pe.sem_inc(s_held, 1)
                for t in range(8):
                    at = 128 * (8 * n + t)
                    mm = pe.transpose(bank[:, E * t:E * t + E], p[:, at:at + 128], ident[0:E, 0:E])
                mm.then_inc(mmm.sem, 1)
                pe.wait_ge(pt_out.sem, pt_out.at(b, n))
                bank = misc_bank(b, ("pool", n))
                for t in range(8):
                    at = 128 * (8 * n + t)
                    mm = pe.matmul(bank[:, 0:E], zt[:, at:at + 128], ptt[:, t, :], start=(t == 0), stop=(t == 7))
                mm.then_inc(mmm.sem, 1)

            def run(steps, b, c):
                late = []
                for st in steps:
                    k, a = st[0], st[1:]
                    if k == "mix":
                        for x in late:
                            values(b, *x)
                        late = []
                    if k == "c1":
                        c1(c, *a)
                    if k == "c2":
                        c2(c, *a)
                    if k == "qkv":
                        qkv(b, *a)
                    if k == "max":
                        max_scores(b, *a)
                    if k == "fold":
                        fold(b, *a)
                    if k == "exp":
                        exp_scores(b, *a)
                        late.append(a)
                        if len(late) > 1:
                            values(b, *late.pop(0))
                    if k == "mix":
                        mix(b, *a)
                    if k == "norm":
                        norm(b, *a)
                    if k == "lin":
                        lin(b, *a)
                    if k == "logit":
                        logit(b, *a)
                    if k == "pool":
                        pool(b, *a)

            run(CONV, None, 0)
            with pe.Fori(0, B - 1) as b:
                run(BOTH, b, b + 1)
            run(ATT, B - 1, None)

            pe.wait_ge(s_px, 2)
            pe.wait_ge(s_fb, 32)

            def first(i):
                if i >= 2:
                    pe.wait_ge(gelu, i - 1)
                pe.wait_ge(wa_in[i % RW], 16 * (i // RW + 1))
                for j in range(4):
                    o = ps[QUAD * j:QUAD * j + QUAD, i % 2, :]
                    pe.matmul(o, eb[:, 4 * i + j, :], fb1[:, :], start=True, stop=False, skip_group_check=True)
                for j in range(4):
                    o = ps[QUAD * j:QUAD * j + QUAD, i % 2, :]
                    mm = pe.matmul(o, px[:, 4 * i + j, :], wa[:, i % RW, j, :], start=False, stop=True,
                                   skip_group_check=True)
                mm.then_inc(ffn1, 1)

            def second(i):
                pe.wait_ge(gelu, i + 1)
                if i >= 2:
                    pe.wait_ge(htc, i - 1)
                for c in range(4):
                    mm = pe.transpose(ps[:, 2 + i % 2, 128 * c:128 * c + 128], hs[:, i % 2, 128 * c:128 * c + 128], ident)
                mm.then_inc(htr, 1)
                pe.wait_ge(htc, i + 1)
                pe.wait_ge(wb_in[i % RW], 16 * (i // RW + 1))
                if i >= 2:
                    pe.wait_ge(o_out, i - 1)
                for j in range(4):
                    o = ps[QUAD * j:QUAD * j + QUAD, 4 + i % 2, 0:C]
                    pe.matmul(o, eb[:, 4 * i + j, :], fb2[:, :], start=True, stop=False, skip_group_check=True)
                for c in range(4):
                    for j in range(4):
                        o = ps[QUAD * j:QUAD * j + QUAD, 4 + i % 2, 0:C]
                        mm = pe.matmul(o, ht[:, i % 2, c, QUAD * j:QUAD * j + QUAD], wb[:, i % RW, j, c, :],
                                       start=False, stop=(c == 3), skip_group_check=True)
                mm.then_inc(ffn2, 1)

            for i in range(E // 4):
                first(i)
                if i:
                    second(i - 1)
            second(E // 4 - 1)
            pe.wait_ge(oo_in, 32)
            pe.wait_ge(p_in, 16 * B)
            for n in range(B * GROUPS):
                b, g = divmod(n, GROUPS)
                if n >= 2:
                    pe.wait_ge(sum_out, n - 1)
                h = E * (b % 2)
                for r in range(NT):
                    t = GT * g + 128 * r
                    mm = pe.matmul(ps[:, 6 + n % 2, 128 * r:128 * r + 128], pp[h:h + E, b // 2, t:t + 128],
                                   oo[h:h + E, b, :], start=True, stop=True)
                mm.then_inc(fin, 1)

        @block.scalar
        def _(act):
            act.wait_ge(s_w, N_W)
            act.wait_ge(s_con, 16)
            act.activation(w1s[:, 0, :, :].rearrange("p t c -> p (t c)"), c3[:, 0:9 * C], ACT.Copy)
            act.activation(w2s[:, 0, :, :].rearrange("p t c -> p (t c)"),
                           T[:, 0:18, :].rearrange("p t c -> p (t c)"), ACT.Copy)
            act.activation(identr[:, :], ident, ACT.Copy)
            act.activation(maskr[:, :, :].rearrange("p a n -> p (a n)"), zr[:, 0:2, :].rearrange("p a n -> p (a n)"),
                           ACT.Copy).then_inc(s_seta, 1)
            act.wait_ge(s_set, 1)

            def elu(b, g):
                lo, hi, r = x_rows(g)
                rows = slice(r, r + hi - lo)
                act.wait_ge(x_in[g % 2].sem, x_in[g % 2].at(b, g // 2))
                act.wait_ge(x_low.sem, x_low.at(b, g - 1) if g else x_low.before(b, GROUPS - 1))
                act.activation(el[:, rows, :], xi[:, g % 2, rows, :], ACT.Exp).then_inc(elu_exp.sem, 1)
                act.wait_ge(elu_out.sem, elu_out.at(b, g))
                k = cmm_index[("c1", (g - 2) % GROUPS)]
                act.wait_ge(cmm.sem, cmm.at(b, k) if g >= 2 else cmm.before(b, k))
                act.activation(xp[:, g % 2, 0, rows, 1:1 + IW], el[:, rows, :], ACT.Copy).then_inc(x_high.sem, 1)

            def c1(b, g):
                act.wait_ge(cmm.sem, cmm.at(b, cmm_index[("c1", g)]))
                act.activation(cp[:, 0, GR * g:GR * g + GR, 1:1 + IW],
                               cbank[g % 2].rearrange("p (r w) -> p r w", w=IW),
                               ACT.Identity, bias=cols[:, 0:1]).then_inc(c_high.sem, 1)

            def c2(b, g):
                act.wait_ge(cmm.sem, cmm.at(b, cmm_index[("c2b", g)]))
                act.wait_ge(c3_out.sem, c3_out.at(b, g - 1) if g else c3_out.before(b, GROUPS - 1))
                act.activation(sg[:, :], cbank[1], ACT.Tanh, scale=0.5, bias=hb[:, 0:1]).then_inc(gate_tanh.sem, 1)

            def qkv(b, g):
                act.wait_ge(mmm.sem, mmm.at(b, midx[("q", g)]))
                act.wait_ge(qm_out.sem, qm_out.at(b, g - 2) if g >= 2 else qm_out.before(b, g + 6))
                act.activation(qv[:, g % 2, :], misc(("q", g)), ACT.Identity, scale=0.25,
                               bias=hb[:, 1:2]).then_inc(q_val.sem, 1)
                act.wait_ge(q_st.sem, q_st.at(b, g - 1) if g else q_st.before(b, GROUPS - 1))
                act.activation(qh[:, :], misc(("q", g)), ACT.Identity, scale=0.25,
                               bias=hb[:, 1:2]).then_inc(q_high.sem, 1)
                act.wait_ge(mmm.sem, mmm.at(b, midx[("k", g)]))
                act.wait_ge(k_st.sem, k_st.at(b, g - 1) if g else k_st.before(b, GROUPS - 1))
                act.activation(kv[:, :], misc(("k", g)), ACT.Identity, bias=cols[:, 4:5]).then_inc(k_val.sem, 1)
                act.activation(kh[:, :], misc(("k", g)), ACT.Identity, bias=cols[:, 4:5]).then_inc(k_high.sem, 1)

            def fold(b, g):
                act.wait_ge(fold_sum.sem, fold_sum.at(b, g))
                act.wait_ge(qm_out.sem, qm_out.at(b, g - 1) if g else qm_out.before(b, GROUPS - 1))
                act.activation(fh[:, :], qv[:, g % 2, :], ACT.Copy).then_inc(fold_high.sem, 1)

            def exponentials(b, g, u):
                n = eidx[("exp", g, u)]
                w = sum(GT - max(0, 128 * (i - NT * g)) for i, _ in score_units(g)[u])
                act.wait_ge(smm.sem, smm.at(b, sidx[("exp", g, u)]))
                m = n - ESL if n >= ESL else [m for m in range(NE) if m % ESL == n % ESL][-1]
                act.wait_ge(pv.sem, pv.at(b, m) if n >= ESL else pv.before(b, m))
                act.activation(ex[:, n % ESL, 0:w], sbank[sidx[("exp", g, u)] % SLOTS][:, 0:w],
                               ACT.Exp).then_inc(e_out.sem, 1)

            def mix(b, g):
                act.wait_ge(pv.sem, pv.at(b, eidx[("exp", g, len(score_units(g)) - 1)]))
                k = midx[("mh", (g - 1) % GROUPS)]
                act.wait_ge(mmm.sem, mmm.at(b, k) if g else mmm.before(b, k))
                act.activation(asb[:, :], pvbank, ACT.Copy).then_inc(a_out.sem, 1)

            def norm(b, g):
                act.wait_ge(mmm.sem, mmm.at(b, midx[("zt", g)]))
                act.activation(zt[:, GT * g:GT * g + GT], misc(("zt", g)), ACT.Copy).then_inc(zt_out.sem, 1)

            def logit(b, g):
                act.wait_ge(mmm.sem, mmm.at(b, midx[("z2t", g)]))
                act.activation(z2t[:, :], misc(("z2t", g)), ACT.Copy).then_inc(z2t_out.sem, 1)
                act.wait_ge(mmm.sem, mmm.at(b, midx[("logit", g)]))
                act.wait_ge(p_store.sem, p_store.before(b, 0))
                act.activation(p[:, GT * g:GT * g + GT], misc(("logit", g))[0:E, :], ACT.Identity,
                               bias=cols[0:E, 5:6]).then_inc(logit_out.sem, 1)

            def topk(b):
                act.wait_ge(tkd.sem, tkd.at(b, 0))
                act.activation(p[:, :], p[:, :], ACT.Exp, bias=tk[:, 0:1], accum_out=tk[:, 1:2]).then_inc(tke.sem, 1)

            def pool(b, n):
                act.wait_ge(mmm.sem, mmm.at(b, midx[("pt", n)]))
                act.activation(ptt[:, :, :].rearrange("p t e -> p (t e)"), misc(("pt", n)),
                               ACT.Copy).then_inc(pt_out.sem, 1)

            stages = {"elu": elu, "c1": c1, "c2": c2}
            astages = {"qkv": qkv, "fold": fold, "exp": exponentials, "mix": mix, "norm": norm,
                       "logit": logit, "topk": topk, "pool": pool}

            def run(steps, b, c):
                for st in steps:
                    if st[0] in stages:
                        stages[st[0]](c, *st[1:])
                    if st[0] in astages:
                        astages[st[0]](b, *st[1:])

            run(CONV, None, 0)
            with act.Fori(0, B - 1) as b:
                run(BOTH, b, b + 1)
            run(ATT, B - 1, None)
            for i in range(E // 4):
                act.wait_ge(ffn1, i + 1)
                if i >= 2:
                    act.wait_ge(htr, i - 1)
                act.activation(hs[:, i % 2, :], ps[:, i % 2, :], ACT.Gelu).then_inc(gelu, 1)

        @block.vector
        def _(dve):
            dve.wait_ge(s_con, 16)
            dve.memset(cols[:, :], 0.0).then_inc(s_dset, 1)
            dve.wait_ge(s_dset, 1)
            dve.tensor_copy(cols[:, 4:5], con[:, K_ONE:K_ONE + 1]).then_inc(s_dset, 1)
            dve.memset(wqs[:, :, :], 0.0)
            dve.memset(wvs[:, :], 0.0)
            dve.memset(bvs[:, :], 0.0).then_inc(s_dset, 1)
            dve.memset(zl[:, :], 0.0)
            dve.memset(zt[:, 0:HEADS * C], 0.0)
            dve.wait_ge(s_dset, 3)
            dve.memset(bvs[:, DV:DV + 1], 1.0).then_inc(s_zero, 1)
            dve.wait_ge(s_seta, 1)
            dve.tensor_tensor(w1s[:, 1, :, :].rearrange("p t c -> p (t c)"), c3[:, 0:9 * C],
                              w1s[:, 0, :, :].rearrange("p t c -> p (t c)").bitcast(F32), ALU.subtract)
            dve.tensor_tensor(w2s[:, 1, :, :].rearrange("p t c -> p (t c)"),
                              T[:, 0:18, :].rearrange("p t c -> p (t c)"),
                              w2s[:, 0, :, :].rearrange("p t c -> p (t c)").bitcast(F32), ALU.subtract)
            dve.wait_ge(s_b, N_B)
            dve.tensor_reduce(w3s[:, :], zt[:, 0:HEADS * C].rearrange("p (h c) -> p c h", h=HEADS), AX.X, ALU.add)
            dve.tensor_scalar(hb[:, 0:1], cols[:, 2:3], 0.5, None, ALU.mult)
            dve.tensor_scalar(hb[:, 1:2], cols[:, 3:4], 0.25, None, ALU.mult).then_inc(s_set, 1)
            dve.wait_ge(s_set, 1)

            def elu(b, g):
                lo, hi, r = x_rows(g)
                rows = slice(r, r + hi - lo)
                dve.wait_ge(elu_min.sem, elu_min.at(b, g))
                dve.scalar_tensor_tensor(out=el[:, rows, :], in0=xi[:, g % 2, rows, :], scalar=0.0,
                                         in1=el[:, rows, :], op0=ALU.max, op1=ALU.add).then_inc(elu_out.sem, 1)
                dve.wait_ge(x_high.sem, x_high.at(b, g))
                dve.tensor_tensor(xp[:, g % 2, 1, rows, 1:1 + IW], el[:, rows, :],
                                  xp[:, g % 2, 0, rows, 1:1 + IW].bitcast(F32), ALU.subtract).then_inc(x_low.sem, 1)

            def c1(b, g):
                dve.wait_ge(c_high.sem, c_high.at(b, g))
                here = slice(GR * g, GR * g + GR)
                dve.scalar_tensor_tensor(out=cp[:, 1, here, 1:1 + IW],
                                         in0=cbank[g % 2].rearrange("p (r w) -> p r w", w=IW), scalar=cols[:, 0:1],
                                         in1=cp[:, 0, here, 1:1 + IW].bitcast(F32), op0=ALU.add,
                                         op1=ALU.subtract).then_inc(c_low.sem, 1)

            def c2(b, g):
                dve.wait_ge(gate_half.sem, gate_half.at(b, g))
                dve.wait_ge(cmm.sem, cmm.at(b, cmm_index[("c2a", g)]))
                dve.wait_ge(mmm.sem, mmm.before(b, midx[("ct", g)]))
                dve.scalar_tensor_tensor(out=c3[:, GT * g:GT * g + GT], in0=cbank[0], scalar=cols[:, 1:2],
                                         in1=sg[:, :], op0=ALU.add, op1=ALU.mult).then_inc(c3_out.sem, 1)

            def qkv(b, g):
                dve.wait_ge(q_high.sem, q_high.at(b, g))
                k = sidx[("max", (g - 2) % GROUPS, NT - 1, (g - 2) % GROUPS)]
                dve.wait_ge(smm.sem, smm.at(b, k) if g >= 2 else smm.before(b, k))
                dve.scalar_tensor_tensor(out=qst[:, g % 2, :], in0=qh[:, :].bitcast(F32), scalar=con[:, K_NQ:K_NQ + 1],
                                         in1=qv[:, g % 2, :], op0=ALU.mult, op1=ALU.add).then_inc(q_st.sem, 1)
                dve.wait_ge(k_high.sem, k_high.at(b, g))
                dve.wait_ge(smm.sem, smm.before(b, NS - 1))
                dve.scalar_tensor_tensor(out=kst[:, GT * g:GT * g + GT], in0=kh[:, :].bitcast(F32),
                                         scalar=con[:, K_NK:K_NK + 1], in1=kv[:, :], op0=ALU.mult,
                                         op1=ALU.add).then_inc(k_st.sem, 1)
                dve.wait_ge(mmm.sem, mmm.at(b, midx[("v", g)]))
                dve.wait_ge(pv.sem, pv.before(b, NE - 1))
                bank = misc(("v", g))
                dve.tensor_tensor(vs[:, NT * g:NT * g + NT, :],
                                  bank[:, 0:NT * QUAD].rearrange("p (t d) -> p t d", d=QUAD),
                                  bvs[:, :].unsqueeze(1).broadcast_to([128, NT, QUAD]),
                                  ALU.add).then_inc(v_out.sem, 1)

            def maxima(b, g, r, c):
                st = ("max", g, r, c)
                dve.wait_ge(smm.sem, smm.at(b, sidx[st]))
                if r == 0 and c == 0:
                    dve.wait_ge(nm_out.sem, nm_out.at(b, g - 1) if g else nm_out.before(b, GROUPS - 1))
                w = GT if c < g else 128 * (r + 1)
                dve.tensor_reduce(mpart[:, r, c:c + 1], sbank[sidx[st] % SLOTS][:, 0:w], AX.X,
                                  ALU.max).then_inc(smax.sem, 1)

            def fold(b, g):
                dve.wait_ge(smax.sem, smax.at(b, xidx[("max", g, NT - 1, g)]))
                dve.wait_ge(dg_out.sem, dg_out.at(b, g - 1) if g else dg_out.before(b, GROUPS - 1))
                dve.tensor_reduce(nm[:, :], mpart[:, :, 0:g + 1], AX.X, ALU.max, negate=True).then_inc(nm_out.sem, 1)
                dve.wait_ge(nm_out.sem, nm_out.at(b, g))
                k = midx[("fold", (g - 1) % GROUPS)]
                dve.wait_ge(mmm.sem, mmm.at(b, k) if g else mmm.before(b, k))
                for r in range(NT):
                    ins = dve.tensor_scalar(dg[:, r, :], ident, nm[:, r:r + 1], None, ALU.mult)
                ins.then_inc(dg_out.sem, 1)
                dve.wait_ge(mmm.sem, mmm.at(b, midx[("fold", g)]))
                dve.tensor_tensor(qv[:, g % 2, :], misc(("fold", g)), qv[:, g % 2, :], ALU.add).then_inc(fold_sum.sem, 1)
                dve.wait_ge(fold_high.sem, fold_high.at(b, g))
                h = (g - 1) % GROUPS
                k = sidx[("exp", h, len(score_units(h)) - 1)]
                dve.wait_ge(smm.sem, smm.at(b, k) if g else smm.before(b, k))
                dve.scalar_tensor_tensor(out=qm[:, :], in0=fh[:, :].bitcast(F32), scalar=con[:, K_NQ:K_NQ + 1],
                                         in1=qv[:, g % 2, :], op0=ALU.mult, op1=ALU.add).then_inc(qm_out.sem, 1)

            def mix(b, g):
                dve.wait_ge(mmm.sem, mmm.at(b, midx[("den", g)]))
                dve.wait_ge(t_scaled.sem, t_scaled.at(b, g - 1) if g else t_scaled.before(b, GROUPS - 1))
                dve.tensor_scalar(rd[:, 0, :], misc(("den", g))[:, 0:NT], TINY, None, ALU.add).then_inc(den_sum.sem, 1)
                dve.wait_ge(den_sum.sem, den_sum.at(b, g))
                dve.reciprocal(rd[:, 1, :], rd[:, 0, :]).then_inc(rd_out.sem, 1)
                dve.wait_ge(rd_out.sem, rd_out.at(b, g))
                dve.wait_ge(xb_out.sem, xb_out.at(b, g))
                dve.wait_ge(mmm.sem, mmm.at(b, midx[("mh", g)]))
                dve.wait_ge(t1_store.sem, t1_store.before(b, g))
                dve.wait_ge(tkd.sem, tkd.before(b, 5))
                for r in range(NT):
                    ins = dve.scalar_tensor_tensor(out=T[:, NT * g + r, :], in0=misc(("mh", g))[:, C * r:C * r + C],
                                                   scalar=rd[:, 1, r:r + 1], in1=xn[:, g % 2, r, :],
                                                   op0=ALU.mult, op1=ALU.add)
                ins.then_inc(t_scaled.sem, 1)
                dve.wait_ge(t_scaled.sem, t_scaled.at(b, g))
                dve.wait_ge(mmm.sem, mmm.at(b, midx[("ct", g)]))
                tg = T[:, NT * g:NT * g + NT, :].rearrange("p t c -> p (t c)")
                dve.tensor_tensor(tg, misc(("ct", g)), tg, ALU.add).then_inc(t_out.sem, 1)

            def layer_norm(b, g, summed, st, mean, rstd, out_tiles, out_sig, free):
                dve.wait_ge(summed.sem, summed.at(b, g))
                for r in range(NT):
                    ins = dve.bn_stats(stat[:, r, :], T[:, NT * g + r, :])
                ins.then_inc(st.sem, 1)
                dve.wait_ge(st.sem, st.at(b, g))
                dve.sem_inc(s_held, 1)
                for r in range(NT):
                    ins = dve.bn_aggr(mv[:, r, :], stat[:, r, :])
                ins.then_inc(mean.sem, 1)
                dve.wait_ge(rstd.sem, rstd.at(b, g))
                dve.wait_ge(mean.sem, mean.at(b, g))
                dve.wait_ge(*free)
                for r in range(NT):
                    ins = dve.tensor_scalar(out_tiles[r], T[:, NT * g + r, :], mv[:, r, 0:1], rs[:, 1, r:r + 1],
                                            ALU.subtract, ALU.mult)
                ins.then_inc(out_sig.sem, 1)

            def norm(b, g):
                k = midx[("zt", (g - 1) % GROUPS)]
                layer_norm(b, g, t_out, st1, mv1, rs1, [zr[:, r, :] for r in range(NT)], z_out,
                           (mmm.sem, mmm.at(b, k) if g else mmm.before(b, k)))
                dve.wait_ge(mmm.sem, mmm.at(b, midx[("gram", g)]))
                if g == 0:
                    dve.tensor_copy(G[:, :], misc(("gram", g))[:, 0:C]).then_inc(gram_out.sem, 1)
                else:
                    dve.wait_ge(gram_out.sem, gram_out.at(b, g - 1))
                    dve.tensor_tensor(G[:, :], misc(("gram", g))[:, 0:C], G[:, :], ALU.add).then_inc(gram_out.sem, 1)

            def lin(b, g):
                dve.wait_ge(mmm.sem, mmm.at(b, midx[("lin", g)]))
                tg = T[:, NT * g:NT * g + NT, :].rearrange("p t c -> p (t c)")
                dve.tensor_tensor(tg, misc(("lin", g)), tg, ALU.add).then_inc(t1_out.sem, 1)
                z = [zt[:, GT * g + 128 * r:GT * g + 128 * r + 128] for r in range(NT)]
                layer_norm(b, g, t1_out, st2, mv2, rs2, z, z2_out, (mmm.sem, mmm.at(b, midx[("lin", g)])))

            def topk(b):
                dve.wait_ge(logit_out.sem, logit_out.at(b, GROUPS - 1))
                dve.tensor_reduce(tk[:, 0:1], p[:, :], AX.X, ALU.max, negate=True).then_inc(tkd.sem, 1)
                dve.wait_ge(tke.sem, tke.at(b, 0))
                dve.reciprocal(tk[:, 2:3], tk[:, 1:2]).then_inc(tkd.sem, 1)
                dve.wait_ge(tkd.sem, tkd.at(b, 1))
                dve.tensor_scalar(p[:, :], p[:, :], tk[:, 2:3], None, ALU.mult).then_inc(tkd.sem, 1)
                dve.wait_ge(tkd.sem, tkd.at(b, 2))
                dve.sem_inc(s_held, 1)
                dve.max(tk[:, 4:12], p[:, :]).then_inc(tkd.sem, 1)
                dve.wait_ge(tkd.sem, tkd.at(b, 3))
                dve.wait_ge(t1_store.sem, t1_store.at(b, GROUPS - 1))
                rest = T[0:E, :, :].rearrange("p t c -> p (t c)")
                dve.sem_inc(s_held, 1)
                dve.match_replace(rest, tk[:, 4:12], p[:, :], 0.0).then_inc(tkd.sem, 1)
                dve.wait_ge(tkd.sem, tkd.at(b, 4))
                dve.tensor_tensor(p[:, :], p[:, :], rest, ALU.subtract).then_inc(tkd.sem, 1)

            def pool(b, n):
                dve.wait_ge(mmm.sem, mmm.at(b, midx[("pool", n)]))
                bank = misc(("pool", n))[:, 0:E]
                dve.wait_ge(pool_out.sem, pool_out.at(b, n - 1) if n else pool_out.before(b, 3))
                if n == 0:
                    dve.tensor_copy(pacc[:, :], bank).then_inc(pool_out.sem, 1)
                elif n < 3:
                    dve.tensor_tensor(pacc[:, :], bank, pacc[:, :], ALU.add).then_inc(pool_out.sem, 1)
                else:
                    dve.tensor_tensor(pooled[:, b, :], bank, pacc[:, :], ALU.add).then_inc(pool_out.sem, 1)

            stages = {"elu": elu, "c1": c1, "c2": c2}
            astages = {"qkv": qkv, "max": maxima, "fold": fold, "mix": mix, "norm": norm, "lin": lin,
                       "topk": topk, "pool": pool}

            def run(steps, b, c):
                for st in steps:
                    if st[0] in stages:
                        stages[st[0]](c, *st[1:])
                    if st[0] in astages:
                        astages[st[0]](b, *st[1:])

            run(CONV, None, 0)
            with dve.Fori(0, B - 1) as b:
                run(BOTH, b, b + 1)
            run(ATT, B - 1, None)

            last = B - 1
            dve.wait_ge(pool_out.sem, pool_out.at(last, 3))
            dve.wait_ge(t1_store.sem, t1_store.at(last, GROUPS - 1))
            dve.wait_ge(p_store.sem, p_store.at(last, 0))
            dve.memset(px[:, :, :], 0.0).then_inc(s_dset, 1)
            dve.wait_ge(s_dset, 4)
            dve.tensor_copy(px[:, :, 0:B], pooled[:, :, :].rearrange("p b e -> p e b")).then_inc(s_px, 1)
            dve.tensor_copy(eb[:, :, :], con[0:E, K_ID:K_ID + E].unsqueeze(2).broadcast_to([E, E, QUAD])).then_inc(s_px, 1)
            for i in range(E // 4):
                dve.wait_ge(htr, i + 1)
                if i >= 2:
                    dve.wait_ge(ffn2, i - 1)
                dve.tensor_copy(ht[:, i % 2, :, :].rearrange("p c n -> p (c n)"), ps[:, 2 + i % 2, :]).then_inc(htc, 1)
                if i:
                    dve.wait_ge(ffn2, i)
                    dve.tensor_copy(oall[:, i - 1, :], ps[:, 4 + (i - 1) % 2, 0:C]).then_inc(o_out, 1)
            dve.wait_ge(ffn2, E // 4)
            dve.tensor_copy(oall[:, E // 4 - 1, :], ps[:, 4 + (E // 4 - 1) % 2, 0:C]).then_inc(o_out, 1)
            for n in range(B * GROUPS):
                dve.wait_ge(fin, n + 1)
                dve.wait_ge(tl_in[n % LT], 16 * (n // LT + 1))
                t = tl[:, n % LT, :, :].rearrange("p t c -> p (t c)")
                dve.tensor_tensor(t, ps[:, 6 + n % 2, :], t, ALU.add).then_inc(sum_out, 1)

        @block.gpsimd
        def _(pool_e):
            for s_ in range(2):
                for h in range(2):
                    for col in (0, PW - 1):
                        pool_e.memset(xp[:, s_, h, :, col:col + 1].bitcast(F32), 0.0)
            for col in (0, PW - 1):
                ins = pool_e.memset(cp[:, :, :, col:col + 1].bitcast(F32), 0.0)
            ins.then_inc(s_setp, 1)
            pool_e.wait_ge(s_w, N_W)
            pool_e.wait_ge(s_con, 16)

            def elu(b, g):
                lo, hi, r = x_rows(g)
                rows = slice(r, r + hi - lo)
                pool_e.wait_ge(elu_exp.sem, elu_exp.at(b, g))
                pool_e.sem_inc(s_held, 1)
                pool_e.tensor_scalar(el[:, rows, :], el[:, rows, :], 1.0, -1.0, ALU.min, ALU.add).then_inc(elu_min.sem, 1)

            def c2(b, g):
                pool_e.wait_ge(gate_tanh.sem, gate_tanh.at(b, g))
                pool_e.sem_inc(s_held, 1)
                pool_e.tensor_scalar(sg[:, :], sg[:, :], 0.5, 0.5, ALU.mult, ALU.add).then_inc(gate_half.sem, 1)

            def bias(b, g):
                pool_e.wait_ge(xn_in[g % 2].sem, xn_in[g % 2].at(b, g // 2))
                pool_e.tensor_tensor(xn[:, g % 2, :, :], xn[:, g % 2, :, :],
                                     b3s[:, :].unsqueeze(1).broadcast_to([128, NT, C]), ALU.add).then_inc(xb_out.sem, 1)

            def rstd(b, g, mean, ve, out_sig, reader, last):
                pool_e.wait_ge(mean.sem, mean.at(b, g))
                pool_e.wait_ge(reader.sem, last)
                pool_e.sem_inc(s_held, 1)
                pool_e.tensor_scalar(rs[:, 0, :], mv[:, :, 1:2].rearrange("p t a -> p (t a)"), EPS, None,
                                     ALU.add).then_inc(ve.sem, 1)
                pool_e.wait_ge(ve.sem, ve.at(b, g))
                pool_e.tensor_tensor(rs[:, 1, :], rs[:, 0, :], con[:, K_POW:K_POW + NT], ALU.pow).then_inc(out_sig.sem, 1)

            def norm(b, g):
                rstd(b, g, mv1, ve1, rs1, z_out if g else z2_out,
                     z_out.at(b, g - 1) if g else z2_out.before(b, GROUPS - 1))

            def lin(b, g):
                rstd(b, g, mv2, ve2, rs2, z2_out if g else z_out,
                     z2_out.at(b, g - 1) if g else z_out.at(b, GROUPS - 1))

            stages = {"elu": elu, "c2": c2}
            astages = {"mix": bias, "norm": norm, "lin": lin}

            def run(steps, b, c):
                for st in steps:
                    if st[0] in stages:
                        stages[st[0]](c, *st[1:])
                    if st[0] in astages:
                        astages[st[0]](b, *st[1:])

            run(CONV, None, 0)
            with pool_e.Fori(0, B - 1) as b:
                run(BOTH, b, b + 1)
            run(ATT, B - 1, None)


def kernel(x, L0_conv_W1, L0_conv_b1, L0_conv_W2, L0_conv_b2, L0_conv_Wq, L0_conv_bq, L0_conv_Wk, L0_conv_bk,
           L0_conv_Wv, L0_conv_bv, L0_conv_W3, L0_conv_b3, L1_ffn_gate_w, L1_ffn_gate_b, L1_ffn_weight1,
           L1_ffn_weight2):
    import numpy as np
    import concourse.bacc as bacc
    from concourse.bass_utils import run_bass_kernel_spmd

    con = np.zeros((128, K_END), np.float32)
    i = np.arange(128)
    con[:, K_ID:K_ID + 128] = np.eye(128)
    masks = np.zeros((128, 2, 128), np.float32)
    masks[:, 0] = np.where(i[None, :] >= i[:, None], -1e10, 0.0)
    masks[:, 1] = np.where(i[:, None] >= i[None, :], -1e30, 0.0)
    con[:, K_SEL + DK] = con[:, K_SEL + QUAD + DK] = 1.0
    con[DV::QUAD, K_DEN] = 1.0
    con[:, K_NQ] = np.where(i // QUAD % 2 == 1, -1.0, 0.0)
    con[:, K_NK] = np.where(i // QUAD >= 2, -1.0, 0.0)
    con[[DK, QUAD + DK], K_ONE] = 1.0
    con[:, K_POW:K_POW + NT] = -0.5

    a = {
        "x_cm": x.reshape(B, TOK, C).transpose(0, 2, 1),
        "x_nat": x.reshape(B, GROUPS, NT, 128, C).transpose(0, 1, 3, 2, 4),
        "w1": L0_conv_W1.reshape(9, C, C).transpose(1, 0, 2),
        "b1": L0_conv_b1.reshape(C, 1),
        "w2": L0_conv_W2.reshape(9, C, 2 * C).transpose(1, 0, 2),
        "b2": L0_conv_b2.reshape(2, C).T,
        "wq": L0_conv_Wq, "bq": L0_conv_bq.reshape(DK, 1),
        "wk": L0_conv_Wk, "bk": L0_conv_bk.reshape(DK, 1),
        "wv": L0_conv_Wv, "bv": L0_conv_bv,
        "w3": L0_conv_W3.reshape(HEADS, DV, C).transpose(1, 0, 2).reshape(DV, HEADS * C),
        "b3": L0_conv_b3,
        "gate_wt": L1_ffn_gate_w.T,
        "gate_b": L1_ffn_gate_b.reshape(E, 1),
        "f1": L1_ffn_weight1[:, :C, :].transpose(1, 0, 2),
        "f1b": L1_ffn_weight1[:, C, :],
        "f2": L1_ffn_weight2[:, :HID, :].reshape(E, 4, 128, C).transpose(2, 0, 1, 3),
        "f2b": L1_ffn_weight2[:, HID, :],
        "consts": con,
        "masks": masks,
    }
    nc = bacc.Bacc("TRN2", target_bir_lowering=False, num_devices=1)
    arrays, aps = {}, {}
    for name, v in a.items():
        v = np.ascontiguousarray(v)
        arrays["in_" + name] = v
        aps[name] = nc.dram_tensor("in_" + name, v.shape, mybir.dt.from_np(v.dtype), kind="ExternalInput").ap()
    aps["out"] = nc.dram_tensor("out_tokens", (B, GROUPS, 128, NT, C), F32, kind="ExternalOutput").ap()
    aps["t1_dram"] = nc.dram_tensor("t1_scratch", (B, GROUPS, 128, NT, C), F32).ap()
    aps["p_dram"] = nc.dram_tensor("p_scratch", (B, E, TOK), F32).ap()
    aps["o_dram"] = nc.dram_tensor("o_scratch", (B, E, C), F32).ap()
    program(nc, **aps)
    r = run_bass_kernel_spmd(nc, [arrays], core_ids=[0])
    o = r.results[0]["out_tokens"]
    return o.transpose(0, 1, 3, 2, 4).reshape(B, IH, IW, C)
```

```python
from contextlib import ExitStack

import concourse.bass as bass
from concourse import mybir

F32 = mybir.dt.float32
F32R = mybir.dt.float32r
ALU = mybir.AluOpType
ACT = mybir.ActivationFunctionType
AX = mybir.AxisListType

B, IH, IW, C = 4, 64, 64, 128
TOK = IH * IW
GROUPS = 8
GT = TOK // GROUPS
GR = IH // GROUPS
NT = GT // 128
PW = IW + 2
DK, DV, HEADS = 4, 16, 8
E, HID, KTOP = 64, 512, 8
SLOTS = 3
ESL = 3
QUAD = 32
TINY = 1e-10
EPS = 1e-5
K_ID, K_SEL, K_DEN, K_NQ, K_NK, K_ONE, K_POW, K_END = 0, 128, 256, 257, 258, 259, 260, 264


class Signal:

    def __init__(self, sem, per, unit=1):
        self.sem, self.per, self.unit = sem, per, unit

    def at(self, b, k):
        return (b * self.per + (self.per + k + 1)) * self.unit

    def before(self, b, k):
        return (b * self.per + (k + 1)) * self.unit


def score_units(g):
    whole = [[(i, 0)] for i in range(NT * g)]
    d = NT * g
    return whole + [[(d, 0)], [(d + 1, 128), (d + 3, 384)], [(d + 2, 256)]]


def attention_steps():
    out = [("qkv", 0), ("qkv", 1), ("stack", 0), ("stack", 1)]
    out += [("max", 0, r, 0) for r in range(NT)]
    out += [("negmax", 0), ("fold", 0), ("foldhigh", 0)]
    for g in range(GROUPS):
        out += [("foldq", g)]
        exps = [("exp", g, u) for u in range(len(score_units(g)))]
        maxs, side = [], []
        if g + 1 < GROUPS:
            maxs = [("max", g + 1, r, c) for c in range(g + 2) for r in range(NT)]
        if g:
            side += [("den", g - 1), ("mix", g - 1)]
        if g + 2 < GROUPS:
            side += [("qkv", g + 2), ("stack", g + 2)]
        if g > 1:
            side += [("gram", g - 2)]
        if g:
            side += [("stats", g - 1), ("z", g - 1)]
        early = max(1, len(exps) * 3 // 4)
        body = [[] for _ in exps]
        for n, m in enumerate(maxs):
            body[min(n * early // len(maxs), len(exps) - 1)].append(m)
        for n, m in enumerate(side):
            body[n * len(exps) // len(side)].append(m)
        if maxs:
            body[min(early, len(exps) - 1)].append(("negmax", g + 1))
            body[min(early + 1, len(exps) - 1)].append(("fold", g + 1))
            body[-1].append(("foldhigh", g + 1))
        for e, more in zip(exps, body):
            out += [e] + more
        out += [("copy", g)]
    g = GROUPS - 1
    out += [("gram", g - 1), ("den", g), ("mix", g), ("stats", g), ("z", g), ("gram", g)]
    for g in range(GROUPS + 3):
        if g < GROUPS:
            out += [("lin", g)]
        if 0 <= g - 1 < GROUPS:
            out += [("z2", g - 1)]
        if 0 <= g - 2 < GROUPS:
            out += [("z2t", g - 2)]
        if 0 <= g - 3 < GROUPS:
            out += [("logit", g - 3)]
    out += [("topk", n) for n in range(6)]
    for n in range(5):
        if n < 4:
            out += [("turn", n)]
        if n:
            out += [("pool", n - 1)]
    return out


def conv_steps():
    runs = []
    for g in range(-2, GROUPS):
        if g + 2 < GROUPS:
            runs += [("c1", g + 2, n) for n in range(3)]
        if g >= 0:
            runs += [("c2b", g, n) for n in range(3)] + [("c2a", g, n) for n in range(3)]
    out = [[("load", 0), ("load", 1), ("exp_x", 0), ("elu", 0), ("high_x", 0), ("low_x", 0), ("exp_x", 1)]]
    out += [[r] for r in runs]
    for n, (k, g, part) in enumerate(runs):
        def later(d, *steps):
            out[min(n + 1 + d, len(runs))] += steps
        if part == 2:
            if k == "c1":
                later(1, ("high_c", g), ("low_c", g))
            if k == "c2b":
                later(1, ("tanh", g))
            if k == "c2a":
                later(1, ("gate", g))
        if k == "c1" and g + 1 < GROUPS:
            if part == 0:
                if g + 2 < GROUPS:
                    later(0, ("load", g + 2))
                later(0, ("elu", g + 1))
            if part == 1:
                later(0, ("high_x", g + 1), ("low_x", g + 1))
            if part == 2 and g + 2 < GROUPS:
                later(0, ("exp_x", g + 2))
    return out


SLACK = {"topk": 3.0, "turn": 1.0, "pool": 1.0, "lin": 1.0, "z2": 0.5, "negmax": 1.0, "fold": 1.0, "foldhigh": 1.0,
         "copy": 1.0, "foldq": 0.5, "den": 0.5, "mix": 0.5, "z": 0.3, "gram": 0.3, "max": 0.05, "exp": 0.1,
         "qkv": 0.3, "stack": 0.3}


def merged():
    att, conv = attention_steps(), conv_steps()
    total = sum(SLACK.get(st[0], 0.0) for st in att)
    out, given, n = list(conv[0]), 0.0, 1
    mixed = set()

    def ready(steps):
        return all(st[0] != "gate" or st[1] in mixed for st in steps)

    for st in att:
        out.append(st)
        if st[0] == "mix":
            mixed.add(st[1])
        given += SLACK.get(st[0], 0.0)
        while n < len(conv) and n - 1 < given / total * (len(conv) - 1) and ready(conv[n]):
            out += conv[n]
            n += 1
    for more in conv[n:]:
        out += more
    return out


def program(nc, x_cm, x_nat, w1, b1, w2, b2, wq, bq, wk, bk, wv, bv, w3, b3, gate_wt, gate_b,
            f1, f1b, f2, f2b, consts, masks, out, t1_dram, p_dram, o_dram):
    ATT, CONV, BOTH = attention_steps(), sum(conv_steps(), []), merged()
    misc_order, score_order, conv_order = [], [], []
    uses = {"qkv": ("q", "k", "v"), "fold": ("fold",), "den": ("den",), "mix": ("mh", "ct"), "gram": ("gram", "zt"),
            "lin": ("lin",), "z2t": ("z2t",), "logit": ("logit",), "turn": ("pt",), "pool": ("pool",)}
    for st in ATT:
        misc_order += [(k, st[1]) for k in uses.get(st[0], ())]
        if st[0] in ("max", "exp"):
            score_order.append(st)
    for st in CONV:
        if st[0] in ("c1", "c2a", "c2b") and st[2] == 2:
            conv_order.append(st[:2])
    NM, NS = len(misc_order), len(score_order)
    exp_order = [st for st in score_order if st[0] == "exp"]
    NE = len(exp_order)

    ctx = ExitStack()
    loopctx = ExitStack()

    def sb(name, shape, dt=F32, c=None):
        return (c or loopctx).enter_context(nc.sbuf_tensor(name, shape, dt))

    def semaphore(name):
        return ctx.enter_context(nc.semaphore(name))

    signals = []

    def signal(name, per, unit=1):
        s = Signal(semaphore(name), per, unit)
        signals.append(s)
        return s

    with ctx:
        ps = ctx.enter_context(nc.psum_tensor("ps", [128, 8, 512], F32))
        cbank = [ps[:, 0, :], ps[:, 1, :]]
        sbank = [ps[:, 2 + n, :] for n in range(SLOTS)]
        pvbank = ps[:, 5, :]
        mbank = [ps[:, 6, :], ps[:, 7, :]]

        con = sb("con", [128, K_END], c=ctx)
        ident = con[:, K_ID:K_ID + 128]
        pooled = sb("pooled", [128, B, E], c=ctx)

        identr = sb("identr", [128, 128], F32R)
        maskr = sb("maskr", [128, 2, 128], F32R)
        wqs = sb("wqs", [128, 2, 128])
        wvs = sb("wvs", [128, QUAD])
        bvs = sb("bvs", [128, QUAD])
        w3s = sb("w3s", [128, C])
        b3s = sb("b3s", [128, C])
        gws = sb("gws", [128, E])
        cols = sb("cols", [128, 8])
        c3 = sb("c3", [128, TOK])
        qv = sb("qv", [128, 2, GT])
        qh = sb("qh", [128, GT], F32R)
        kv = sb("kv", [128, GT])
        kh = sb("kh", [128, GT], F32R)
        qst = sb("qst", [128, 2, GT], F32R)
        qm = sb("qm", [128, GT], F32R)
        kst = sb("kst", [128, TOK], F32R)
        vs = sb("vs", [128, TOK // 128, QUAD])
        zl = sb("zl", [128, QUAD])
        hb = sb("hb", [128, 2])
        fh = sb("fh", [128, GT], F32R)
        mpart = sb("mpart", [128, NT, GROUPS])
        nm = sb("nm", [128, NT])
        dg = sb("dg", [128, NT, 128])
        ex = sb("ex", [128, ESL, GT])
        asb = sb("asb", [128, GT])
        xn = sb("xn", [128, 2, NT, C])
        rd = sb("rd", [128, 2, NT])
        T = sb("T", [128, TOK // 128, C])
        stat = sb("stat", [128, NT, 6])
        mv = sb("mv", [128, 2, NT, 2])
        rs = sb("rs", [128, 2, 2, NT])
        zr = sb("zr", [128, NT, C])
        zt = sb("zt", [128, TOK])
        G = sb("G", [128, C])
        z2t = sb("z2t", [128, GT])
        p = sb("p", [E, TOK])
        ptt = z2t[:, :].rearrange("p (t e) -> p t e", e=E)
        pacc = sb("pacc", [128, E])
        tk = sb("tk", [E, 12])
        w1s = sb("w1s", [128, 2, 9, C], F32R)
        w2s = sb("w2s", [128, 2, 9, 2 * C], F32R)
        xi = sb("xi", [128, 2, GR + 2, IW])
        el = sb("el", [128, GR + 2, IW])
        xp = sb("xp", [128, 2, 2, GR + 2, PW], F32R)
        cp = sb("cp", [128, 2, IH, PW], F32R)
        sg = sb("sg", [128, GT])
        loopctx.close()

        tail = ExitStack()
        RW = 4
        wa = sb("wa", [128, RW, 4, HID], c=tail)
        wb = sb("wb", [128, RW, 4, 4, C], c=tail)
        fb1 = sb("fb1", [E, HID], c=tail)
        fb2 = sb("fb2", [E, C], c=tail)
        px = sb("px", [128, E, QUAD], c=tail)
        eb = sb("eb", [E, E, QUAD], c=tail)
        hs = sb("hs", [128, 2, HID], c=tail)
        ht = sb("ht", [128, 2, 4, 128], c=tail)
        oall = sb("oall", [128, E // 4, C], c=tail)
        oo = sb("oo", [128, B, C], c=tail)
        pp = sb("pp", [128, 2, TOK], c=tail)
        LT = 4
        tl = sb("tl", [128, LT, NT, C], c=tail)
        tail.close()

        s_con, s_w, s_b = semaphore("consts_in"), semaphore("weights_in"), semaphore("biases_in")
        s_zero, s_set, s_setp, s_seta = (semaphore(n) for n in ("zeroed", "setup_dve", "setup_pool", "setup_act"))
        s_dset = semaphore("setup_steps")
        s_held = semaphore("held")
        x_in = [signal(f"x_in{n}", GROUPS // 2, 16) for n in range(2)]
        elu_exp = signal("elu_exp", GROUPS)
        elu_min = signal("elu_min", GROUPS)
        elu_out = signal("elu_out", GROUPS)
        x_high = signal("x_high", GROUPS)
        x_low = signal("x_low", GROUPS)
        cmm = signal("conv_products", 3 * GROUPS)
        c_high = signal("c_high", GROUPS)
        c_low = signal("c_low", GROUPS)
        gate_tanh = signal("gate_tanh", GROUPS)
        gate_half = signal("gate_half", GROUPS)
        c3_out = signal("c3_out", GROUPS)
        cmm_index = {k: n for n, k in enumerate(conv_order)}
        mmm = signal("misc_products", NM)
        smm = signal("scores", NS)
        q_val, q_high, q_st = (signal(n, GROUPS) for n in ("q_value", "q_high", "q_stacked"))
        k_val, k_high, k_st = (signal(n, GROUPS) for n in ("k_value", "k_high", "k_stacked"))
        v_out = signal("v_out", GROUPS)
        smax = signal("max_parts", NS - NE)
        nm_out = signal("neg_max", GROUPS)
        dg_out = signal("max_diagonal", GROUPS)
        fold_sum, fold_high, qm_out = (signal(n, GROUPS) for n in ("fold_sum", "fold_high", "q_with_max"))
        e_out = signal("exponentials", NE)
        pv = signal("pv_used", NE)
        a_out = signal("attention_copied", GROUPS)
        xn_in = [signal(f"xn_in{n}", GROUPS // 2, 16) for n in range(2)]
        xb_out = signal("x_plus_b3", GROUPS)
        den_sum, rd_out = signal("den_sum", GROUPS), signal("den_reciprocal", GROUPS)
        t_scaled, t_out = signal("t_scaled", GROUPS), signal("t_out", GROUPS)
        st1, mv1, ve1, rs1 = (signal(n, GROUPS) for n in ("ln1_stats", "ln1_mean_var", "ln1_var_eps", "ln1_rstd"))
        z_out, gram_out, zt_out = (signal(n, GROUPS) for n in ("z_out", "gram_out", "z_transposed"))
        t1_out = signal("t1_out", GROUPS)
        t1_store = signal("t1_stored", GROUPS, 16)
        st2, mv2, ve2, rs2 = (signal(n, GROUPS) for n in ("ln2_stats", "ln2_mean_var", "ln2_var_eps", "ln2_rstd"))
        z2_out, z2t_out, logit_out = (signal(n, GROUPS) for n in ("z2_out", "z2_transposed", "logits_out"))
        tkd = signal("topk_steps", 6)
        tke = signal("topk_exp", 1)
        p_store = signal("p_stored", 1, 16)
        pt_out, pool_out = signal("p_transposed", 4), signal("pooled_part", 4)

        midx = {k: n for n, k in enumerate(misc_order)}
        sidx = {k: n for n, k in enumerate(score_order)}
        eidx = {k: n for n, k in enumerate(exp_order)}

        xidx = {st: n for n, st in enumerate(st for st in score_order if st[0] == "max")}
        readers = {"q": q_high, "k": k_high, "v": v_out, "fold": fold_sum, "den": den_sum, "mh": t_scaled,
                   "ct": t_out, "gram": gram_out, "zt": zt_out, "lin": t1_out, "z2t": z2t_out,
                   "logit": logit_out, "pt": pt_out, "pool": pool_out, "c1": c_low, "c2a": c3_out,
                   "c2b": gate_tanh}

        def read_of(key):
            if key[0] == "max":
                return smax, xidx[key]
            if key[0] == "exp":
                return e_out, eidx[key]
            return readers[key[0]], key[1]

        def reused(order, bank_of, n, b):
            same = [m for m in range(n) if bank_of(m) == bank_of(n)]
            if same:
                s, k = read_of(order[same[-1]])
                return s.sem, s.at(b, k)
            s, k = read_of(order[[m for m in range(len(order)) if bank_of(m) == bank_of(n)][-1]])
            return s.sem, s.before(b, k)

        def conv_bank(key):
            return cbank[cmm_index[key] % 2]

        def misc(key):
            return mbank[midx[key] % 2]

        def x_rows(g):
            lo, hi = max(GR * g - 1, 0), min(GR * g + GR + 1, IH)
            return lo, hi, lo - (GR * g - 1)

        s_fb = semaphore("ffn_biases_in")
        wa_in = [semaphore(f"wa_in{n}") for n in range(RW)]
        wb_in = [semaphore(f"wb_in{n}") for n in range(RW)]
        ffn1, ffn2, gelu, htr, htc = (semaphore(n) for n in ("ffn1", "ffn2", "gelu", "h_transposed", "h_copied"))
        p_in, o_out, o_stored, oo_in = (semaphore(n) for n in ("p_in", "o_out", "o_stored", "oo_in"))
        tl_in = [semaphore(f"tl_in{n}") for n in range(LT)]
        out_st = [semaphore(f"out_stored{n}") for n in range(LT)]
        sum_out, fin, s_px = semaphore("sum_out"), semaphore("final_products"), semaphore("ffn_operands")

        N_W, N_B = 16 * 5, 16 * (16 + 4 + 5)
        block = ctx.enter_context(nc.Block())

        @block.sync
        def _(sp):
            for s in signals:
                sp.sem_inc(s.sem, s.per * s.unit)
            sp.dma_start(con[:, :], consts).then_inc(s_con, 16)
            sp.dma_start(zr[:, 0:2, :], masks).then_inc(s_w, 16)
            sp.dma_start(c3[:, 0:9 * C], w1.rearrange("p t c -> p (t c)")).then_inc(s_w, 16)
            sp.dma_start(T[:, :, :].rearrange("p t c -> p (t c)")[:, 0:18 * C],
                         w2.rearrange("p t c -> p (t c)")).then_inc(s_w, 16)
            sp.dma_start(gws[:, :], gate_wt).then_inc(s_w, 16)
            sp.dma_start(b3s[:, :], b3.partition_broadcast(128)).then_inc(s_w, 16)
            sp.wait_ge(s_zero, 1)
            for q in range(4):
                sp.dma_start(wqs[:, 0, QUAD * q:QUAD * q + DK], wq).then_inc(s_b, 16)
                sp.dma_start(wqs[:, 1, QUAD * q:QUAD * q + DK], wk).then_inc(s_b, 16)
                sp.dma_start(cols[QUAD * q:QUAD * q + DK, 3:4], bq).then_inc(s_b, 16)
                sp.dma_start(cols[QUAD * q:QUAD * q + DK, 4:5], bk).then_inc(s_b, 16)
            for q in range(4):
                sp.dma_start(zt[QUAD * q:QUAD * q + DV, 0:HEADS * C], w3).then_inc(s_b, 16)
            sp.dma_start(wvs[:, 0:DV], wv).then_inc(s_b, 16)
            sp.dma_start(bvs[:, 0:DV], bv.partition_broadcast(128)).then_inc(s_b, 16)
            sp.dma_start(cols[:, 0:1], b1).then_inc(s_b, 16)
            sp.dma_start(cols[:, 1:3], b2).then_inc(s_b, 16)
            sp.dma_start(cols[0:E, 5:6], gate_b).then_inc(s_b, 16)

            def load(b, g):
                sp.wait_ge(elu_out.sem, elu_out.at(b, g - 2) if g >= 2 else elu_out.before(b, g + 6))
                lo, hi, r = x_rows(g)
                sp.dma_start(xi[:, g % 2, r:r + hi - lo, :].rearrange("p r w -> p (r w)"),
                             x_cm[b, :, lo * IW:hi * IW]).then_inc(x_in[g % 2].sem, 16)

            def load_nat(b, g):
                sp.wait_ge(t_scaled.sem, t_scaled.at(b, g - 2) if g >= 2 else t_scaled.before(b, g + 6))
                sp.dma_start(xn[:, g % 2, :, :], x_nat[b, g, :, :, :]).then_inc(xn_in[g % 2].sem, 16)

            def store_t1(b, g):
                sp.wait_ge(t1_out.sem, t1_out.at(b, g))
                sp.dma_start(t1_dram[b, g, :, :, :], T[:, NT * g:NT * g + NT, :]).then_inc(t1_store.sem, 16)

            def store_p(b):
                sp.wait_ge(tkd.sem, tkd.at(b, 5))
                sp.dma_start(p_dram[b, :, :], p[:, :]).then_inc(p_store.sem, 16)

            def run(steps, b, c):
                for st in steps:
                    if st[0] == "load":
                        load(c, st[1])
                    if st[0] == "foldq":
                        load_nat(b, st[1])
                    if st[0] == "lin":
                        store_t1(b, st[1])
                    if st == ("topk", 5):
                        store_p(b)

            run(CONV, None, 0)
            with sp.Fori(0, B - 1) as b:
                run(BOTH, b, b + 1)
            run(ATT, B - 1, None)

            last = B - 1
            sp.wait_ge(pool_out.sem, pool_out.at(last, 3))
            sp.wait_ge(p_store.sem, p_store.at(last, 0))
            sp.wait_ge(t1_store.sem, t1_store.at(last, GROUPS - 1))
            sp.dma_start(fb1[:, :], f1b).then_inc(s_fb, 16)
            sp.dma_start(fb2[:, :], f2b).then_inc(s_fb, 16)
            for i in range(E // 4):
                if i >= RW:
                    sp.wait_ge(ffn1, i - RW + 1)
                sp.dma_start(wa[:, i % RW, :, :], f1[:, 4 * i:4 * i + 4, :]).then_inc(wa_in[i % RW], 16)
                if i >= RW:
                    sp.wait_ge(ffn2, i - RW + 1)
                sp.dma_start(wb[:, i % RW, :, :, :], f2[:, 4 * i:4 * i + 4, :, :]).then_inc(wb_in[i % RW], 16)
                if i % 4 == 3:
                    n = i // 4
                    sp.dma_start(pp[E * (n % 2):E * (n % 2) + E, n // 2, :], p_dram[n, :, :]).then_inc(p_in, 16)
            for n in range(LT):
                sp.dma_start(tl[:, n, :, :], t1_dram[n // GROUPS, n % GROUPS, :, :, :]).then_inc(tl_in[n], 16)
            sp.wait_ge(o_out, E // 4)
            for n in range(B):
                sp.dma_start(o_dram[n, :, :].rearrange("(i j) o -> j i o", j=4),
                             oall[n:128:QUAD, :, :]).then_inc(o_stored, 16)
            sp.wait_ge(o_stored, 16 * B)
            for h in range(2):
                sp.dma_start(oo[E * h:E * h + E, :, :], o_dram.rearrange("b e o -> e b o")).then_inc(oo_in, 16)
            for n in range(B * GROUPS):
                sp.wait_ge(sum_out, n + 1)
                sp.dma_start(out[n // GROUPS, n % GROUPS, :, :, :], tl[:, n % LT, :, :]).then_inc(out_st[n % LT], 16)
                m = n + LT
                if m < B * GROUPS:
                    sp.wait_ge(out_st[n % LT], 16 * (n // LT + 1))
                    sp.dma_start(tl[:, n % LT, :, :], t1_dram[m // GROUPS, m % GROUPS, :, :, :]).then_inc(tl_in[n % LT], 16)
            for n in range(LT):
                sp.wait_ge(out_st[n], 16 * (B * GROUPS // LT))



        @block.tensor
        def _(pe):
            pe.wait_ge(s_setp, 1)
            pe.wait_ge(s_set, 1)
            pe.wait_ge(s_seta, 1)

            def conv(bank, w, lo, x, part, rows):
                acc = bank.rearrange("p (r w) -> p r w", w=IW)
                dy = (1, 0, 2)[part]
                src, dst = rows(dy)
                for dx in range(3):
                    for wi, xi_ in ((0, 0), (0, 1), (1, 0)):
                        first, last = part == dx == wi == xi_ == 0, part == dx == 2 and wi == 1
                        mm = pe.matmul(acc[:, dst, :], w[:, wi, 3 * dy + dx, lo:lo + C],
                                       x[:, xi_, src, dx:dx + IW], start=first, stop=last)
                if part == 2:
                    mm.then_inc(cmm.sem, 1)

            def edges(g, dy):
                return (1 if g == 0 and dy == 0 else 0), (GR - 1 if g == GROUPS - 1 and dy == 2 else GR)

            def bank_wait(key, b):
                pe.wait_ge(*reused(conv_order, lambda m: m % 2, cmm_index[key], b))

            def c1(b, g, part):
                def rows(dy):
                    r0, r1 = edges(g, dy)
                    return slice(r0 + dy, r1 + dy), slice(r0, r1)
                if part == 0:
                    pe.wait_ge(x_low.sem, x_low.at(b, g))
                    bank_wait(("c1", g), b)
                conv(conv_bank(("c1", g)), w1s, 0, xp[:, g % 2], part, rows)

            def c2(b, g, part, key, half):
                def rows(dy):
                    r0, r1 = edges(g, dy)
                    return slice(GR * g + r0 + dy - 1, GR * g + r1 + dy - 1), slice(r0, r1)
                if part == 0:
                    if half:
                        pe.wait_ge(c_low.sem, c_low.at(b, min(g + 1, GROUPS - 1)))
                    bank_wait((key, g), b)
                conv(conv_bank((key, g)), w2s, half * C, cp, part, rows)

            def misc_bank(b, key):
                pe.wait_ge(*reused(misc_order, lambda m: m % 2, midx[key], b))
                return misc(key)

            def qkv(b, g):
                x = c3[:, GT * g:GT * g + GT]
                pe.wait_ge(c3_out.sem, c3_out.at(b, g))
                bank = misc_bank(b, ("q", g))
                pe.matmul(bank, wqs[:, 0, :], x, start=True, stop=True).then_inc(mmm.sem, 1)
                bank = misc_bank(b, ("k", g))
                pe.matmul(bank, wqs[:, 1, :], x, start=True, stop=True).then_inc(mmm.sem, 1)
                bank = misc_bank(b, ("v", g))
                for r in range(NT):
                    mm = pe.matmul(bank[:, QUAD * r:QUAD * r + QUAD], x[:, 128 * r:128 * r + 128], wvs[:, :],
                                   start=True, stop=True)
                mm.then_inc(mmm.sem, 1)

            def score_bank(b, st):
                n = sidx[st]
                pe.wait_ge(*reused(score_order, lambda m: m % SLOTS, n, b))
                return sbank[n % SLOTS]

            def max_scores(b, g, r, c):
                if r == 0 and c == 0:
                    pe.wait_ge(k_st.sem, k_st.at(b, g))
                bank = score_bank(b, ("max", g, r, c))
                w = GT if c < g else 128 * (r + 1)
                mm = pe.matmul(bank[:, 0:w], qst[:, g % 2, 128 * r:128 * r + 128], kst[:, GT * c:GT * c + w],
                               start=True, stop=(c < g))
                if c == g:
                    mm = pe.matmul(bank[:, w - 128:w], identr[:, :], maskr[:, 0, :], start=False, stop=True)
                mm.then_inc(smm.sem, 1)

            def fold(b, g):
                pe.wait_ge(dg_out.sem, dg_out.at(b, g))
                bank = misc_bank(b, ("fold", g))
                pe.matmul(bank, con[:, K_SEL:K_SEL + 128], dg[:, :, :].rearrange("p t n -> p (t n)"),
                          start=True, stop=True).then_inc(mmm.sem, 1)

            def exp_scores(b, g, u):
                if u == 0:
                    pe.wait_ge(qm_out.sem, qm_out.at(b, g))
                bank = score_bank(b, ("exp", g, u))
                at = 0
                for i, n0 in score_units(g)[u]:
                    w = GT - n0 if i >= NT * g else GT
                    diag = i >= NT * g
                    q0 = 128 * (i - NT * g) if diag else 0
                    w = GT - q0
                    mm = pe.matmul(bank[:, at:at + w], kst[:, 128 * i:128 * i + 128], qm[:, q0:GT],
                                   start=True, stop=not diag)
                    if diag:
                        mm = pe.matmul(bank[:, at:at + 128], identr[:, :], maskr[:, 1, :], start=False, stop=True)
                    at += w
                mm.then_inc(smm.sem, 1)

            def values(b, g, u):
                n = eidx[("exp", g, u)]
                if u == 0:
                    pe.wait_ge(a_out.sem, a_out.at(b, g - 1) if g else a_out.before(b, GROUPS - 1))
                pe.wait_ge(e_out.sem, e_out.at(b, n))
                e = ex[:, n % ESL, :]
                if g == 0 and u == 0:
                    for q in range(1, 4):
                        pe.matmul(pvbank[QUAD * q:QUAD * q + QUAD, :], zl[:, :], e, start=True, stop=False,
                                  skip_group_check=True)
                at = 0
                for i, _ in score_units(g)[u]:
                    q0 = 128 * (i - NT * g) if i >= NT * g else 0
                    w = GT - q0
                    q = i % 4
                    mm = pe.matmul(pvbank[QUAD * q:QUAD * q + QUAD, q0:GT], vs[:, i, :], e[:, at:at + w],
                                   start=(i < 4 and not (g == 0 and i > 0)), stop=(i >= NT * g),
                                   skip_group_check=True)
                    at += w
                mm.then_inc(pv.sem, 1)

            def den(b, g):
                pe.wait_ge(a_out.sem, a_out.at(b, g))
                bank = misc_bank(b, ("den", g))
                for r in range(NT):
                    mm = pe.matmul(bank[:, r:r + 1], asb[:, 128 * r:128 * r + 128], con[:, K_DEN:K_DEN + 1],
                                   start=True, stop=True)
                mm.then_inc(mmm.sem, 1)

            def mix(b, g):
                bank = misc_bank(b, ("mh", g))
                for r in range(NT):
                    mm = pe.matmul(bank[:, 128 * r:128 * r + 128], asb[:, 128 * r:128 * r + 128], w3s[:, :],
                                   start=True, stop=True)
                mm.then_inc(mmm.sem, 1)
                turn(b, ("ct", g), c3[:, GT * g:GT * g + GT])

            def turn(b, key, x):
                bank = misc_bank(b, key)
                for r in range(NT):
                    mm = pe.transpose(bank[:, 128 * r:128 * r + 128], x[:, 128 * r:128 * r + 128], ident)
                mm.then_inc(mmm.sem, 1)

            def gram(b, g):
                pe.wait_ge(z_out.sem, z_out.at(b, g))
                bank = misc_bank(b, ("gram", g))
                for r in range(NT):
                    mm = pe.matmul(bank[:, 0:C], zr[:, r, :], zr[:, r, :], start=(r == 0), stop=(r == NT - 1))
                mm.then_inc(mmm.sem, 1)
                turn(b, ("zt", g), zr[:, :, :].rearrange("p t c -> p (t c)"))

            def lin(b, g):
                if g == 0:
                    pe.wait_ge(gram_out.sem, gram_out.at(b, GROUPS - 1))
                    pe.wait_ge(zt_out.sem, zt_out.at(b, GROUPS - 1))
                bank = misc_bank(b, ("lin", g))
                for r in range(NT):
                    t = GT * g + 128 * r
                    mm = pe.matmul(bank[:, 128 * r:128 * r + 128], zt[:, t:t + 128], G[:, :], start=True, stop=True)
                mm.then_inc(mmm.sem, 1)

            def z2turn(b, g):
                pe.wait_ge(z2_out.sem, z2_out.at(b, g))
                turn(b, ("z2t", g), zt[:, GT * g:GT * g + GT])

            def logit(b, g):
                pe.wait_ge(z2t_out.sem, z2t_out.at(b, g))
                bank = misc_bank(b, ("logit", g))
                pe.matmul(bank[0:E, :], gws[:, :], z2t[:, :], start=True, stop=True).then_inc(mmm.sem, 1)

            def turn_p(b, n):
                if n == 0:
                    pe.wait_ge(tkd.sem, tkd.at(b, 5))
                bank = misc_bank(b, ("pt", n))
                pe.sem_inc(s_held, 1)
                for t in range(8):
                    at = 128 * (8 * n + t)
                    mm = pe.transpose(bank[:, E * t:E * t + E], p[:, at:at + 128], ident[0:E, 0:E])
                mm.then_inc(mmm.sem, 1)

            def pool(b, n):
                pe.wait_ge(pt_out.sem, pt_out.at(b, n))
                bank = misc_bank(b, ("pool", n))
                for t in range(8):
                    at = 128 * (8 * n + t)
                    mm = pe.matmul(bank[:, 0:E], zt[:, at:at + 128], ptt[:, t, :], start=(t == 0), stop=(t == 7))
                mm.then_inc(mmm.sem, 1)

            stages = {"c1": c1, "c2b": lambda b, g, n: c2(b, g, n, "c2b", 1), "c2a": lambda b, g, n: c2(b, g, n, "c2a", 0)}
            astages = {"qkv": qkv, "max": max_scores, "fold": fold, "exp": exp_scores, "den": den, "mix": mix,
                       "gram": gram, "lin": lin, "z2t": z2turn, "logit": logit, "turn": turn_p, "pool": pool}

            def run(steps, b, c):
                late = []
                for st in steps:
                    k, a = st[0], st[1:]
                    if k in stages:
                        stages[k](c, *a)
                    if k in astages:
                        astages[k](b, *a)
                    if k == "exp":
                        late.append(a)
                    while len(late) > (0 if k == "copy" else 1):
                        values(b, *late.pop(0))

            run(CONV, None, 0)
            with pe.Fori(0, B - 1) as b:
                run(BOTH, b, b + 1)
            run(ATT, B - 1, None)

            pe.wait_ge(s_px, 2)
            pe.wait_ge(s_fb, 32)

            def first(i):
                if i >= 2:
                    pe.wait_ge(gelu, i - 1)
                pe.wait_ge(wa_in[i % RW], 16 * (i // RW + 1))
                for j in range(4):
                    o = ps[QUAD * j:QUAD * j + QUAD, i % 2, :]
                    pe.matmul(o, eb[:, 4 * i + j, :], fb1[:, :], start=True, stop=False, skip_group_check=True)
                for j in range(4):
                    o = ps[QUAD * j:QUAD * j + QUAD, i % 2, :]
                    mm = pe.matmul(o, px[:, 4 * i + j, :], wa[:, i % RW, j, :], start=False, stop=True,
                                   skip_group_check=True)
                mm.then_inc(ffn1, 1)

            def second(i):
                pe.wait_ge(gelu, i + 1)
                if i >= 2:
                    pe.wait_ge(htc, i - 1)
                for c in range(4):
                    mm = pe.transpose(ps[:, 2 + i % 2, 128 * c:128 * c + 128], hs[:, i % 2, 128 * c:128 * c + 128], ident)
                mm.then_inc(htr, 1)
                pe.wait_ge(htc, i + 1)
                pe.wait_ge(wb_in[i % RW], 16 * (i // RW + 1))
                if i >= 2:
                    pe.wait_ge(o_out, i - 1)
                for j in range(4):
                    o = ps[QUAD * j:QUAD * j + QUAD, 4 + i % 2, 0:C]
                    pe.matmul(o, eb[:, 4 * i + j, :], fb2[:, :], start=True, stop=False, skip_group_check=True)
                for c in range(4):
                    for j in range(4):
                        o = ps[QUAD * j:QUAD * j + QUAD, 4 + i % 2, 0:C]
                        mm = pe.matmul(o, ht[:, i % 2, c, QUAD * j:QUAD * j + QUAD], wb[:, i % RW, j, c, :],
                                       start=False, stop=(c == 3), skip_group_check=True)
                mm.then_inc(ffn2, 1)

            for i in range(E // 4):
                first(i)
                if i:
                    second(i - 1)
            second(E // 4 - 1)
            pe.wait_ge(oo_in, 32)
            pe.wait_ge(p_in, 16 * B)
            for n in range(B * GROUPS):
                b, g = divmod(n, GROUPS)
                if n >= 2:
                    pe.wait_ge(sum_out, n - 1)
                h = E * (b % 2)
                for r in range(NT):
                    t = GT * g + 128 * r
                    mm = pe.matmul(ps[:, 6 + n % 2, 128 * r:128 * r + 128], pp[h:h + E, b // 2, t:t + 128],
                                   oo[h:h + E, b, :], start=True, stop=True)
                mm.then_inc(fin, 1)

        @block.scalar
        def _(act):
            act.wait_ge(s_w, N_W)
            act.wait_ge(s_con, 16)
            act.activation(w1s[:, 0, :, :].rearrange("p t c -> p (t c)"), c3[:, 0:9 * C], ACT.Copy)
            act.activation(w2s[:, 0, :, :].rearrange("p t c -> p (t c)"),
                           T[:, 0:18, :].rearrange("p t c -> p (t c)"), ACT.Copy)
            act.activation(identr[:, :], ident, ACT.Copy)
            act.activation(maskr[:, :, :].rearrange("p a n -> p (a n)"), zr[:, 0:2, :].rearrange("p a n -> p (a n)"),
                           ACT.Copy).then_inc(s_seta, 1)
            act.wait_ge(s_set, 1)

            def exp_x(b, g):
                lo, hi, r = x_rows(g)
                rows = slice(r, r + hi - lo)
                act.wait_ge(x_in[g % 2].sem, x_in[g % 2].at(b, g // 2))
                act.wait_ge(x_low.sem, x_low.at(b, g - 1) if g else x_low.before(b, GROUPS - 1))
                act.activation(el[:, rows, :], xi[:, g % 2, rows, :], ACT.Exp).then_inc(elu_exp.sem, 1)

            def high_x(b, g):
                lo, hi, r = x_rows(g)
                rows = slice(r, r + hi - lo)
                act.wait_ge(elu_out.sem, elu_out.at(b, g))
                k = cmm_index[("c1", (g - 2) % GROUPS)]
                act.wait_ge(cmm.sem, cmm.at(b, k) if g >= 2 else cmm.before(b, k))
                act.activation(xp[:, g % 2, 0, rows, 1:1 + IW], el[:, rows, :], ACT.Copy).then_inc(x_high.sem, 1)

            def high_c(b, g):
                act.wait_ge(cmm.sem, cmm.at(b, cmm_index[("c1", g)]))
                act.activation(cp[:, 0, GR * g:GR * g + GR, 1:1 + IW],
                               conv_bank(("c1", g)).rearrange("p (r w) -> p r w", w=IW),
                               ACT.Identity, bias=cols[:, 0:1]).then_inc(c_high.sem, 1)

            def tanh(b, g):
                act.wait_ge(cmm.sem, cmm.at(b, cmm_index[("c2b", g)]))
                act.wait_ge(c3_out.sem, c3_out.at(b, g - 1) if g else c3_out.before(b, GROUPS - 1))
                act.activation(sg[:, :], conv_bank(("c2b", g)), ACT.Tanh, scale=0.5,
                               bias=hb[:, 0:1]).then_inc(gate_tanh.sem, 1)

            def qkv(b, g):
                act.wait_ge(mmm.sem, mmm.at(b, midx[("q", g)]))
                act.wait_ge(qm_out.sem, qm_out.at(b, g - 2) if g >= 2 else qm_out.before(b, g + 6))
                act.activation(qv[:, g % 2, :], misc(("q", g)), ACT.Identity, scale=0.25,
                               bias=hb[:, 1:2]).then_inc(q_val.sem, 1)
                act.wait_ge(q_st.sem, q_st.at(b, g - 1) if g else q_st.before(b, GROUPS - 1))
                act.activation(qh[:, :], misc(("q", g)), ACT.Identity, scale=0.25,
                               bias=hb[:, 1:2]).then_inc(q_high.sem, 1)
                act.wait_ge(mmm.sem, mmm.at(b, midx[("k", g)]))
                act.wait_ge(k_st.sem, k_st.at(b, g - 1) if g else k_st.before(b, GROUPS - 1))
                act.activation(kv[:, :], misc(("k", g)), ACT.Identity, bias=cols[:, 4:5]).then_inc(k_val.sem, 1)
                act.activation(kh[:, :], misc(("k", g)), ACT.Identity, bias=cols[:, 4:5]).then_inc(k_high.sem, 1)

            def foldhigh(b, g):
                act.wait_ge(fold_sum.sem, fold_sum.at(b, g))
                act.wait_ge(qm_out.sem, qm_out.at(b, g - 1) if g else qm_out.before(b, GROUPS - 1))
                act.activation(fh[:, :], qv[:, g % 2, :], ACT.Copy).then_inc(fold_high.sem, 1)

            def exponentials(b, g, u):
                n = eidx[("exp", g, u)]
                w = sum(GT - max(0, 128 * (i - NT * g)) for i, _ in score_units(g)[u])
                act.wait_ge(smm.sem, smm.at(b, sidx[("exp", g, u)]))
                m = n - ESL if n >= ESL else [m for m in range(NE) if m % ESL == n % ESL][-1]
                act.wait_ge(pv.sem, pv.at(b, m) if n >= ESL else pv.before(b, m))
                act.activation(ex[:, n % ESL, 0:w], sbank[sidx[("exp", g, u)] % SLOTS][:, 0:w],
                               ACT.Exp).then_inc(e_out.sem, 1)

            def copy(b, g):
                act.wait_ge(pv.sem, pv.at(b, eidx[("exp", g, len(score_units(g)) - 1)]))
                k = midx[("mh", (g - 1) % GROUPS)]
                act.wait_ge(mmm.sem, mmm.at(b, k) if g else mmm.before(b, k))
                act.activation(asb[:, :], pvbank, ACT.Copy).then_inc(a_out.sem, 1)

            def turned(b, g):
                act.wait_ge(mmm.sem, mmm.at(b, midx[("zt", g)]))
                act.activation(zt[:, GT * g:GT * g + GT], misc(("zt", g)), ACT.Copy).then_inc(zt_out.sem, 1)

            def z2turned(b, g):
                act.wait_ge(mmm.sem, mmm.at(b, midx[("z2t", g)]))
                k = ("logit", g - 1) if g else ("pool", 3)
                if g and midx[k] > midx[("z2t", g)]:
                    act.wait_ge(mmm.sem, mmm.at(b, midx[k]))
                act.activation(z2t[:, :], misc(("z2t", g)), ACT.Copy).then_inc(z2t_out.sem, 1)

            def logit(b, g):
                act.wait_ge(mmm.sem, mmm.at(b, midx[("logit", g)]))
                act.wait_ge(p_store.sem, p_store.before(b, 0))
                act.activation(p[:, GT * g:GT * g + GT], misc(("logit", g))[0:E, :], ACT.Identity,
                               bias=cols[0:E, 5:6]).then_inc(logit_out.sem, 1)

            def topk(b, n):
                if n:
                    return
                act.wait_ge(tkd.sem, tkd.at(b, 0))
                act.activation(p[:, :], p[:, :], ACT.Exp, bias=tk[:, 0:1], accum_out=tk[:, 1:2]).then_inc(tke.sem, 1)

            def pool(b, n):
                act.wait_ge(mmm.sem, mmm.at(b, midx[("pt", n)]))
                k = ("pool", n - 1) if n else ("logit", GROUPS - 1)
                if midx[k] > midx[("pt", n)]:
                    act.wait_ge(mmm.sem, mmm.at(b, midx[k]))
                act.activation(ptt[:, :, :].rearrange("p t e -> p (t e)"), misc(("pt", n)),
                               ACT.Copy).then_inc(pt_out.sem, 1)

            stages = {"exp_x": exp_x, "high_x": high_x, "high_c": high_c, "tanh": tanh}
            astages = {"qkv": qkv, "foldhigh": foldhigh, "exp": exponentials, "copy": copy, "gram": turned,
                       "z2t": z2turned, "logit": logit, "topk": topk, "turn": pool}

            def run(steps, b, c):
                for st in steps:
                    if st[0] in stages:
                        stages[st[0]](c, *st[1:])
                    if st[0] in astages:
                        astages[st[0]](b, *st[1:])

            run(CONV, None, 0)
            with act.Fori(0, B - 1) as b:
                run(BOTH, b, b + 1)
            run(ATT, B - 1, None)
            for i in range(E // 4):
                act.wait_ge(ffn1, i + 1)
                if i >= 2:
                    act.wait_ge(htr, i - 1)
                act.activation(hs[:, i % 2, :], ps[:, i % 2, :], ACT.Gelu).then_inc(gelu, 1)

        @block.vector
        def _(dve):
            dve.wait_ge(s_con, 16)
            dve.memset(cols[:, :], 0.0).then_inc(s_dset, 1)
            dve.wait_ge(s_dset, 1)
            dve.tensor_copy(cols[:, 4:5], con[:, K_ONE:K_ONE + 1]).then_inc(s_dset, 1)
            dve.memset(wqs[:, :, :], 0.0)
            dve.memset(wvs[:, :], 0.0)
            dve.memset(bvs[:, :], 0.0).then_inc(s_dset, 1)
            dve.memset(zl[:, :], 0.0)
            dve.memset(zt[:, 0:HEADS * C], 0.0)
            dve.wait_ge(s_dset, 3)
            dve.memset(bvs[:, DV:DV + 1], 1.0).then_inc(s_zero, 1)
            dve.wait_ge(s_seta, 1)
            dve.tensor_tensor(w1s[:, 1, :, :].rearrange("p t c -> p (t c)"), c3[:, 0:9 * C],
                              w1s[:, 0, :, :].rearrange("p t c -> p (t c)").bitcast(F32), ALU.subtract)
            dve.tensor_tensor(w2s[:, 1, :, :].rearrange("p t c -> p (t c)"),
                              T[:, 0:18, :].rearrange("p t c -> p (t c)"),
                              w2s[:, 0, :, :].rearrange("p t c -> p (t c)").bitcast(F32), ALU.subtract)
            dve.wait_ge(s_b, N_B)
            dve.tensor_reduce(w3s[:, :], zt[:, 0:HEADS * C].rearrange("p (h c) -> p c h", h=HEADS), AX.X, ALU.add)
            dve.tensor_scalar(hb[:, 0:1], cols[:, 2:3], 0.5, None, ALU.mult)
            dve.tensor_scalar(hb[:, 1:2], cols[:, 3:4], 0.25, None, ALU.mult).then_inc(s_set, 1)
            dve.wait_ge(s_set, 1)

            def elu(b, g):
                lo, hi, r = x_rows(g)
                rows = slice(r, r + hi - lo)
                dve.wait_ge(elu_min.sem, elu_min.at(b, g))
                dve.scalar_tensor_tensor(out=el[:, rows, :], in0=xi[:, g % 2, rows, :], scalar=0.0,
                                         in1=el[:, rows, :], op0=ALU.max, op1=ALU.add).then_inc(elu_out.sem, 1)

            def low_x(b, g):
                lo, hi, r = x_rows(g)
                rows = slice(r, r + hi - lo)
                dve.wait_ge(x_high.sem, x_high.at(b, g))
                dve.tensor_tensor(xp[:, g % 2, 1, rows, 1:1 + IW], el[:, rows, :],
                                  xp[:, g % 2, 0, rows, 1:1 + IW].bitcast(F32), ALU.subtract).then_inc(x_low.sem, 1)

            def low_c(b, g):
                dve.wait_ge(c_high.sem, c_high.at(b, g))
                here = slice(GR * g, GR * g + GR)
                dve.scalar_tensor_tensor(out=cp[:, 1, here, 1:1 + IW],
                                         in0=conv_bank(("c1", g)).rearrange("p (r w) -> p r w", w=IW),
                                         scalar=cols[:, 0:1],
                                         in1=cp[:, 0, here, 1:1 + IW].bitcast(F32), op0=ALU.add,
                                         op1=ALU.subtract).then_inc(c_low.sem, 1)

            def gate(b, g):
                dve.wait_ge(gate_half.sem, gate_half.at(b, g))
                dve.wait_ge(cmm.sem, cmm.at(b, cmm_index[("c2a", g)]))
                dve.wait_ge(mmm.sem, mmm.before(b, midx[("ct", g)]))
                dve.scalar_tensor_tensor(out=c3[:, GT * g:GT * g + GT], in0=conv_bank(("c2a", g)), scalar=cols[:, 1:2],
                                         in1=sg[:, :], op0=ALU.add, op1=ALU.mult).then_inc(c3_out.sem, 1)

            def stack(b, g):
                dve.wait_ge(q_high.sem, q_high.at(b, g))
                k = sidx[("max", (g - 2) % GROUPS, NT - 1, (g - 2) % GROUPS)]
                dve.wait_ge(smm.sem, smm.at(b, k) if g >= 2 else smm.before(b, k))
                dve.scalar_tensor_tensor(out=qst[:, g % 2, :], in0=qh[:, :].bitcast(F32), scalar=con[:, K_NQ:K_NQ + 1],
                                         in1=qv[:, g % 2, :], op0=ALU.mult, op1=ALU.add).then_inc(q_st.sem, 1)
                dve.wait_ge(k_high.sem, k_high.at(b, g))
                dve.wait_ge(smm.sem, smm.before(b, NS - 1))
                dve.scalar_tensor_tensor(out=kst[:, GT * g:GT * g + GT], in0=kh[:, :].bitcast(F32),
                                         scalar=con[:, K_NK:K_NK + 1], in1=kv[:, :], op0=ALU.mult,
                                         op1=ALU.add).then_inc(k_st.sem, 1)
                dve.wait_ge(mmm.sem, mmm.at(b, midx[("v", g)]))
                dve.wait_ge(pv.sem, pv.before(b, NE - 1))
                bank = misc(("v", g))
                dve.tensor_tensor(vs[:, NT * g:NT * g + NT, :],
                                  bank[:, 0:NT * QUAD].rearrange("p (t d) -> p t d", d=QUAD),
                                  bvs[:, :].unsqueeze(1).broadcast_to([128, NT, QUAD]),
                                  ALU.add).then_inc(v_out.sem, 1)

            def maxima(b, g, r, c):
                st = ("max", g, r, c)
                dve.wait_ge(smm.sem, smm.at(b, sidx[st]))
                if r == 0 and c == 0:
                    dve.wait_ge(nm_out.sem, nm_out.at(b, g - 1) if g else nm_out.before(b, GROUPS - 1))
                w = GT if c < g else 128 * (r + 1)
                dve.tensor_reduce(mpart[:, r, c:c + 1], sbank[sidx[st] % SLOTS][:, 0:w], AX.X,
                                  ALU.max).then_inc(smax.sem, 1)

            def negmax(b, g):
                dve.wait_ge(smax.sem, smax.at(b, xidx[("max", g, NT - 1, g)]))
                dve.wait_ge(dg_out.sem, dg_out.at(b, g - 1) if g else dg_out.before(b, GROUPS - 1))
                dve.tensor_reduce(nm[:, :], mpart[:, :, 0:g + 1], AX.X, ALU.max, negate=True).then_inc(nm_out.sem, 1)
                dve.wait_ge(nm_out.sem, nm_out.at(b, g))
                k = midx[("fold", (g - 1) % GROUPS)]
                dve.wait_ge(mmm.sem, mmm.at(b, k) if g else mmm.before(b, k))
                for r in range(NT):
                    ins = dve.tensor_scalar(dg[:, r, :], ident, nm[:, r:r + 1], None, ALU.mult)
                ins.then_inc(dg_out.sem, 1)

            def fold(b, g):
                dve.wait_ge(mmm.sem, mmm.at(b, midx[("fold", g)]))
                dve.tensor_tensor(qv[:, g % 2, :], misc(("fold", g)), qv[:, g % 2, :], ALU.add).then_inc(fold_sum.sem, 1)

            def foldq(b, g):
                dve.wait_ge(fold_high.sem, fold_high.at(b, g))
                h = (g - 1) % GROUPS
                k = sidx[("exp", h, len(score_units(h)) - 1)]
                dve.wait_ge(smm.sem, smm.at(b, k) if g else smm.before(b, k))
                dve.scalar_tensor_tensor(out=qm[:, :], in0=fh[:, :].bitcast(F32), scalar=con[:, K_NQ:K_NQ + 1],
                                         in1=qv[:, g % 2, :], op0=ALU.mult, op1=ALU.add).then_inc(qm_out.sem, 1)

            def den(b, g):
                dve.wait_ge(mmm.sem, mmm.at(b, midx[("den", g)]))
                dve.wait_ge(t_scaled.sem, t_scaled.at(b, g - 1) if g else t_scaled.before(b, GROUPS - 1))
                dve.tensor_scalar(rd[:, 0, :], misc(("den", g))[:, 0:NT], TINY, None, ALU.add).then_inc(den_sum.sem, 1)
                dve.wait_ge(den_sum.sem, den_sum.at(b, g))
                dve.reciprocal(rd[:, 1, :], rd[:, 0, :]).then_inc(rd_out.sem, 1)

            def mix(b, g):
                dve.wait_ge(rd_out.sem, rd_out.at(b, g))
                dve.wait_ge(xb_out.sem, xb_out.at(b, g))
                dve.wait_ge(mmm.sem, mmm.at(b, midx[("mh", g)]))
                dve.wait_ge(t1_store.sem, t1_store.before(b, g))
                dve.wait_ge(tkd.sem, tkd.before(b, 5))
                for r in range(NT):
                    ins = dve.scalar_tensor_tensor(out=T[:, NT * g + r, :], in0=misc(("mh", g))[:, C * r:C * r + C],
                                                   scalar=rd[:, 1, r:r + 1], in1=xn[:, g % 2, r, :],
                                                   op0=ALU.mult, op1=ALU.add)
                ins.then_inc(t_scaled.sem, 1)
                dve.wait_ge(t_scaled.sem, t_scaled.at(b, g))
                dve.wait_ge(mmm.sem, mmm.at(b, midx[("ct", g)]))
                tg = T[:, NT * g:NT * g + NT, :].rearrange("p t c -> p (t c)")
                dve.tensor_tensor(tg, misc(("ct", g)), tg, ALU.add).then_inc(t_out.sem, 1)

            def statistics(b, g, st, mean):
                for r in range(NT):
                    ins = dve.bn_stats(stat[:, r, :], T[:, NT * g + r, :])
                ins.then_inc(st.sem, 1)
                dve.wait_ge(st.sem, st.at(b, g))
                dve.sem_inc(s_held, 1)
                for r in range(NT):
                    ins = dve.bn_aggr(mv[:, g % 2, r, :], stat[:, r, :])
                ins.then_inc(mean.sem, 1)

            def normalised(g, out_tiles, out_sig):
                for r in range(NT):
                    ins = dve.tensor_scalar(out_tiles[r], T[:, NT * g + r, :], mv[:, g % 2, r, 0:1],
                                            rs[:, 1, g % 2, r:r + 1], ALU.subtract, ALU.mult)
                ins.then_inc(out_sig.sem, 1)

            def stats(b, g):
                dve.wait_ge(t_out.sem, t_out.at(b, g))
                dve.wait_ge(mv1.sem, mv1.at(b, g - 1) if g else mv1.before(b, GROUPS - 1))
                s_, k = (z_out, g - 2) if g >= 2 else (z2_out, g + 6)
                dve.wait_ge(s_.sem, s_.at(b, k) if g >= 2 else s_.before(b, k))
                dve.wait_ge(mv2.sem, mv2.before(b, GROUPS - 1))
                statistics(b, g, st1, mv1)

            def z(b, g):
                dve.wait_ge(rs1.sem, rs1.at(b, g))
                k = midx[("zt", (g - 1) % GROUPS)]
                dve.wait_ge(mmm.sem, mmm.at(b, k) if g else mmm.before(b, k))
                normalised(g, [zr[:, r, :] for r in range(NT)], z_out)

            def gram(b, g):
                dve.wait_ge(mmm.sem, mmm.at(b, midx[("gram", g)]))
                if g == 0:
                    dve.tensor_copy(G[:, :], misc(("gram", g))[:, 0:C]).then_inc(gram_out.sem, 1)
                else:
                    dve.wait_ge(gram_out.sem, gram_out.at(b, g - 1))
                    dve.tensor_tensor(G[:, :], misc(("gram", g))[:, 0:C], G[:, :], ALU.add).then_inc(gram_out.sem, 1)

            def lin(b, g):
                dve.wait_ge(mmm.sem, mmm.at(b, midx[("lin", g)]))
                tg = T[:, NT * g:NT * g + NT, :].rearrange("p t c -> p (t c)")
                dve.tensor_tensor(tg, misc(("lin", g)), tg, ALU.add).then_inc(t1_out.sem, 1)
                dve.wait_ge(t1_out.sem, t1_out.at(b, g))
                s_, k = (z2_out, g - 2) if g >= 2 else (z_out, g + 6)
                dve.wait_ge(s_.sem, s_.at(b, k))
                s_, k = (mv2, g - 1) if g else (mv1, GROUPS - 1)
                dve.wait_ge(s_.sem, s_.at(b, k))
                statistics(b, g, st2, mv2)

            def z2(b, g):
                dve.wait_ge(rs2.sem, rs2.at(b, g))
                normalised(g, [zt[:, GT * g + 128 * r:GT * g + 128 * r + 128] for r in range(NT)], z2_out)

            def topk(b, n):
                rest = T[0:E, :, :].rearrange("p t c -> p (t c)")
                if n == 0:
                    dve.wait_ge(logit_out.sem, logit_out.at(b, GROUPS - 1))
                    ins = dve.tensor_reduce(tk[:, 0:1], p[:, :], AX.X, ALU.max, negate=True)
                else:
                    dve.wait_ge(tkd.sem, tkd.at(b, n - 1))
                if n == 1:
                    dve.wait_ge(tke.sem, tke.at(b, 0))
                    ins = dve.reciprocal(tk[:, 2:3], tk[:, 1:2])
                if n == 2:
                    ins = dve.tensor_scalar(p[:, :], p[:, :], tk[:, 2:3], None, ALU.mult)
                if n == 3:
                    dve.sem_inc(s_held, 1)
                    ins = dve.max(tk[:, 4:12], p[:, :])
                if n == 4:
                    dve.wait_ge(t1_store.sem, t1_store.at(b, GROUPS - 1))
                    dve.sem_inc(s_held, 1)
                    ins = dve.match_replace(rest, tk[:, 4:12], p[:, :], 0.0)
                if n == 5:
                    ins = dve.tensor_tensor(p[:, :], p[:, :], rest, ALU.subtract)
                ins.then_inc(tkd.sem, 1)

            def pool(b, n):
                dve.wait_ge(mmm.sem, mmm.at(b, midx[("pool", n)]))
                bank = misc(("pool", n))[:, 0:E]
                dve.wait_ge(pool_out.sem, pool_out.at(b, n - 1) if n else pool_out.before(b, 3))
                if n == 0:
                    dve.tensor_copy(pacc[:, :], bank).then_inc(pool_out.sem, 1)
                elif n < 3:
                    dve.tensor_tensor(pacc[:, :], bank, pacc[:, :], ALU.add).then_inc(pool_out.sem, 1)
                else:
                    dve.tensor_tensor(pooled[:, b, :], bank, pacc[:, :], ALU.add).then_inc(pool_out.sem, 1)

            stages = {"elu": elu, "low_x": low_x, "low_c": low_c, "gate": gate}
            astages = {"stack": stack, "max": maxima, "negmax": negmax, "fold": fold, "foldq": foldq, "den": den,
                       "mix": mix, "stats": stats, "z": z, "gram": gram, "lin": lin, "z2": z2, "topk": topk,
                       "pool": pool}

            def run(steps, b, c):
                for st in steps:
                    if st[0] in stages:
                        stages[st[0]](c, *st[1:])
                    if st[0] in astages:
                        astages[st[0]](b, *st[1:])

            run(CONV, None, 0)
            with dve.Fori(0, B - 1) as b:
                run(BOTH, b, b + 1)
            run(ATT, B - 1, None)

            last = B - 1
            dve.wait_ge(pool_out.sem, pool_out.at(last, 3))
            dve.wait_ge(t1_store.sem, t1_store.at(last, GROUPS - 1))
            dve.wait_ge(p_store.sem, p_store.at(last, 0))
            dve.memset(px[:, :, :], 0.0).then_inc(s_dset, 1)
            dve.wait_ge(s_dset, 4)
            dve.tensor_copy(px[:, :, 0:B], pooled[:, :, :].rearrange("p b e -> p e b")).then_inc(s_px, 1)
            dve.tensor_copy(eb[:, :, :], con[0:E, K_ID:K_ID + E].unsqueeze(2).broadcast_to([E, E, QUAD])).then_inc(s_px, 1)
            for i in range(E // 4):
                dve.wait_ge(htr, i + 1)
                if i >= 2:
                    dve.wait_ge(ffn2, i - 1)
                dve.tensor_copy(ht[:, i % 2, :, :].rearrange("p c n -> p (c n)"), ps[:, 2 + i % 2, :]).then_inc(htc, 1)
                if i:
                    dve.wait_ge(ffn2, i)
                    dve.tensor_copy(oall[:, i - 1, :], ps[:, 4 + (i - 1) % 2, 0:C]).then_inc(o_out, 1)
            dve.wait_ge(ffn2, E // 4)
            dve.tensor_copy(oall[:, E // 4 - 1, :], ps[:, 4 + (E // 4 - 1) % 2, 0:C]).then_inc(o_out, 1)
            for n in range(B * GROUPS):
                dve.wait_ge(fin, n + 1)
                dve.wait_ge(tl_in[n % LT], 16 * (n // LT + 1))
                t = tl[:, n % LT, :, :].rearrange("p t c -> p (t c)")
                dve.tensor_tensor(t, ps[:, 6 + n % 2, :], t, ALU.add).then_inc(sum_out, 1)

        @block.gpsimd
        def _(pool_e):
            for s_ in range(2):
                for h in range(2):
                    for col in (0, PW - 1):
                        pool_e.memset(xp[:, s_, h, :, col:col + 1].bitcast(F32), 0.0)
            for col in (0, PW - 1):
                ins = pool_e.memset(cp[:, :, :, col:col + 1].bitcast(F32), 0.0)
            ins.then_inc(s_setp, 1)
            pool_e.wait_ge(s_w, N_W)
            pool_e.wait_ge(s_con, 16)

            def elu(b, g):
                lo, hi, r = x_rows(g)
                rows = slice(r, r + hi - lo)
                pool_e.wait_ge(elu_exp.sem, elu_exp.at(b, g))
                pool_e.sem_inc(s_held, 1)
                pool_e.tensor_scalar(el[:, rows, :], el[:, rows, :], 1.0, -1.0, ALU.min, ALU.add).then_inc(elu_min.sem, 1)

            def c2(b, g):
                pool_e.wait_ge(gate_tanh.sem, gate_tanh.at(b, g))
                pool_e.sem_inc(s_held, 1)
                pool_e.tensor_scalar(sg[:, :], sg[:, :], 0.5, 0.5, ALU.mult, ALU.add).then_inc(gate_half.sem, 1)

            def bias(b, g):
                pool_e.wait_ge(xn_in[g % 2].sem, xn_in[g % 2].at(b, g // 2))
                pool_e.tensor_tensor(xn[:, g % 2, :, :], xn[:, g % 2, :, :],
                                     b3s[:, :].unsqueeze(1).broadcast_to([128, NT, C]), ALU.add).then_inc(xb_out.sem, 1)

            def rstd(b, g, mean, ve, out_sig, reader, count):
                h = g % 2
                pool_e.wait_ge(mean.sem, mean.at(b, g))
                pool_e.wait_ge(reader.sem, count)
                pool_e.sem_inc(s_held, 1)
                pool_e.tensor_scalar(rs[:, 0, h, :], mv[:, h, :, 1:2].rearrange("p t a -> p (t a)"), EPS, None,
                                     ALU.add).then_inc(ve.sem, 1)
                pool_e.wait_ge(ve.sem, ve.at(b, g))
                pool_e.tensor_tensor(rs[:, 1, h, :], rs[:, 0, h, :], con[:, K_POW:K_POW + NT],
                                     ALU.pow).then_inc(out_sig.sem, 1)

            def stats(b, g):
                s_, k = (z_out, g - 2) if g >= 2 else (z2_out, g + 6)
                rstd(b, g, mv1, ve1, rs1, s_, s_.at(b, k) if g >= 2 else s_.before(b, k))

            def lin(b, g):
                s_, k = (z2_out, g - 2) if g >= 2 else (z_out, g + 6)
                rstd(b, g, mv2, ve2, rs2, s_, s_.at(b, k))

            stages = {"exp_x": elu, "tanh": c2}
            astages = {"foldq": bias, "stats": stats, "lin": lin}

            def run(steps, b, c):
                for st in steps:
                    if st[0] in stages:
                        stages[st[0]](c, *st[1:])
                    if st[0] in astages:
                        astages[st[0]](b, *st[1:])

            run(CONV, None, 0)
            with pool_e.Fori(0, B - 1) as b:
                run(BOTH, b, b + 1)
            run(ATT, B - 1, None)


def kernel(x, L0_conv_W1, L0_conv_b1, L0_conv_W2, L0_conv_b2, L0_conv_Wq, L0_conv_bq, L0_conv_Wk, L0_conv_bk,
           L0_conv_Wv, L0_conv_bv, L0_conv_W3, L0_conv_b3, L1_ffn_gate_w, L1_ffn_gate_b, L1_ffn_weight1,
           L1_ffn_weight2):
    import numpy as np
    import concourse.bacc as bacc
    from concourse.bass_utils import run_bass_kernel_spmd

    con = np.zeros((128, K_END), np.float32)
    i = np.arange(128)
    con[:, K_ID:K_ID + 128] = np.eye(128)
    masks = np.zeros((128, 2, 128), np.float32)
    masks[:, 0] = np.where(i[None, :] >= i[:, None], -1e10, 0.0)
    masks[:, 1] = np.where(i[:, None] >= i[None, :], -1e30, 0.0)
    con[:, K_SEL + DK] = con[:, K_SEL + QUAD + DK] = 1.0
    con[DV::QUAD, K_DEN] = 1.0
    con[:, K_NQ] = np.where(i // QUAD % 2 == 1, -1.0, 0.0)
    con[:, K_NK] = np.where(i // QUAD >= 2, -1.0, 0.0)
    con[[DK, QUAD + DK], K_ONE] = 1.0
    con[:, K_POW:K_POW + NT] = -0.5

    a = {
        "x_cm": x.reshape(B, TOK, C).transpose(0, 2, 1),
        "x_nat": x.reshape(B, GROUPS, NT, 128, C).transpose(0, 1, 3, 2, 4),
        "w1": L0_conv_W1.reshape(9, C, C).transpose(1, 0, 2),
        "b1": L0_conv_b1.reshape(C, 1),
        "w2": L0_conv_W2.reshape(9, C, 2 * C).transpose(1, 0, 2),
        "b2": L0_conv_b2.reshape(2, C).T,
        "wq": L0_conv_Wq, "bq": L0_conv_bq.reshape(DK, 1),
        "wk": L0_conv_Wk, "bk": L0_conv_bk.reshape(DK, 1),
        "wv": L0_conv_Wv, "bv": L0_conv_bv,
        "w3": L0_conv_W3.reshape(HEADS, DV, C).transpose(1, 0, 2).reshape(DV, HEADS * C),
        "b3": L0_conv_b3,
        "gate_wt": L1_ffn_gate_w.T,
        "gate_b": L1_ffn_gate_b.reshape(E, 1),
        "f1": L1_ffn_weight1[:, :C, :].transpose(1, 0, 2),
        "f1b": L1_ffn_weight1[:, C, :],
        "f2": L1_ffn_weight2[:, :HID, :].reshape(E, 4, 128, C).transpose(2, 0, 1, 3),
        "f2b": L1_ffn_weight2[:, HID, :],
        "consts": con,
        "masks": masks,
    }
    nc = bacc.Bacc("TRN2", target_bir_lowering=False, num_devices=1)
    arrays, aps = {}, {}
    for name, v in a.items():
        v = np.ascontiguousarray(v)
        arrays["in_" + name] = v
        aps[name] = nc.dram_tensor("in_" + name, v.shape, mybir.dt.from_np(v.dtype), kind="ExternalInput").ap()
    aps["out"] = nc.dram_tensor("out_tokens", (B, GROUPS, 128, NT, C), F32, kind="ExternalOutput").ap()
    aps["t1_dram"] = nc.dram_tensor("t1_scratch", (B, GROUPS, 128, NT, C), F32).ap()
    aps["p_dram"] = nc.dram_tensor("p_scratch", (B, E, TOK), F32).ap()
    aps["o_dram"] = nc.dram_tensor("o_scratch", (B, E, C), F32).ap()
    program(nc, **aps)
    r = run_bass_kernel_spmd(nc, [arrays], core_ids=[0])
    o = r.results[0]["out_tokens"]
    return o.transpose(0, 1, 3, 2, 4).reshape(B, IH, IW, C)
```

```python
from contextlib import ExitStack

import concourse.bass as bass
from concourse import mybir

F32 = mybir.dt.float32
F32R = mybir.dt.float32r
ALU = mybir.AluOpType
ACT = mybir.ActivationFunctionType
AX = mybir.AxisListType

B, IH, IW, C = 4, 64, 64, 128
TOK = IH * IW
GROUPS = 8
TAPS = 9
HEAD = 110
GT = TOK // GROUPS
GR = IH // GROUPS
NT = GT // 128
PW = IW + 2
DK, DV, HEADS = 4, 16, 8
VW = DV + 1
VROW = 8
E, HID = 64, 512
SLOTS = 3
ESL = 3
QUAD = 32
TINY = 1e-10
GONE = -3e38
EPS = 1e-5
TKS = 5
POOLS = 8
PT = TOK // 128 // POOLS
WARM = 18
AHEAD = 9
LAG = 2
K_ID, K_NQ, K_NK, K_ONE, K_DEN, K_POW, K_END = 0, 128, 129, 130, 131, 132, 136


class Signal:

    def __init__(self, sem, per, unit=1):
        self.sem, self.per, self.unit = sem, per, unit

    def at(self, b, k):
        return (b * self.per + (self.per + k + 1)) * self.unit

    def before(self, b, k):
        return (b * self.per + (k + 1)) * self.unit


def score_units(g):
    whole = [[(i, 0)] for i in range(NT * g)]
    d = NT * g
    return whole + [[(d, 0)], [(d + 1, 128), (d + 3, 384)], [(d + 2, 256)]]


def attention_steps():
    out = [("qkv", 0), ("stack", 0), ("v", 0), ("qkv", 1), ("stack", 1), ("v", 1)]
    out += [("max", 0, r, 0) for r in range(NT)]
    out += [("negmax", 0), ("fold", 0), ("foldhigh", 0)]
    out += [("foldq", 0)]
    for g in range(GROUPS):
        exps = [("exp", g, u) for u in range(len(score_units(g)))]
        maxs, side = [], []
        if g + 1 < GROUPS:
            maxs = [("max", g + 1, r, c) for c in range(g + 2) for r in range(NT)]
        if g:
            side += [("mix", g - 1), ("ct", g - 1)]
        if g + 2 < GROUPS:
            side += [("qkv", g + 2), ("stack", g + 2), ("v", g + 2)]
        if g > 1:
            side += [("gram", g - 2)]
        if g:
            side += [("stats", g - 1), ("z", g - 1)]
        early = max(1, len(exps) * 3 // 4)
        body = [[] for _ in exps]
        for n, m in enumerate(maxs):
            body[min(n * early // len(maxs), len(exps) - 1)].append(m)
        for n, m in enumerate(side):
            body[n * len(exps) // len(side)].append(m)
        if maxs:
            body[min(early, len(exps) - 1)].append(("negmax", g + 1))
            body[min(early + 1, len(exps) - 1)].append(("fold", g + 1))
            body[min(early + 2, len(exps) - 1)].append(("foldhigh", g + 1))
            body[min(early + 3, len(exps) - 1)].append(("foldq", g + 1))
        for e, more in zip(exps, body):
            out += [e] + more
        out += [("copy", g)]
    g = GROUPS - 1
    out += [("mix", g), ("gram", g - 1), ("ct", g), ("stats", g), ("z", g), ("gram", g)]
    for g in range(GROUPS + 4):
        if g < GROUPS:
            out += [("lin", g)]
        if 0 <= g - 1 < GROUPS:
            out += [("z2", g - 1)]
        if 0 <= g - 2 < GROUPS:
            out += [("z2t", g - 2)]
        if 0 <= g - 3 < GROUPS:
            out += [("logit", g - 3)]
        if 0 <= g - 4 < GROUPS:
            out += [("top", g - 4)]
    out += [("topk", n) for n in range(6)]
    for n in range(POOLS + 1):
        if n < POOLS:
            out += [("turn", n)]
        if n:
            out += [("pool", n - 1)]
    out += [("poolt", 0)]
    return out


def conv_steps():
    runs = []
    for g in range(-2, GROUPS):
        if g + 2 < GROUPS:
            runs += [("c1", g + 2, n) for n in range(TAPS)]
        if g >= 0:
            runs += [("c2b", g, n) for n in range(TAPS)] + [("c2a", g, n) for n in range(TAPS)]
    out = [[("load", 0), ("load", 1), ("exp_x", 0), ("elu", 0), ("high_x", 0), ("low_x", 0), ("exp_x", 1)]]
    out += [[r] for r in runs]
    for n, (k, g, part) in enumerate(runs):
        def later(d, *steps):
            out[min(n + 1 + d, len(runs))] += steps
        if part == TAPS - 1:
            if k == "c1":
                later(2, ("high_c", g), ("low_c", g))
            if k == "c2b":
                later(2, ("tanh", g))
            if k == "c2a":
                later(2, ("gate", g))
        if k == "c1" and g + 1 < GROUPS:
            if part == 0:
                if g + 2 < GROUPS:
                    later(0, ("load", g + 2))
                later(0, ("elu", g + 1))
            if part == TAPS // 2:
                later(0, ("high_x", g + 1), ("low_x", g + 1))
            if part == TAPS - 1 and g + 2 < GROUPS:
                later(0, ("exp_x", g + 2))
    return out


SLACK = {"topk": 4.0, "turn": 0.3, "pool": 0.5, "lin": 1.5, "z2": 0.5, "negmax": 0.7, "fold": 0.7,
         "foldhigh": 0.42, "copy": 0.7, "foldq": 0.7, "mix": 0.6, "z": 0.6, "gram": 0.3, "max": 0.4,
         "exp": 0.338, "qkv": 0.48, "stack": 0.3}


def body():
    att, conv = attention_steps(), conv_steps()
    chunks = [[("this", st) for st in c] for c in conv[HEAD:]]
    chunks[-AHEAD] += [("next", st) for st in conv[0]]
    chunks += [[("next", st) for st in c] for c in [[]] + conv[1:HEAD]]
    done_by = {st[1]: max(n + 1 - HEAD, 0) for n, c in enumerate(conv) for st in c if st[0] == "gate"}
    due, at = [], 0.0
    for st in att:
        if st[0] == "qkv":
            due.append((at, done_by[st[1]]))
        at += SLACK.get(st[0], 0.0)
    due.append((at, len(chunks)))

    out, mixed = [], set()
    at, n, level = 0.0, 0, 0.0
    for st in att:
        must = max([k for a, k in due if a <= at], default=0)
        while n < must:
            out.extend(chunks[n])
            n += 1
        out.append(("att", st))
        if st[0] == "ct":
            mixed.add(st[1])
        step = SLACK.get(st[0], 0.0)
        rate = max([(k - n) / (a - at) for a, k in due if a > at], default=0.0)
        at += step
        level = max(level, n) + max(rate, 0.0) * step
        while n < len(chunks) and n + 1 <= level:
            if any(w == "next" and x[0] == "gate" and x[1] not in mixed for w, x in chunks[n]):
                break
            out.extend(chunks[n])
            n += 1
    for c in chunks[n:]:
        out.extend(c)
    return out


def program(nc, x_cm, x_nat, w1, b1, w2, b2, wq, bq, wk, bk, wv, bv, w3, b3, gate_wt, gate_b,
            f1, f1b, f2, f2b, consts, masks, spots, out, t1_dram, p_dram):
    ATT, CONV, BODY = attention_steps(), sum(conv_steps(), []), body()
    FIRST = []
    for n, c in enumerate(conv_steps()[:HEAD]):
        if ("high_c", 0) in c:
            FIRST.append(("this", ("small",)))
        FIRST += [("this", st) for st in c]
        if n == 0:
            FIRST.append(("this", ("split",)))
    FIRST.append(("this", ("ready",)))
    LAST = [(w, st) for w, st in BODY if w != "next"]
    misc_order, score_order, conv_order = [], [], []
    uses = {"qkv": ("q", "k"), "v": ("v",), "poolt": ("poolt",), "fold": ("fold",), "mix": ("mh0", "mh1"), "ct": ("ct",), "gram": ("gram", "zt"),
            "lin": ("lin",), "z2t": ("z2t",), "logit": ("logit",), "turn": ("pt",), "pool": ("pool",)}
    for st in ATT:
        misc_order += [(k, st[1]) for k in uses.get(st[0], ())]
        if st[0] in ("max", "exp"):
            score_order.append(st)
    for st in CONV:
        if st[0] in ("c1", "c2a", "c2b") and st[2] == TAPS - 1:
            conv_order.append(st[:2])
    NM, NS = len(misc_order), len(score_order)
    exp_order = [st for st in score_order if st[0] == "exp"]
    NE = len(exp_order)

    ctx = ExitStack()
    attctx, convctx = ExitStack(), ExitStack()

    def sb(name, shape, dt=F32, c=None):
        return (c or attctx).enter_context(nc.sbuf_tensor(name, shape, dt))

    def semaphore(name):
        return ctx.enter_context(nc.semaphore(name))

    signals = []

    def signal(name, per, unit=1):
        s = Signal(semaphore(name), per, unit)
        signals.append(s)
        return s

    with ctx:
        ps = ctx.enter_context(nc.psum_tensor("ps", [128, 8, 512], F32))
        cbank = [ps[:, 0, :], ps[:, 1, :]]
        sbank = [ps[:, 2 + n, :] for n in range(SLOTS)]
        pvbank = ps[:, 5, :]
        mbank = [ps[:, 6, :], ps[:, 7, :]]

        con = sb("con", [128, K_END], c=ctx)
        ident = con[:, K_ID:K_ID + 128]
        pooled = sb("pooled", [128, E + QUAD // B - 1, B], c=ctx)

        RW = 5
        ring = ExitStack()
        wa = sb("wa", [128, RW, 4, HID], c=ring)
        wb = sb("wb", [128, RW, 4, 4, C], c=ring)
        ring.close()

        w1s = sb("w1s", [128, 2, 9, C], F32R, c=convctx)
        w2s = sb("w2s", [128, 2, 9, 2 * C], F32R, c=convctx)
        xi = sb("xi", [128, 2, GR + 2, IW], c=convctx)
        el = sb("el", [128, GR + 2, IW], c=convctx)
        xp = sb("xp", [128, 2, 2, GR + 2, PW], F32R, c=convctx)
        cp = sb("cp", [128, 2, IH, PW], F32R, c=convctx)
        sg = sb("sg", [128, GT], c=convctx)
        sb("spare", [128, 64], c=convctx)

        small = ExitStack()
        hs = sb("hs", [128, 2, HID], c=small)
        ht = sb("ht", [128, 2, 4, 128], c=small)
        oall = sb("oall", [128, E // 4, C], c=small)
        small.close()

        keep = ExitStack()
        zt = sb("zt", [128, TOK], c=keep)
        T = sb("T", [128, TOK // 128, C], c=keep)
        p_both = sb("p_both", [128, TOK], c=keep)
        p = p_both[0:E, :]
        z2t = sb("z2t", [128, GT], c=keep)
        ptt = z2t[:, :].rearrange("p (n t e) -> p n t e", n=2, e=E)
        pacc = sb("pacc", [2 * E, C], c=keep)
        phalf = sb("phalf", [C, E], c=keep)
        tk = sb("tk", [E, 12], c=keep)
        tops = sb("tops", [E, GROUPS, 8], c=keep)

        identr = sb("identr", [128, 128], F32R)
        maskr = sb("maskr", [128, 2, 128], F32R)
        wqs = sb("wqs", [128, 2, 128])
        w3s = sb("w3s", [128, C + 1])
        b3s = sb("b3s", [128, C])
        gws = sb("gws", [128, E])
        cols = sb("cols", [128, 8])
        c3 = sb("c3", [128, TOK])
        qv = sb("qv", [128, 2, GT])
        qh = sb("qh", [128, GT], F32R)
        kv = sb("kv", [128, GT])
        kh = sb("kh", [128, GT], F32R)
        qst = sb("qst", [128, 2, GT], F32R)
        qm = sb("qm", [128, 2, GT], F32R)
        over = ExitStack()
        left = sb("left", [E, TOK], c=over)
        over.close()
        kst = sb("kst", [128, TOK], F32R)
        vs = sb("vs", [128, TOK // 128, VW])
        zl = sb("zl", [128, VW])
        hb = sb("hb", [128, 2])
        fh = sb("fh", [128, GT], F32R)
        mpart = sb("mpart", [128, NT, GROUPS])
        nm = sb("nm", [128, NT])
        dg = sb("dg", [128, NT, 128])
        ex = sb("ex", [128, ESL, GT])
        asb = sb("asb", [128, GT])
        xn = sb("xn", [128, 2, NT, C])
        rd = sb("rd", [128, 2, NT])
        stat = sb("stat", [128, NT, 6])
        mv = sb("mv", [128, 2, NT, 2])
        rs = sb("rs", [128, 2, 2, NT])
        zr = sb("zr", [128, NT, C])
        G = sb("G", [128, C])

        attctx.close()
        tail = ExitStack()
        fb1 = sb("fb1", [E, HID], c=tail)
        fb2 = sb("fb2", [E, C], c=tail)
        eb = sb("eb", [E, E, B], c=tail)
        spot = sb("spot", [128, B, 2 * E - 4], c=tail)
        oo = sb("oo", [128, 2, 2, C], c=tail)
        pp = sb("pp", [128, TOK], c=tail)
        tl = sb("tl", [128, B - 1, TOK // 128, C], c=tail)
        tail.close()
        keep.close()
        convctx.close()

        s_con, s_w1, s_w2, s_cb, s_b = (semaphore(n) for n in (
            "consts_in", "w1_in", "w2_in", "conv_biases_in", "small_weights_in"))
        s_lo, s_hb = semaphore("low_weights"), semaphore("half_bias")
        s_zero, s_set, s_setp, s_seta = (semaphore(n) for n in ("zeroed", "setup_dve", "setup_pool", "setup_act"))
        s_dset = semaphore("setup_steps")
        s_held = semaphore("held")
        x_in = [signal(f"x_in{n}", GROUPS // 2, 16) for n in range(2)]
        elu_exp = signal("elu_exp", GROUPS)
        elu_min = signal("elu_min", GROUPS)
        elu_out = signal("elu_out", GROUPS)
        x_high = signal("x_high", GROUPS)
        x_low = signal("x_low", GROUPS)
        cmm = signal("conv_products", 3 * GROUPS)
        c_high = signal("c_high", GROUPS)
        c_low = signal("c_low", GROUPS)
        gate_tanh = signal("gate_tanh", GROUPS)
        gate_half = signal("gate_half", GROUPS)
        c3_out = signal("c3_out", GROUPS)
        cmm_index = {k: n for n, k in enumerate(conv_order)}
        mmm = signal("misc_products", NM)
        smm = signal("scores", NS)
        q_val, q_high, q_st = (signal(n, GROUPS) for n in ("q_value", "q_high", "q_stacked"))
        k_val, k_high, k_st = (signal(n, GROUPS) for n in ("k_value", "k_high", "k_stacked"))
        v_out = signal("v_out", GROUPS)
        smax = signal("max_parts", NS - NE)
        nm_out = signal("neg_max", GROUPS)
        dg_out = signal("max_columns", GROUPS)
        fold_sum, fold_high, qm_out = (signal(n, GROUPS) for n in ("fold_sum", "fold_high", "q_with_max"))
        e_out = signal("exponentials", NE)
        pv = signal("pv_used", NE)
        a_out = signal("attention_copied", GROUPS)
        xn_in = [signal(f"xn_in{n}", GROUPS // 2, 16) for n in range(2)]
        xb_out = signal("x_plus_b3", GROUPS)
        den_sum, rd_out = signal("den_sum", 2 * GROUPS), signal("den_reciprocal", 2 * GROUPS)
        t_half = signal("t_first_half", GROUPS)
        t_scaled, t_out = signal("t_scaled", GROUPS), signal("t_out", GROUPS)
        st1, mv1, ve1, rs1 = (signal(n, GROUPS) for n in ("ln1_stats", "ln1_mean_var", "ln1_var_eps", "ln1_rstd"))
        z_out, gram_out, zt_out = (signal(n, GROUPS) for n in ("z_out", "gram_out", "z_transposed"))
        t1_out = signal("t1_out", GROUPS)
        t1_store = signal("t1_stored", GROUPS, 16)
        st2, mv2, ve2, rs2 = (signal(n, GROUPS) for n in ("ln2_stats", "ln2_mean_var", "ln2_var_eps", "ln2_rstd"))
        z2_out, z2t_out, logit_out = (signal(n, GROUPS) for n in ("z2_out", "z2_transposed", "logits_out"))
        tkd = signal("topk_steps", TKS)
        top_out = signal("group_top8", GROUPS)
        tk_scaled = signal("topk_scaled", 1)
        tke = signal("topk_exp", 1)
        p_store = signal("p_stored", 1, 16)
        pt_out, pool_out = signal("p_transposed", POOLS), signal("pooled_part", POOLS)
        phalf_out, pooled_out = signal("pooled_half", 1), signal("pooled", 1)

        midx = {k: n for n, k in enumerate(misc_order)}
        sidx = {k: n for n, k in enumerate(score_order)}
        eidx = {k: n for n, k in enumerate(exp_order)}

        xidx = {st: n for n, st in enumerate(st for st in score_order if st[0] == "max")}
        readers = {"q": q_high, "k": k_high, "v": v_out, "fold": fold_sum, "mh0": t_half, "mh1": t_scaled,
                   "ct": t_out, "gram": gram_out, "zt": zt_out, "lin": t1_out, "z2t": z2t_out,
                   "logit": logit_out, "pt": pt_out, "pool": pool_out, "poolt": pooled_out, "c1": c_low, "c2a": c3_out,
                   "c2b": gate_tanh}

        def read_of(key):
            if key[0] == "max":
                return smax, xidx[key]
            if key[0] == "exp":
                return e_out, eidx[key]
            return readers[key[0]], key[1]

        def reused(order, bank_of, n, b):
            same = [m for m in range(n) if bank_of(m) == bank_of(n)]
            if same:
                s, k = read_of(order[same[-1]])
                return s.sem, s.at(b, k)
            s, k = read_of(order[[m for m in range(len(order)) if bank_of(m) == bank_of(n)][-1]])
            return s.sem, s.before(b, k)

        def conv_bank(key):
            return cbank[cmm_index[key] % 2]

        def misc(key):
            return mbank[midx[key] % 2]

        def x_rows(g):
            lo, hi = max(GR * g - 1, 0), min(GR * g + GR + 1, IH)
            return lo, hi, lo - (GR * g - 1)

        pairs = ((0, 1), (3, 2))
        finals = [(w, g) for w in range(2) for g in range(GROUPS)]

        def t1_tiles(b, g):
            here = slice(NT * g, NT * g + NT)
            return T[:, here, :] if b == B - 1 else tl[:, b, here, :]

        def topk_place(final):
            a, c = (tl[0:E, 2, :, :], tl[0:E, 1, :, :].rearrange("p t c -> p (t c)")) if final else (
                T[0:E, :, :], left[:, :])
            return a.rearrange("p t c -> p (t c)"), c

        s_fb = semaphore("ffn_biases_in")
        wa_in = [semaphore(f"wa_in{n}") for n in range(RW)]
        wb_in = [semaphore(f"wb_in{n}") for n in range(RW)]
        ffn1, ffn2, gelu, htr, htc = (semaphore(n) for n in ("ffn1", "ffn2", "gelu", "h_transposed", "h_copied"))
        p_in, o_out, placed, oo_out = (semaphore(n) for n in ("p_in", "o_out", "placed", "oo_out"))
        tl_in = [semaphore(f"tl_in{n}") for n in range(B - 1)]
        out_st = semaphore("out_stored")
        sum_out, fin, s_px = semaphore("sum_out"), semaphore("final_products"), semaphore("ffn_operands")

        N_B = 16 * (16 + 4 + 5)
        block = ctx.enter_context(nc.Block())

        @block.sync
        def _(sp):
            sp.dma_start(c3[:, 0:9 * C], w1.rearrange("p t c -> p (t c)")).then_inc(s_w1, 16)
            for s in signals:
                sp.sem_inc(s.sem, s.per * s.unit)

            def load_small():
                sp.dma_start(con[:, :], consts).then_inc(s_con, 16)
                sp.dma_start(T[:, :, :].rearrange("p t c -> p (t c)")[:, 0:18 * C],
                             w2.rearrange("p t c -> p (t c)")).then_inc(s_w2, 16)
                sp.dma_start(zr[:, 0:2, :], masks).then_inc(s_w2, 16)
                sp.wait_ge(s_zero, 1)
                sp.dma_start(cols[:, 0:1], b1).then_inc(s_cb, 16)
                sp.dma_start(cols[:, 1:3], b2).then_inc(s_cb, 16)
                for q in range(4):
                    sp.dma_start(wqs[:, 0, QUAD * q:QUAD * q + DK], wq).then_inc(s_b, 16)
                    sp.dma_start(wqs[:, 1, QUAD * q:QUAD * q + DK], wk).then_inc(s_b, 16)
                    sp.dma_start(cols[QUAD * q:QUAD * q + DK, 3:4], bq).then_inc(s_b, 16)
                    sp.dma_start(cols[QUAD * q:QUAD * q + DK, 4:5], bk).then_inc(s_b, 16)
                for q in range(4):
                    sp.dma_start(zt[QUAD * q:QUAD * q + DV, 0:HEADS * C], w3).then_inc(s_b, 16)
                sp.dma_start(wqs[:, 1, VROW:VROW + DV], wv).then_inc(s_b, 16)
                sp.dma_start(cols[VROW:VROW + DV, 4:5], bv).then_inc(s_b, 16)
                sp.dma_start(cols[0:E, 5:6], gate_b).then_inc(s_b, 16)
                sp.dma_start(gws[:, :], gate_wt).then_inc(s_b, 16)
                sp.dma_start(b3s[:, :], b3.partition_broadcast(128)).then_inc(s_b, 16)

            def load(b, g):
                sp.wait_ge(elu_out.sem, elu_out.at(b, g - 2) if g >= 2 else elu_out.before(b, g + 6))
                lo, hi, r = x_rows(g)
                sp.dma_start(xi[:, g % 2, r:r + hi - lo, :].rearrange("p r w -> p (r w)"),
                             x_cm[b, :, lo * IW:hi * IW]).then_inc(x_in[g % 2].sem, 16)

            def load_nat(b, g):
                sp.wait_ge(t_scaled.sem, t_scaled.at(b, g - 2) if g >= 2 else t_scaled.before(b, g + 6))
                sp.sem_inc(s_held, 1)
                sp.dma_start(xn[:, g % 2, :, :], x_nat[b, g, :, :, :]).then_inc(xn_in[g % 2].sem, 16)

            def store_t1(b, g):
                sp.wait_ge(t1_out.sem, t1_out.at(b, g))
                sp.dma_start(t1_dram[b, g, :, :, :], T[:, NT * g:NT * g + NT, :]).then_inc(t1_store.sem, 16)

            def store_p(b):
                sp.wait_ge(tkd.sem, tkd.at(b, TKS - 1))
                sp.dma_start(p_dram[b, :, :], p[:, :]).then_inc(p_store.sem, 16)

            def load_w1(i):
                sp.dma_start(wa[:, i % RW, :, :], f1[:, 4 * i:4 * i + 4, :]).then_inc(wa_in[i % RW], 16)

            def load_w2(i):
                sp.dma_start(wb[:, i % RW, :, :, :], f2[:, 4 * i:4 * i + 4, :, :]).then_inc(wb_in[i % RW], 16)

            def load_last(b):
                sp.wait_ge(logit_out.sem, logit_out.at(b, GROUPS - 1))
                sp.dma_start(fb1[:, :], f1b).then_inc(s_fb, 16)
                sp.dma_start(fb2[:, :], f2b).then_inc(s_fb, 16)
                sp.dma_start(spot[:, :, :], spots).then_inc(s_fb, 16)
                sp.wait_ge(t1_store.sem, t1_store.at(b - 1, GROUPS - 1))
                sp.wait_ge(p_store.sem, p_store.at(b - 1, 0))
                load_t1(0)
                for n, dst in enumerate((pp[0:E, :], pp[E:2 * E, :], p_both[E:2 * E, :])):
                    sp.dma_start(dst, p_dram[n, :, :]).then_inc(p_in, 16)

            def load_t1(n):
                sp.dma_start(tl[:, n, :, :].rearrange("p (g t) c -> p g (t c)", g=GROUPS),
                             t1_dram[n, :, :, :, :].rearrange("g p t c -> p g (t c)")).then_inc(tl_in[n], 16)

            def run(steps, b, final=False):
                for which, st in steps:
                    c = b + (which == "next")
                    if st[0] == "load":
                        load(c, st[1])
                    if st[0] == "split":
                        load_small()
                    if st[0] == "foldq":
                        load_nat(b, st[1])
                    if st[0] == "lin" and not final:
                        store_t1(b, st[1])
                    if st == ("topk", 5) and not final:
                        store_p(b)
                    if final and st == ("logit", GROUPS - 1):
                        load_last(b)
                    if final and st == ("gate", GROUPS - 1):
                        sp.wait_ge(c3_out.sem, c3_out.at(b, GROUPS - 1))
                        for i in range(RW):
                            load_w1(i)
                            load_w2(i)

            run(FIRST, 0)
            with sp.Fori(0, B - 1) as b:
                run(BODY, b)
            run(LAST, B - 1, final=True)

            sp.wait_ge(tkd.sem, tkd.at(B - 1, TKS - 1))
            load_t1(1)
            load_t1(2)

            for k in range(E // 4 + 2):
                if k + RW < E // 4:
                    sp.wait_ge(ffn1, k + 1)
                    load_w1(k + RW)
                if 0 <= k - 2 and k - 2 + RW < E // 4:
                    sp.wait_ge(ffn2, k - 1)
                    load_w2(k - 2 + RW)
            for n, (w, g) in enumerate(finals):
                for a, b in enumerate(pairs[w]):
                    sp.wait_ge(sum_out, 2 * n + a + 1)
                    sp.dma_start(out[b, g, :, :, :], t1_tiles(b, g)).then_inc(out_st, 16)
            sp.wait_ge(out_st, 16 * B * GROUPS)

        @block.tensor
        def _(pe):
            pe.wait_ge(s_setp, 1)
            pe.wait_ge(s_lo, 1)

            def small():
                pe.wait_ge(s_lo, 2)

            def ready():
                pe.wait_ge(s_set, 1)
                pe.wait_ge(s_seta, 2)

            def conv(bank, w, lo, x, part, rows):
                acc = bank.rearrange("p (r w) -> p r w", w=IW)
                dy, dx = (1, 0, 2)[part // 3], part % 3
                src, dst = rows(dy)
                for wi, xi_ in ((0, 0), (0, 1), (1, 0)):
                    mm = pe.matmul(acc[:, dst, :], w[:, wi, 3 * dy + dx, lo:lo + C], x[:, xi_, src, dx:dx + IW],
                                   start=(part == wi == xi_ == 0), stop=(part == TAPS - 1 and wi == 1))
                if part == TAPS - 1:
                    mm.then_inc(cmm.sem, 1)

            def edges(g, dy):
                return (1 if g == 0 and dy == 0 else 0), (GR - 1 if g == GROUPS - 1 and dy == 2 else GR)

            def bank_wait(key, b):
                pe.wait_ge(*reused(conv_order, lambda m: m % 2, cmm_index[key], b))

            def c1(b, g, part):
                def rows(dy):
                    r0, r1 = edges(g, dy)
                    return slice(r0 + dy, r1 + dy), slice(r0, r1)
                if part == 0:
                    pe.wait_ge(x_low.sem, x_low.at(b, g))
                    bank_wait(("c1", g), b)
                conv(conv_bank(("c1", g)), w1s, 0, xp[:, g % 2], part, rows)

            def c2(b, g, part, key, half):
                def rows(dy):
                    r0, r1 = edges(g, dy)
                    return slice(GR * g + r0 + dy - 1, GR * g + r1 + dy - 1), slice(r0, r1)
                if part == 0:
                    if half:
                        pe.wait_ge(c_low.sem, c_low.at(b, min(g + 1, GROUPS - 1)))
                    bank_wait((key, g), b)
                conv(conv_bank((key, g)), w2s, half * C, cp, part, rows)

            def misc_bank(b, key):
                pe.wait_ge(*reused(misc_order, lambda m: m % 2, midx[key], b))
                return misc(key)

            def qkv(b, g):
                x = c3[:, GT * g:GT * g + GT]
                pe.wait_ge(c3_out.sem, c3_out.at(b, g))
                bank = misc_bank(b, ("q", g))
                pe.matmul(bank, wqs[:, 0, :], x, start=True, stop=True).then_inc(mmm.sem, 1)
                bank = misc_bank(b, ("k", g))
                pe.matmul(bank, wqs[:, 1, :], x, start=True, stop=True).then_inc(mmm.sem, 1)

            def v_turn(b, g):
                pe.wait_ge(k_val.sem, k_val.at(b, g))
                turn(b, ("v", g), kv)

            def score_bank(b, st):
                n = sidx[st]
                pe.wait_ge(*reused(score_order, lambda m: m % SLOTS, n, b))
                return sbank[n % SLOTS]

            def max_scores(b, g, r, c):
                if r == 0 and c == 0:
                    pe.wait_ge(k_st.sem, k_st.at(b, g))
                bank = score_bank(b, ("max", g, r, c))
                w = GT if c < g else 128 * (r + 1)
                mm = pe.matmul(bank[:, 0:w], qst[:, g % 2, 128 * r:128 * r + 128], kst[:, GT * c:GT * c + w],
                               start=True, stop=(c < g))
                if c == g:
                    mm = pe.matmul(bank[:, w - 128:w], identr[:, :], maskr[:, 0, :], start=False, stop=True)
                mm.then_inc(smm.sem, 1)

            def fold(b, g):
                pe.wait_ge(dg_out.sem, dg_out.at(b, g))
                turn(b, ("fold", g), dg[:, :, :].rearrange("p t n -> p (t n)"))

            def exp_scores(b, g, u):
                if u == 0:
                    pe.wait_ge(qm_out.sem, qm_out.at(b, g))
                bank = score_bank(b, ("exp", g, u))
                at = 0
                for i, n0 in score_units(g)[u]:
                    w = GT - n0 if i >= NT * g else GT
                    diag = i >= NT * g
                    q0 = 128 * (i - NT * g) if diag else 0
                    w = GT - q0
                    mm = pe.matmul(bank[:, at:at + w], kst[:, 128 * i:128 * i + 128], qm[:, g % 2, q0:GT],
                                   start=True, stop=not diag)
                    if diag:
                        mm = pe.matmul(bank[:, at:at + 128], identr[:, :], maskr[:, 1, :], start=False, stop=True)
                    at += w
                mm.then_inc(smm.sem, 1)

            def values(b, g, u):
                n = eidx[("exp", g, u)]
                if u == 0:
                    pe.wait_ge(a_out.sem, a_out.at(b, g - 1) if g else a_out.before(b, GROUPS - 1))
                pe.wait_ge(e_out.sem, e_out.at(b, n))
                e = ex[:, n % ESL, :]
                if g == 0 and u == 0:
                    for q in range(1, 4):
                        pe.matmul(pvbank[QUAD * q:QUAD * q + VW, :], zl[:, :], e, start=True, stop=False,
                                  skip_group_check=True)
                at = 0
                for i, _ in score_units(g)[u]:
                    q0 = 128 * (i - NT * g) if i >= NT * g else 0
                    w = GT - q0
                    q = i % 4
                    mm = pe.matmul(pvbank[QUAD * q:QUAD * q + VW, q0:GT], vs[:, i, :], e[:, at:at + w],
                                   start=(i < 4 and not (g == 0 and i > 0)), stop=(i >= NT * g),
                                   skip_group_check=True)
                    at += w
                mm.then_inc(pv.sem, 1)

            def mix(b, g):
                pe.wait_ge(a_out.sem, a_out.at(b, g))
                for h in range(2):
                    bank = misc_bank(b, (f"mh{h}", g))
                    for r in range(2):
                        t = 128 * (2 * h + r)
                        mm = pe.matmul(bank[:, (C + 1) * r:(C + 1) * (r + 1)], asb[:, t:t + 128], w3s[:, :],
                                       start=True, stop=True)
                    mm.then_inc(mmm.sem, 1)

            def turn(b, key, x):
                bank = misc_bank(b, key)
                for r in range(NT):
                    mm = pe.transpose(bank[:, 128 * r:128 * r + 128], x[:, 128 * r:128 * r + 128], ident)
                mm.then_inc(mmm.sem, 1)

            def gram(b, g):
                pe.wait_ge(z_out.sem, z_out.at(b, g))
                bank = misc_bank(b, ("gram", g))
                for r in range(NT):
                    mm = pe.matmul(bank[:, 0:C], zr[:, r, :], zr[:, r, :], start=(r == 0), stop=(r == NT - 1))
                mm.then_inc(mmm.sem, 1)
                turn(b, ("zt", g), zr[:, :, :].rearrange("p t c -> p (t c)"))

            def lin(b, g):
                if g == 0:
                    pe.wait_ge(gram_out.sem, gram_out.at(b, GROUPS - 1))
                    pe.wait_ge(zt_out.sem, zt_out.at(b, GROUPS - 1))
                bank = misc_bank(b, ("lin", g))
                for r in range(NT):
                    t = GT * g + 128 * r
                    mm = pe.matmul(bank[:, 128 * r:128 * r + 128], zt[:, t:t + 128], G[:, :], start=True, stop=True)
                mm.then_inc(mmm.sem, 1)

            def z2turn(b, g):
                pe.wait_ge(z2_out.sem, z2_out.at(b, g))
                turn(b, ("z2t", g), zt[:, GT * g:GT * g + GT])

            def logit(b, g):
                pe.wait_ge(z2t_out.sem, z2t_out.at(b, g))
                bank = misc_bank(b, ("logit", g))
                pe.matmul(bank[0:E, :], gws[:, :], z2t[:, :], start=True, stop=True).then_inc(mmm.sem, 1)

            def turn_p(b, n):
                if n == 0:
                    pe.wait_ge(tkd.sem, tkd.at(b, TKS - 1))
                bank = misc_bank(b, ("pt", n))
                pe.sem_inc(s_held, 1)
                for t in range(PT):
                    at = 128 * (PT * n + t)
                    mm = pe.transpose(bank[:, E * t:E * t + E], p[:, at:at + 128], ident[0:E, 0:E])
                mm.then_inc(mmm.sem, 1)

            def pool(b, n):
                pe.wait_ge(pt_out.sem, pt_out.at(b, n))
                bank = misc_bank(b, ("pool", n))
                for t in range(PT):
                    at = 128 * (PT * n + t)
                    h = E * (t % 2)
                    mm = pe.matmul(bank[h:h + E, 0:C], ptt[:, n % 2, t, :], zt[:, at:at + 128],
                                   start=(t < 2), stop=(t >= PT - 2),
                                   skip_group_check=True)
                mm.then_inc(mmm.sem, 1)

            def pool_turn(b, n):
                pe.wait_ge(pool_out.sem, pool_out.at(b, POOLS - 1))
                bank = misc_bank(b, ("poolt", n))
                pe.transpose(bank[:, 0:128], pacc[:, :], ident).then_inc(mmm.sem, 1)

            stages = {"small": lambda b: small(), "ready": lambda b: ready(), "c1": c1, "c2b": lambda b, g, n: c2(b, g, n, "c2b", 1), "c2a": lambda b, g, n: c2(b, g, n, "c2a", 0)}
            astages = {"qkv": qkv, "max": max_scores, "fold": fold, "exp": exp_scores, "mix": mix,
                       "ct": lambda b, g: turn(b, ("ct", g), c3[:, GT * g:GT * g + GT]), "v": v_turn, "poolt": pool_turn,
                       "gram": gram, "lin": lin, "z2t": z2turn, "logit": logit, "turn": turn_p, "pool": pool}

            def stay_warm():
                for n in range(WARM):
                    t = NT * (n % GROUPS)
                    pe.matmul(ps[:, 0, :], ident, T[:, t:t + NT, :].rearrange("p t c -> p (t c)"), start=True, stop=True)

            def run(steps, b, final=False):
                late = []
                for which, st in steps:
                    k, a = st[0], st[1:]
                    if k in stages:
                        stages[k](b + (which == "next"), *a)
                    if k in astages:
                        astages[k](b, *a)
                    if final and st == ("topk", 0):
                        stay_warm()
                    if k == "exp":
                        late.append(a)
                    while len(late) > (0 if k == "copy" else LAG):
                        values(b, *late.pop(0))

            run(FIRST, 0)
            with pe.Fori(0, B - 1) as b:
                run(BODY, b)
            run(LAST, B - 1, final=True)

            pe.wait_ge(s_px, 1)
            pe.wait_ge(pooled_out.sem, pooled_out.at(B - 1, 0))
            pe.wait_ge(s_fb, 48)

            pooled_flat = pooled[:, :, :].rearrange("p e b -> p (e b)")

            def first(i):
                if i >= 2:
                    pe.wait_ge(gelu, i - 1)
                pe.wait_ge(wa_in[i % RW], 16 * (i // RW + 1))
                for j in range(4):
                    e = 4 * i + j
                    pe.matmul(ps[QUAD * j:QUAD * j + QUAD, i % 2, :], pooled_flat[:, B * e:B * e + QUAD], wa[:, i % RW, j, :],
                              start=True, stop=False, skip_group_check=True)
                for j in range(4):
                    mm = pe.matmul(ps[QUAD * j:QUAD * j + B, i % 2, :], eb[:, 4 * i + j, :], fb1[:, :],
                                   start=False, stop=True, skip_group_check=True)
                mm.then_inc(ffn1, 1)

            def turn_h(i):
                pe.wait_ge(gelu, i + 1)
                if i >= 2:
                    pe.wait_ge(htc, i - 1)
                for c in range(4):
                    mm = pe.transpose(ps[:, 2 + i % 2, 128 * c:128 * c + 128], hs[:, i % 2, 128 * c:128 * c + 128], ident)
                mm.then_inc(htr, 1)

            def second(i):
                pe.wait_ge(htc, i + 1)
                pe.wait_ge(wb_in[i % RW], 16 * (i // RW + 1))
                if i >= 2:
                    pe.wait_ge(o_out, i - 1)
                for c in range(4):
                    for j in range(4):
                        pe.matmul(ps[QUAD * j:QUAD * j + QUAD, 4 + i % 2, 0:C], ht[:, i % 2, c, QUAD * j:QUAD * j + QUAD],
                                  wb[:, i % RW, j, c, :], start=(c == 0), stop=False, skip_group_check=True)
                for j in range(4):
                    mm = pe.matmul(ps[QUAD * j:QUAD * j + B, 4 + i % 2, 0:C], eb[:, 4 * i + j, :], fb2[:, :],
                                   start=False, stop=True, skip_group_check=True)
                mm.then_inc(ffn2, 1)

            first(0)
            first(1)
            def place(i):
                pe.wait_ge(o_out, i + 1)
                for w in range(2):
                    for a, b in enumerate(pairs[w]):
                        at = 4 * (E // 4 - 1 - i)
                        mm = pe.matmul(ps[E * a:E * a + E, 6 + w, 0:C], spot[:, b, at:at + E], oall[:, i, :],
                                       start=(i == 0), stop=(i == E // 4 - 1), skip_group_check=True)
                mm.then_inc(placed, 1)

            for i in range(E // 4):
                turn_h(i)
                if i + 2 < E // 4:
                    first(i + 2)
                if i >= 2:
                    place(i - 2)
                second(i)
            place(E // 4 - 2)
            place(E // 4 - 1)
            pe.wait_ge(oo_out, 4)
            pe.wait_ge(p_in, 16 * (B - 1))
            for n, (w, g) in enumerate(finals):
                if n >= 4:
                    pe.wait_ge(sum_out, 2 * (n - 3))
                for r in range(NT):
                    t = GT * g + 128 * r
                    mm = pe.matmul(ps[:, 2 * (n % 4) + r // 2, 2 * C * (r % 2):2 * C * (r % 2 + 1)],
                                   (pp, p_both)[w][:, t:t + 128], oo[:, w, :, :].rearrange("p a c -> p (a c)"),
                                   start=True, stop=True)
                mm.then_inc(fin, 1)

        @block.scalar
        def _(act):
            act.wait_ge(s_w1, 16)
            act.activation(w1s[:, 0, :, :].rearrange("p t c -> p (t c)"), c3[:, 0:9 * C], ACT.Copy).then_inc(s_seta, 1)

            def split():
                act.wait_ge(s_w2, 32)
                act.wait_ge(s_con, 16)
                act.activation(w2s[:, 0, :, :].rearrange("p t c -> p (t c)"),
                               T[:, 0:18, :].rearrange("p t c -> p (t c)"), ACT.Copy)
                act.activation(identr[:, :], ident, ACT.Copy)
                act.activation(maskr[:, :, :].rearrange("p a n -> p (a n)"), zr[:, 0:2, :].rearrange("p a n -> p (a n)"),
                               ACT.Copy).then_inc(s_seta, 1)

            def small():
                act.wait_ge(s_cb, 32)
                act.wait_ge(s_hb, 1)

            def ready():
                act.wait_ge(s_set, 1)

            def exp_x(b, g):
                lo, hi, r = x_rows(g)
                rows = slice(r, r + hi - lo)
                act.wait_ge(x_in[g % 2].sem, x_in[g % 2].at(b, g // 2))
                act.wait_ge(x_low.sem, x_low.at(b, g - 1) if g else x_low.before(b, GROUPS - 1))
                act.activation(el[:, rows, :], xi[:, g % 2, rows, :], ACT.Exp).then_inc(elu_exp.sem, 1)

            def high_x(b, g):
                lo, hi, r = x_rows(g)
                rows = slice(r, r + hi - lo)
                act.wait_ge(elu_out.sem, elu_out.at(b, g))
                k = cmm_index[("c1", (g - 2) % GROUPS)]
                act.wait_ge(cmm.sem, cmm.at(b, k) if g >= 2 else cmm.before(b, k))
                act.activation(xp[:, g % 2, 0, rows, 1:1 + IW], el[:, rows, :], ACT.Copy).then_inc(x_high.sem, 1)

            def high_c(b, g):
                act.wait_ge(cmm.sem, cmm.at(b, cmm_index[("c1", g)]))
                act.activation(cp[:, 0, GR * g:GR * g + GR, 1:1 + IW],
                               conv_bank(("c1", g)).rearrange("p (r w) -> p r w", w=IW),
                               ACT.Identity, bias=cols[:, 0:1]).then_inc(c_high.sem, 1)

            def tanh(b, g):
                act.wait_ge(cmm.sem, cmm.at(b, cmm_index[("c2b", g)]))
                act.wait_ge(c3_out.sem, c3_out.at(b, g - 1) if g else c3_out.before(b, GROUPS - 1))
                act.activation(sg[:, :], conv_bank(("c2b", g)), ACT.Tanh, scale=0.5,
                               bias=hb[:, 0:1]).then_inc(gate_tanh.sem, 1)

            def qkv(b, g):
                act.wait_ge(mmm.sem, mmm.at(b, midx[("q", g)]))
                act.wait_ge(qm_out.sem, qm_out.at(b, g - 2) if g >= 2 else qm_out.before(b, g + 6))
                act.activation(qv[:, g % 2, :], misc(("q", g)), ACT.Identity, scale=0.25,
                               bias=hb[:, 1:2]).then_inc(q_val.sem, 1)
                act.wait_ge(q_st.sem, q_st.at(b, g - 1) if g else q_st.before(b, GROUPS - 1))
                act.activation(qh[:, :], misc(("q", g)), ACT.Identity, scale=0.25,
                               bias=hb[:, 1:2]).then_inc(q_high.sem, 1)
                act.wait_ge(mmm.sem, mmm.at(b, midx[("k", g)]))
                act.wait_ge(k_st.sem, k_st.at(b, g - 1) if g else k_st.before(b, GROUPS - 1))
                act.activation(kv[:, :], misc(("k", g)), ACT.Identity, bias=cols[:, 4:5]).then_inc(k_val.sem, 1)
                act.activation(kh[:, :], misc(("k", g)), ACT.Identity, bias=cols[:, 4:5]).then_inc(k_high.sem, 1)

            def foldhigh(b, g):
                act.wait_ge(fold_sum.sem, fold_sum.at(b, g))
                act.wait_ge(qm_out.sem, qm_out.at(b, g - 1) if g else qm_out.before(b, GROUPS - 1))
                act.activation(fh[:, :], qv[:, g % 2, :], ACT.Copy).then_inc(fold_high.sem, 1)

            def exponentials(b, g, u):
                n = eidx[("exp", g, u)]
                w = sum(GT - max(0, 128 * (i - NT * g)) for i, _ in score_units(g)[u])
                act.wait_ge(smm.sem, smm.at(b, sidx[("exp", g, u)]))
                m = n - ESL if n >= ESL else [m for m in range(NE) if m % ESL == n % ESL][-1]
                act.wait_ge(pv.sem, pv.at(b, m) if n >= ESL else pv.before(b, m))
                act.activation(ex[:, n % ESL, 0:w], sbank[sidx[("exp", g, u)] % SLOTS][:, 0:w],
                               ACT.Exp).then_inc(e_out.sem, 1)

            def copy(b, g):
                act.wait_ge(pv.sem, pv.at(b, eidx[("exp", g, len(score_units(g)) - 1)]))
                k = midx[("mh1", (g - 1) % GROUPS)]
                act.wait_ge(mmm.sem, mmm.at(b, k) if g else mmm.before(b, k))
                act.activation(asb[:, :], pvbank, ACT.Copy).then_inc(a_out.sem, 1)

            def turned(b, g):
                act.wait_ge(mmm.sem, mmm.at(b, midx[("zt", g)]))
                act.activation(zt[:, GT * g:GT * g + GT], misc(("zt", g)), ACT.Copy).then_inc(zt_out.sem, 1)

            def z2turned(b, g):
                act.wait_ge(mmm.sem, mmm.at(b, midx[("z2t", g)]))
                k = ("logit", g - 1) if g else ("pool", POOLS - 1)
                if g and midx[k] > midx[("z2t", g)]:
                    act.wait_ge(mmm.sem, mmm.at(b, midx[k]))
                act.activation(z2t[:, :], misc(("z2t", g)), ACT.Copy).then_inc(z2t_out.sem, 1)

            def logit(b, g):
                act.wait_ge(mmm.sem, mmm.at(b, midx[("logit", g)]))
                act.wait_ge(p_store.sem, p_store.before(b, 0))
                act.activation(p[:, GT * g:GT * g + GT], misc(("logit", g))[0:E, :], ACT.Identity,
                               bias=cols[0:E, 5:6]).then_inc(logit_out.sem, 1)

            def topk(b, n, final):
                probs, _ = topk_place(final)
                if n == 2:
                    act.wait_ge(tkd.sem, tkd.at(b, 1))
                    if not final:
                        act.wait_ge(t1_store.sem, t1_store.at(b, GROUPS - 1))
                    act.activation(probs, p[:, :], ACT.Exp, bias=tk[:, 0:1], accum_out=tk[:, 1:2]).then_inc(tke.sem, 1)
                if n == 4:
                    act.wait_ge(tkd.sem, tkd.at(b, 3))
                    act.activation(probs, probs, ACT.Copy, scale=tk[:, 2:3]).then_inc(tk_scaled.sem, 1)

            def pool(b, n):
                act.wait_ge(mmm.sem, mmm.at(b, midx[("pt", n)]))
                act.activation(ptt[:, n % 2, :, :].rearrange("p t e -> p (t e)"), misc(("pt", n))[:, 0:PT * E],
                               ACT.Copy).then_inc(pt_out.sem, 1)

            stages = {"split": lambda b: split(), "small": lambda b: small(), "ready": lambda b: ready(),
                      "exp_x": exp_x, "high_x": high_x, "high_c": high_c, "tanh": tanh}
            astages = {"qkv": qkv, "foldhigh": foldhigh, "exp": exponentials, "copy": copy, "gram": turned,
                       "z2t": z2turned, "logit": logit, "topk": topk, "turn": pool}

            def run(steps, b, final=False):
                for which, st in steps:
                    if st[0] in stages:
                        stages[st[0]](b + (which == "next"), *st[1:])
                    if st[0] in astages:
                        more = (final,) if st[0] == "topk" else ()
                        astages[st[0]](b, *st[1:], *more)

            run(FIRST, 0)
            with act.Fori(0, B - 1) as b:
                run(BODY, b)
            run(LAST, B - 1, final=True)
            for i in range(E // 4):
                act.wait_ge(ffn1, i + 1)
                if i >= 2:
                    act.wait_ge(htr, i - 1)
                act.activation(hs[:, i % 2, :], ps[:, i % 2, :], ACT.Gelu).then_inc(gelu, 1)

        @block.vector
        def _(dve):
            dve.memset(cols[:, :], 0.0).then_inc(s_dset, 1)
            dve.memset(wqs[:, :, :], 0.0)
            dve.memset(zl[:, :], 0.0)
            dve.memset(pooled[:, E:, :], 0.0)
            dve.memset(pvbank, 0.0)
            dve.memset(dg[:, :, :], 0.0)
            dve.memset(zt[:, 0:HEADS * C], 0.0)
            dve.wait_ge(s_con, 16)
            dve.wait_ge(s_dset, 1)
            dve.tensor_copy(cols[:, 4:5], con[:, K_ONE:K_ONE + 1]).then_inc(s_zero, 1)
            dve.wait_ge(s_seta, 1)
            dve.tensor_tensor(w1s[:, 1, :, :].rearrange("p t c -> p (t c)"), c3[:, 0:9 * C],
                              w1s[:, 0, :, :].rearrange("p t c -> p (t c)").bitcast(F32), ALU.subtract).then_inc(s_lo, 1)

            def split():
                dve.wait_ge(s_seta, 2)
                dve.tensor_tensor(w2s[:, 1, :, :].rearrange("p t c -> p (t c)"),
                                  T[:, 0:18, :].rearrange("p t c -> p (t c)"),
                                  w2s[:, 0, :, :].rearrange("p t c -> p (t c)").bitcast(F32), ALU.subtract).then_inc(s_lo, 1)

            def small():
                dve.wait_ge(s_cb, 32)
                dve.tensor_scalar(hb[:, 0:1], cols[:, 2:3], 0.5, None, ALU.mult).then_inc(s_hb, 1)

            def ready():
                dve.wait_ge(s_b, N_B)
                dve.tensor_copy(w3s[:, C:C + 1], con[:, K_DEN:K_DEN + 1])
                dve.tensor_reduce(w3s[:, 0:C], zt[:, 0:HEADS * C].rearrange("p (h c) -> p c h", h=HEADS), AX.X, ALU.add)
                dve.tensor_scalar(hb[:, 1:2], cols[:, 3:4], 0.25, None, ALU.mult).then_inc(s_set, 1)
                dve.wait_ge(s_set, 1)

            def elu(b, g):
                lo, hi, r = x_rows(g)
                rows = slice(r, r + hi - lo)
                dve.wait_ge(elu_min.sem, elu_min.at(b, g))
                dve.scalar_tensor_tensor(out=el[:, rows, :], in0=xi[:, g % 2, rows, :], scalar=0.0,
                                         in1=el[:, rows, :], op0=ALU.max, op1=ALU.add).then_inc(elu_out.sem, 1)

            def low_x(b, g):
                lo, hi, r = x_rows(g)
                rows = slice(r, r + hi - lo)
                dve.wait_ge(x_high.sem, x_high.at(b, g))
                dve.tensor_tensor(xp[:, g % 2, 1, rows, 1:1 + IW], el[:, rows, :],
                                  xp[:, g % 2, 0, rows, 1:1 + IW].bitcast(F32), ALU.subtract).then_inc(x_low.sem, 1)

            def low_c(b, g):
                dve.wait_ge(c_high.sem, c_high.at(b, g))
                here = slice(GR * g, GR * g + GR)
                dve.scalar_tensor_tensor(out=cp[:, 1, here, 1:1 + IW],
                                         in0=conv_bank(("c1", g)).rearrange("p (r w) -> p r w", w=IW),
                                         scalar=cols[:, 0:1],
                                         in1=cp[:, 0, here, 1:1 + IW].bitcast(F32), op0=ALU.add,
                                         op1=ALU.subtract).then_inc(c_low.sem, 1)

            def gate(b, g):
                dve.wait_ge(gate_half.sem, gate_half.at(b, g))
                dve.wait_ge(cmm.sem, cmm.at(b, cmm_index[("c2a", g)]))
                dve.wait_ge(mmm.sem, mmm.before(b, midx[("ct", g)]))
                dve.scalar_tensor_tensor(out=c3[:, GT * g:GT * g + GT], in0=conv_bank(("c2a", g)), scalar=cols[:, 1:2],
                                         in1=sg[:, :], op0=ALU.add, op1=ALU.mult).then_inc(c3_out.sem, 1)

            def stack(b, g):
                dve.wait_ge(q_high.sem, q_high.at(b, g))
                k = sidx[("max", (g - 2) % GROUPS, NT - 1, (g - 2) % GROUPS)]
                dve.wait_ge(smm.sem, smm.at(b, k) if g >= 2 else smm.before(b, k))
                dve.scalar_tensor_tensor(out=qst[:, g % 2, :], in0=qh[:, :].bitcast(F32), scalar=con[:, K_NQ:K_NQ + 1],
                                         in1=qv[:, g % 2, :], op0=ALU.mult, op1=ALU.add).then_inc(q_st.sem, 1)
                dve.wait_ge(k_high.sem, k_high.at(b, g))
                dve.wait_ge(smm.sem, smm.before(b, NS - 1))
                dve.scalar_tensor_tensor(out=kst[:, GT * g:GT * g + GT], in0=kh[:, :].bitcast(F32),
                                         scalar=con[:, K_NK:K_NK + 1], in1=kv[:, :], op0=ALU.mult,
                                         op1=ALU.add).then_inc(k_st.sem, 1)

            def v(b, g):
                dve.wait_ge(mmm.sem, mmm.at(b, midx[("v", g)]))
                dve.wait_ge(pv.sem, pv.before(b, NE - 1))
                bank = misc(("v", g)).rearrange("p (t d) -> p t d", d=128)
                dve.tensor_copy(vs[:, NT * g:NT * g + NT, :], bank[:, :, VROW:VROW + VW]).then_inc(v_out.sem, 1)

            def maxima(b, g, r, c):
                st = ("max", g, r, c)
                dve.wait_ge(smm.sem, smm.at(b, sidx[st]))
                if r == 0 and c == 0:
                    dve.wait_ge(nm_out.sem, nm_out.at(b, g - 1) if g else nm_out.before(b, GROUPS - 1))
                w = GT if c < g else 128 * (r + 1)
                dve.tensor_reduce(mpart[:, r, c:c + 1], sbank[sidx[st] % SLOTS][:, 0:w], AX.X,
                                  ALU.max).then_inc(smax.sem, 1)

            def negmax(b, g):
                dve.wait_ge(smax.sem, smax.at(b, xidx[("max", g, NT - 1, g)]))
                dve.wait_ge(dg_out.sem, dg_out.at(b, g - 1) if g else dg_out.before(b, GROUPS - 1))
                dve.tensor_reduce(nm[:, :], mpart[:, :, 0:g + 1], AX.X, ALU.max, negate=True).then_inc(nm_out.sem, 1)
                dve.wait_ge(nm_out.sem, nm_out.at(b, g))
                k = midx[("fold", (g - 1) % GROUPS)]
                dve.wait_ge(mmm.sem, mmm.at(b, k) if g else mmm.before(b, k))
                dve.tensor_copy(dg[:, :, DK:QUAD + DK + 1:QUAD],
                                nm[:, :].unsqueeze(2).broadcast_to([128, NT, 2])).then_inc(dg_out.sem, 1)

            def fold(b, g):
                dve.wait_ge(mmm.sem, mmm.at(b, midx[("fold", g)]))
                dve.tensor_tensor(qv[:, g % 2, :], misc(("fold", g)), qv[:, g % 2, :], ALU.add).then_inc(fold_sum.sem, 1)

            def foldq(b, g):
                dve.wait_ge(fold_high.sem, fold_high.at(b, g))
                h = (g - 2) % GROUPS
                k = sidx[("exp", h, len(score_units(h)) - 1)]
                dve.wait_ge(smm.sem, smm.at(b, k) if g >= 2 else smm.before(b, k))
                dve.scalar_tensor_tensor(out=qm[:, g % 2, :], in0=fh[:, :].bitcast(F32), scalar=con[:, K_NQ:K_NQ + 1],
                                         in1=qv[:, g % 2, :], op0=ALU.mult, op1=ALU.add).then_inc(qm_out.sem, 1)

            def mix(b, g):
                dve.wait_ge(t_scaled.sem, t_scaled.at(b, g - 1) if g else t_scaled.before(b, GROUPS - 1))
                dve.wait_ge(t1_store.sem, t1_store.before(b, g))
                dve.wait_ge(tkd.sem, tkd.before(b, TKS - 1))
                for h in range(2):
                    here = slice(2 * h, 2 * h + 2)
                    dve.wait_ge(mmm.sem, mmm.at(b, midx[(f"mh{h}", g)]))
                    bank = misc((f"mh{h}", g))[:, 0:2 * (C + 1)].rearrange("p (t c) -> p t c", c=C + 1)
                    dve.tensor_scalar(rd[:, 0, here], bank[:, :, C], TINY, None, ALU.add).then_inc(den_sum.sem, 1)
                    dve.wait_ge(den_sum.sem, den_sum.at(b, 2 * g + h))
                    dve.reciprocal(rd[:, 1, here], rd[:, 0, here]).then_inc(rd_out.sem, 1)
                    dve.wait_ge(rd_out.sem, rd_out.at(b, 2 * g + h))
                    dve.wait_ge(xb_out.sem, xb_out.at(b, g))
                    for r in range(2):
                        t = 2 * h + r
                        ins = dve.scalar_tensor_tensor(out=T[:, NT * g + t, :], in0=bank[:, r, 0:C],
                                                       scalar=rd[:, 1, t:t + 1], in1=xn[:, g % 2, t, :],
                                                       op0=ALU.mult, op1=ALU.add)
                    ins.then_inc((t_half, t_scaled)[h].sem, 1)

            def ct(b, g):
                dve.wait_ge(t_scaled.sem, t_scaled.at(b, g))
                dve.wait_ge(mmm.sem, mmm.at(b, midx[("ct", g)]))
                tg = T[:, NT * g:NT * g + NT, :].rearrange("p t c -> p (t c)")
                dve.tensor_tensor(tg, misc(("ct", g)), tg, ALU.add).then_inc(t_out.sem, 1)

            def statistics(b, g, st, mean):
                for r in range(NT):
                    ins = dve.bn_stats(stat[:, r, :], T[:, NT * g + r, :])
                ins.then_inc(st.sem, 1)
                dve.wait_ge(st.sem, st.at(b, g))
                dve.sem_inc(s_held, 1)
                for r in range(NT):
                    ins = dve.bn_aggr(mv[:, g % 2, r, :], stat[:, r, :])
                ins.then_inc(mean.sem, 1)

            def normalised(g, out_tiles, out_sig):
                for r in range(NT):
                    ins = dve.tensor_scalar(out_tiles[r], T[:, NT * g + r, :], mv[:, g % 2, r, 0:1],
                                            rs[:, 1, g % 2, r:r + 1], ALU.subtract, ALU.mult)
                ins.then_inc(out_sig.sem, 1)

            def stats(b, g):
                dve.wait_ge(t_out.sem, t_out.at(b, g))
                dve.wait_ge(mv1.sem, mv1.at(b, g - 1) if g else mv1.before(b, GROUPS - 1))
                s_, k = (z_out, g - 2) if g >= 2 else (z2_out, g + 6)
                dve.wait_ge(s_.sem, s_.at(b, k) if g >= 2 else s_.before(b, k))
                dve.wait_ge(mv2.sem, mv2.before(b, GROUPS - 1))
                statistics(b, g, st1, mv1)

            def z(b, g):
                dve.wait_ge(rs1.sem, rs1.at(b, g))
                k = midx[("zt", (g - 1) % GROUPS)]
                dve.wait_ge(mmm.sem, mmm.at(b, k) if g else mmm.before(b, k))
                normalised(g, [zr[:, r, :] for r in range(NT)], z_out)

            def gram(b, g):
                dve.wait_ge(mmm.sem, mmm.at(b, midx[("gram", g)]))
                if g == 0:
                    dve.tensor_copy(G[:, :], misc(("gram", g))[:, 0:C]).then_inc(gram_out.sem, 1)
                else:
                    dve.wait_ge(gram_out.sem, gram_out.at(b, g - 1))
                    dve.tensor_tensor(G[:, :], misc(("gram", g))[:, 0:C], G[:, :], ALU.add).then_inc(gram_out.sem, 1)

            def lin(b, g):
                dve.wait_ge(mmm.sem, mmm.at(b, midx[("lin", g)]))
                tg = T[:, NT * g:NT * g + NT, :].rearrange("p t c -> p (t c)")
                dve.tensor_tensor(tg, misc(("lin", g)), tg, ALU.add).then_inc(t1_out.sem, 1)
                dve.wait_ge(t1_out.sem, t1_out.at(b, g))
                s_, k = (z2_out, g - 2) if g >= 2 else (z_out, g + 6)
                dve.wait_ge(s_.sem, s_.at(b, k))
                s_, k = (mv2, g - 1) if g else (mv1, GROUPS - 1)
                dve.wait_ge(s_.sem, s_.at(b, k))
                statistics(b, g, st2, mv2)

            def z2(b, g):
                dve.wait_ge(rs2.sem, rs2.at(b, g))
                normalised(g, [zt[:, GT * g + 128 * r:GT * g + 128 * r + 128] for r in range(NT)], z2_out)

            def top(b, g):
                dve.wait_ge(logit_out.sem, logit_out.at(b, g))
                dve.sem_inc(s_held, 1)
                dve.max(tops[:, g, :], p[:, GT * g:GT * g + GT]).then_inc(top_out.sem, 1)

            def topk(b, n, final):
                probs, rest = topk_place(final)
                if n == 4:
                    return
                if n:
                    dve.wait_ge(tkd.sem, tkd.at(b, min(n, 4) - 1))
                if n == 0:
                    dve.wait_ge(top_out.sem, top_out.at(b, GROUPS - 1))
                    dve.sem_inc(s_held, 1)
                    ins = dve.max(tk[:, 4:12], tops[:, :, :].rearrange("p g k -> p (g k)"))
                if n == 1:
                    ins = dve.tensor_scalar(tk[:, 0:1], tk[:, 4:5], -1.0, None, ALU.mult)
                if n == 2:
                    dve.sem_inc(s_held, 1)
                    ins = dve.match_replace(rest, tk[:, 4:12], p[:, :], GONE)
                if n == 3:
                    dve.wait_ge(tke.sem, tke.at(b, 0))
                    ins = dve.reciprocal(tk[:, 2:3], tk[:, 1:2])
                if n == 5:
                    dve.wait_ge(tk_scaled.sem, tk_scaled.at(b, 0))
                    ins = dve.scalar_tensor_tensor(out=p[:, :], in0=rest, scalar=GONE / 2, in1=probs,
                                                   op0=ALU.is_lt, op1=ALU.mult)
                ins.then_inc(tkd.sem, 1)

            def pool(b, n):
                dve.wait_ge(mmm.sem, mmm.at(b, midx[("pool", n)]))
                bank = misc(("pool", n))[:, 0:C]
                dve.wait_ge(pool_out.sem, pool_out.at(b, n - 1) if n else pool_out.before(b, POOLS - 1))
                if n == 0:
                    dve.tensor_copy(pacc[:, :], bank).then_inc(pool_out.sem, 1)
                else:
                    dve.tensor_tensor(pacc[:, :], bank, pacc[:, :], ALU.add).then_inc(pool_out.sem, 1)

            def pool_turn(b, n):
                dve.wait_ge(mmm.sem, mmm.at(b, midx[("poolt", n)]))
                bank = misc(("poolt", n))
                dve.tensor_copy(phalf[:, :], bank[:, E:2 * E]).then_inc(phalf_out.sem, 1)
                dve.wait_ge(phalf_out.sem, phalf_out.at(b, 0))
                dve.tensor_tensor(pooled[:, 0:E, b], bank[:, 0:E], phalf[:, :], ALU.add).then_inc(pooled_out.sem, 1)

            stages = {"split": lambda b: split(), "small": lambda b: small(), "ready": lambda b: ready(),
                      "elu": elu, "low_x": low_x, "low_c": low_c, "gate": gate}
            astages = {"stack": stack, "max": maxima, "negmax": negmax, "fold": fold, "foldq": foldq,
                       "mix": mix, "ct": ct, "v": v, "stats": stats, "z": z, "gram": gram, "lin": lin, "z2": z2,
                       "top": top, "topk": topk, "pool": pool, "poolt": pool_turn}

            def ffn_setup(b):
                dve.wait_ge(logit_out.sem, logit_out.at(b, GROUPS - 1))
                dve.memset(oo[:, :, :, :], 0.0)
                dve.tensor_copy(eb[:, :, :], con[0:E, K_ID:K_ID + E].unsqueeze(2).broadcast_to([E, E, B])).then_inc(s_px, 1)

            def run(steps, b, final=False):
                for which, st in steps:
                    if st[0] in stages:
                        stages[st[0]](b + (which == "next"), *st[1:])
                    if st[0] in astages:
                        more = (final,) if st[0] == "topk" else ()
                        astages[st[0]](b, *st[1:], *more)
                    if final and st == ("topk", 0):
                        ffn_setup(b)

            run(FIRST, 0)
            with dve.Fori(0, B - 1) as b:
                run(BODY, b)
            run(LAST, B - 1, final=True)

            for i in range(E // 4):
                dve.wait_ge(htr, i + 1)
                if i >= 2:
                    dve.wait_ge(ffn2, i - 1)
                dve.tensor_copy(ht[:, i % 2, :, :].rearrange("p c n -> p (c n)"), ps[:, 2 + i % 2, :]).then_inc(htc, 1)
                if i:
                    dve.wait_ge(ffn2, i)
                    dve.tensor_copy(oall[:, i - 1, :], ps[:, 4 + (i - 1) % 2, 0:C]).then_inc(o_out, 1)
            dve.wait_ge(ffn2, E // 4)
            dve.tensor_copy(oall[:, E // 4 - 1, :], ps[:, 4 + (E // 4 - 1) % 2, 0:C]).then_inc(o_out, 1)
            for w in range(2):
                for a in range(2):
                    dve.wait_ge(placed, E // 4)
                    dve.tensor_copy(oo[E * a:E * a + E, w, a, :], ps[E * a:E * a + E, 6 + w, 0:C]).then_inc(oo_out, 1)
            for n, (w, g) in enumerate(finals):
                dve.wait_ge(fin, n + 1)
                banks = ps[:, 2 * (n % 4):2 * (n % 4) + 2, :].rearrange("p k (t a c) -> p (k t) a c", t=2, a=2)
                for a, b in enumerate(pairs[w]):
                    if g == 0 and b < B - 1:
                        dve.wait_ge(tl_in[b], 16)
                    t = t1_tiles(b, g)
                    dve.tensor_tensor(t, banks[:, :, a, :], t, ALU.add).then_inc(sum_out, 1)

        @block.gpsimd
        def _(pool_e):
            for s_ in range(2):
                for h in range(2):
                    for col in (0, PW - 1):
                        pool_e.memset(xp[:, s_, h, :, col:col + 1].bitcast(F32), 0.0)
            for col in (0, PW - 1):
                ins = pool_e.memset(cp[:, :, :, col:col + 1].bitcast(F32), 0.0)
            ins.then_inc(s_setp, 1)

            def ready():
                pool_e.wait_ge(s_b, N_B)
                pool_e.wait_ge(s_con, 16)

            def elu(b, g):
                lo, hi, r = x_rows(g)
                rows = slice(r, r + hi - lo)
                pool_e.wait_ge(elu_exp.sem, elu_exp.at(b, g))
                pool_e.sem_inc(s_held, 1)
                pool_e.tensor_scalar(el[:, rows, :], el[:, rows, :], 1.0, -1.0, ALU.min, ALU.add).then_inc(elu_min.sem, 1)

            def c2(b, g):
                pool_e.wait_ge(gate_tanh.sem, gate_tanh.at(b, g))
                pool_e.sem_inc(s_held, 1)
                pool_e.tensor_scalar(sg[:, :], sg[:, :], 0.5, 0.5, ALU.mult, ALU.add).then_inc(gate_half.sem, 1)

            def bias(b, g):
                pool_e.wait_ge(xn_in[g % 2].sem, xn_in[g % 2].at(b, g // 2))
                pool_e.tensor_tensor(xn[:, g % 2, :, :], xn[:, g % 2, :, :],
                                     b3s[:, :].unsqueeze(1).broadcast_to([128, NT, C]), ALU.add).then_inc(xb_out.sem, 1)

            def rstd(b, g, mean, ve, out_sig, reader, count):
                h = g % 2
                pool_e.wait_ge(mean.sem, mean.at(b, g))
                pool_e.wait_ge(reader.sem, count)
                pool_e.sem_inc(s_held, 1)
                pool_e.tensor_scalar(rs[:, 0, h, :], mv[:, h, :, 1:2].rearrange("p t a -> p (t a)"), EPS, None,
                                     ALU.add).then_inc(ve.sem, 1)
                pool_e.wait_ge(ve.sem, ve.at(b, g))
                pool_e.tensor_tensor(rs[:, 1, h, :], rs[:, 0, h, :], con[:, K_POW:K_POW + NT],
                                     ALU.pow).then_inc(out_sig.sem, 1)

            def stats(b, g):
                s_, k = (z_out, g - 2) if g >= 2 else (z2_out, g + 6)
                rstd(b, g, mv1, ve1, rs1, s_, s_.at(b, k) if g >= 2 else s_.before(b, k))

            def lin(b, g):
                s_, k = (z2_out, g - 2) if g >= 2 else (z_out, g + 6)
                rstd(b, g, mv2, ve2, rs2, s_, s_.at(b, k))

            stages = {"ready": lambda b: ready(), "exp_x": elu, "tanh": c2}
            astages = {"foldq": bias, "stats": stats, "lin": lin}

            def run(steps, b):
                for which, st in steps:
                    if st[0] in stages:
                        stages[st[0]](b + (which == "next"), *st[1:])
                    if st[0] in astages:
                        astages[st[0]](b, *st[1:])

            run(FIRST, 0)
            with pool_e.Fori(0, B - 1) as b:
                run(BODY, b)
            run(LAST, B - 1)


def kernel(x, L0_conv_W1, L0_conv_b1, L0_conv_W2, L0_conv_b2, L0_conv_Wq, L0_conv_bq, L0_conv_Wk, L0_conv_bk,
           L0_conv_Wv, L0_conv_bv, L0_conv_W3, L0_conv_b3, L1_ffn_gate_w, L1_ffn_gate_b, L1_ffn_weight1,
           L1_ffn_weight2):
    import numpy as np
    import concourse.bacc as bacc
    from concourse.bass_utils import run_bass_kernel_spmd

    con = np.zeros((128, K_END), np.float32)
    i = np.arange(128)
    con[:, K_ID:K_ID + 128] = np.eye(128)
    masks = np.zeros((128, 2, 128), np.float32)
    masks[:, 0] = np.where(i[None, :] >= i[:, None], -1e10, 0.0)
    masks[:, 1] = np.where(i[:, None] >= i[None, :], -1e30, 0.0)
    con[DV::QUAD, K_DEN] = 1.0
    con[:, K_NQ] = np.where(i // QUAD % 2 == 1, -1.0, 0.0)
    con[:, K_NK] = np.where(i // QUAD >= 2, -1.0, 0.0)
    con[[DK, QUAD + DK, VROW + DV], K_ONE] = 1.0
    con[:, K_POW:K_POW + NT] = -0.5

    spots = np.zeros((128, B, 2 * E - 4), np.float32)
    for b in range(B):
        for j in range(4):
            spots[QUAD * j + b, b, E - 4 + j] = 1.0

    a = {
        "x_cm": x.reshape(B, TOK, C).transpose(0, 2, 1),
        "x_nat": x.reshape(B, GROUPS, NT, 128, C).transpose(0, 1, 3, 2, 4),
        "w1": L0_conv_W1.reshape(9, C, C).transpose(1, 0, 2),
        "b1": L0_conv_b1.reshape(C, 1),
        "w2": L0_conv_W2.reshape(9, C, 2 * C).transpose(1, 0, 2),
        "b2": L0_conv_b2.reshape(2, C).T,
        "wq": L0_conv_Wq, "bq": L0_conv_bq.reshape(DK, 1),
        "wk": L0_conv_Wk, "bk": L0_conv_bk.reshape(DK, 1),
        "wv": L0_conv_Wv, "bv": L0_conv_bv.reshape(DV, 1),
        "w3": L0_conv_W3.reshape(HEADS, DV, C).transpose(1, 0, 2).reshape(DV, HEADS * C),
        "b3": L0_conv_b3,
        "gate_wt": L1_ffn_gate_w.T,
        "gate_b": L1_ffn_gate_b.reshape(E, 1),
        "f1": L1_ffn_weight1[:, :C, :].transpose(1, 0, 2),
        "f1b": L1_ffn_weight1[:, C, :],
        "f2": L1_ffn_weight2[:, :HID, :].reshape(E, 4, 128, C).transpose(2, 0, 1, 3),
        "f2b": L1_ffn_weight2[:, HID, :],
        "consts": con,
        "masks": masks,
        "spots": spots,
    }
    nc = bacc.Bacc("TRN2", target_bir_lowering=False, num_devices=1)
    arrays, aps = {}, {}
    for name, v in a.items():
        v = np.ascontiguousarray(v)
        arrays["in_" + name] = v
        aps[name] = nc.dram_tensor("in_" + name, v.shape, mybir.dt.from_np(v.dtype), kind="ExternalInput").ap()
    aps["out"] = nc.dram_tensor("out_tokens", (B, GROUPS, 128, NT, C), F32, kind="ExternalOutput").ap()
    aps["t1_dram"] = nc.dram_tensor("t1_scratch", (B, GROUPS, 128, NT, C), F32).ap()
    aps["p_dram"] = nc.dram_tensor("p_scratch", (B, E, TOK), F32).ap()
    program(nc, **aps)
    r = run_bass_kernel_spmd(nc, [arrays], core_ids=[0])
    o = r.results[0]["out_tokens"]
    return o.transpose(0, 1, 3, 2, 4).reshape(B, IH, IW, C)
```
